# Optimizing a Trainium2 kernel written in Bass

```python
import numpy as np
import jax
import jax.numpy as jnp

def _softmax(x, axis=-1):
    return jax.nn.softmax(x, axis=axis)

def _gelu(x):
    return jax.nn.gelu(x, approximate=True)

def _silu(x):
    return jax.nn.silu(x)

def _sigmoid(x):
    return jax.nn.sigmoid(x)

def _layernorm(x, axis=-1, eps=1e-05):
    m = jnp.mean(x, axis=axis, keepdims=True)
    v = jnp.var(x, axis=axis, keepdims=True)
    return (x - m) / jnp.sqrt(v + eps)

def _scatter_add(tgt, idx, src, axis=0):
    return tgt.at[idx].add(src)

def _segment_sum(src, seg, n):
    return jax.ops.segment_sum(src, seg, n)
kernel_name = 'mk_gnn_ffn_d1_gnn_r8_29f4da'

def setup_inputs(seed: int=0):
    np.random.seed(seed)
    _w = jnp.asarray

    def _rec_inputs():
        import jax
        import jax.numpy as jnp
        _gk = jax.random.key(seed)
        x = -6.415e-05 + 1 * jax.random.normal(jax.random.fold_in(_gk, 1), (1250, 1024), jnp.float32)
        src = jax.random.randint(jax.random.fold_in(_gk, 2), (40000,), 0, 1250, jnp.int32)
        dst = jax.random.randint(jax.random.fold_in(_gk, 3), (40000,), 0, 1250, jnp.int32)
        _o = jnp.argsort(dst, stable=True)
        src = src[_o]
        dst = dst[_o]
        return (x, src, dst)
    x, src, dst = _rec_inputs()

    def _L0_gnn_setup():
        import jax, jax.numpy as jnp
        import numpy as np
        N_NODES = 1250
        N_EDGES = 20000
        DIM = 1024
        key = jax.random.key(seed)
        k1, k2, k3 = jax.random.split(key, 3)
        x = jax.random.normal(k1, (N_NODES, DIM), dtype=jnp.float32)
        edge_index = jax.random.randint(k2, (2, N_EDGES), 0, N_NODES, dtype=jnp.int64)
        W = jax.random.normal(k3, (DIM, DIM), dtype=jnp.float32) * (1.0 / np.sqrt(DIM))
        b = jnp.zeros((DIM,), dtype=jnp.float32)
        return {'x': x, 'edge_index': edge_index, 'W': W, 'b': b}
    _L0_gnn_all = _L0_gnn_setup()
    _L0_gnn_in = {k: v for k, v in _L0_gnn_all.items() if k in ('W', 'b')}
    del _L0_gnn_all

    def _L0_ffn_setup():
        import jax, jax.numpy as jnp
        import numpy as np
        B, N, DIM = (2, 256, 1024)
        HEADS, DIM_HEAD, EXPERTS = (8, 64, 8)
        SCALE = DIM_HEAD ** (-0.5)
        key = jax.random.key(seed)
        ks = jax.random.split(key, 6)
        dim_inner = HEADS * DIM_HEAD
        return {'x': jax.random.normal(ks[0], (B, N, DIM), jnp.float32), 'w_q': jax.random.normal(ks[1], (DIM, dim_inner), jnp.float32) * 0.02, 'w_k': jax.random.normal(ks[2], (DIM, dim_inner), jnp.float32) * 0.02, 'w_gate': jax.random.normal(ks[3], (DIM, HEADS * EXPERTS), jnp.float32) * 0.02, 'value_experts': jax.random.normal(ks[4], (EXPERTS, HEADS, DIM, DIM_HEAD), jnp.float32) * 0.02, 'output_experts': jax.random.normal(ks[5], (EXPERTS, HEADS, DIM_HEAD, DIM), jnp.float32) * 0.02}
    _L0_ffn_all = _L0_ffn_setup()
    _L0_ffn_in = {k: v for k, v in _L0_ffn_all.items() if k in ('w_q', 'w_k', 'w_gate', 'value_experts', 'output_experts')}
    del _L0_ffn_all
    return {'x': x, 'src': src, 'dst': dst, 'L0_gnn_W': _L0_gnn_in['W'], 'L0_gnn_b': _L0_gnn_in['b'], 'L0_ffn_w_q': _L0_ffn_in['w_q'], 'L0_ffn_w_k': _L0_ffn_in['w_k'], 'L0_ffn_w_gate': _L0_ffn_in['w_gate'], 'L0_ffn_value_experts': _L0_ffn_in['value_experts'], 'L0_ffn_output_experts': _L0_ffn_in['output_experts']}

def reference(x, src, dst, L0_gnn_W, L0_gnn_b, L0_ffn_w_q, L0_ffn_w_k, L0_ffn_w_gate, L0_ffn_value_experts, L0_ffn_output_experts):
    import jax
    import jax.numpy as jnp

    def _L0_gnn_ref(x, edge_index, W, b):
        import jax, jax.numpy as jnp
        import numpy as np
        N_NODES = 1250
        N_EDGES = 20000
        DIM = 1024
        'GCNConv (add_self_loops=True, symmetric norm) -> Dropout(eval=identity) -> ReLU.'
        n = x.shape[0]
        loops = jnp.arange(n, dtype=edge_index.dtype)
        src = jnp.concatenate([edge_index[0], loops])
        dst = jnp.concatenate([edge_index[1], loops])
        deg = jax.ops.segment_sum(jnp.ones_like(dst, dtype=x.dtype), dst, num_segments=n)
        dinv = jnp.where(deg > 0, jax.lax.rsqrt(deg), jnp.zeros_like(deg))
        norm = dinv[src] * dinv[dst]
        h = x @ W
        msg = h[src] * norm[:, None]
        out = jax.ops.segment_sum(msg, dst, num_segments=n) + b
        return jax.nn.relu(out)

    def _L0_ffn_ref(x, w_q, w_k, w_gate, value_experts, output_experts):
        import jax, jax.numpy as jnp
        import numpy as np
        B, N, DIM = (2, 256, 1024)
        HEADS, DIM_HEAD, EXPERTS = (8, 64, 8)
        SCALE = DIM_HEAD ** (-0.5)
        b, n, _ = x.shape
        q = (x @ w_q).reshape(b, n, HEADS, DIM_HEAD).transpose(0, 2, 1, 3)
        k = (x @ w_k).reshape(b, n, HEADS, DIM_HEAD).transpose(0, 2, 1, 3)
        gates = jax.nn.sigmoid((x @ w_gate).reshape(b, n, HEADS, EXPERTS).transpose(0, 2, 1, 3))
        sel = jnp.argmax(gates, axis=-1)
        gm = jax.nn.one_hot(sel, EXPERTS, dtype=x.dtype) * gates
        values = jnp.einsum('bhne,ehdk,bnd->bhnk', gm, value_experts, x)
        sim = jnp.einsum('bhid,bhjd->bhij', q * SCALE, k)
        causal_mask = jnp.triu(jnp.ones((n, n), dtype=bool), 1)
        sim = jnp.where(causal_mask, jnp.finfo(sim.dtype).min, sim)
        attn = jax.nn.softmax(sim, axis=-1)
        out = jnp.einsum('bhij,bhjk->bhik', attn, values)
        out = jnp.einsum('bhne,ehkd,bhnk->bhnd', gm, output_experts, out)
        return out.sum(axis=1)
    edge_index = jnp.stack([src, dst])
    x = x + _L0_gnn_ref(_layernorm(x, axis=-1), edge_index, L0_gnn_W, L0_gnn_b)
    x = x + _L0_ffn_ref(_layernorm(x, axis=-1)[None], L0_ffn_w_q, L0_ffn_w_k, L0_ffn_w_gate, L0_ffn_value_experts, L0_ffn_output_experts)[0]
    return x

_drawn_inputs = setup_inputs


def setup_inputs(seed=0):
    import zlib

    import numpy as np

    out = dict(_drawn_inputs(seed))
    spreads = {'L0_gnn_b': (0.0, 0.1)}
    factors = {'L0_ffn_w_q': 8.0,
     'L0_ffn_w_k': 8.0,
     'L0_ffn_w_gate': 4.557,
     'L0_ffn_value_experts': 4.481,
     'L0_ffn_output_experts': 4.522}
    for name, (base, spread) in spreads.items():
        noise = np.random.default_rng([zlib.crc32(name.encode()), seed]).standard_normal(out[name].shape)
        drawn = base * np.exp(spread * noise) if base else spread * noise
        out[name] = jnp.asarray(drawn.astype(out[name].dtype))
    for name, factor in factors.items():
        out[name] = (out[name] * factor).astype(out[name].dtype)
    return out
```

```python
from contextlib import ExitStack

import concourse.bass as bass
from concourse import mybir

F32 = mybir.dt.float32
F32R = mybir.dt.float32r
BF16 = mybir.dt.bfloat16
FP16 = mybir.dt.float16
I32 = mybir.dt.int32
U16 = mybir.dt.uint16
ALU = mybir.AluOpType
ACT = mybir.ActivationFunctionType
AX_X = mybir.AxisListType.X

P = 128
N = 1250
D = 1024
E = 40000
HEADS, DH, EXPERTS = 8, 64, 8
PAIRS = HEADS // 2
TILES = -(-N // P)
NP = TILES * P
LAST = N - (TILES - 1) * P
KT = D // P
HALF = 512
SCALE = DH ** -0.5
LN_EPS = 1e-5
NEG = -3.0e38

GROUP = 512
SUB = GROUP // P
GROUPS = -(-E // GROUP)
FULL_GROUPS = E // GROUP
REST = E - FULL_GROUPS * GROUP
BLOCK = 32
BLOCKS = NP // BLOCK
KEYS = BLOCK * TILES
BLOCK_KEY = 1024
OH_SLOTS = 2
PART = SUB // OH_SLOTS
POOL_SUBS = 1

RING, RAW = 10, 4

SLOTS = {
    "W0": [0, 1, 2, 3, 4, 5, 6, 7],
    "W1": [8, 9, 0, 1, 2, 3, 4, 5],
    "G": [6],
    "VA": [0, 1, 2, 3, 4, 5, 6, 7],
    "O0": [8, 9, 0, 1, 2, 3, 4, 5],
    "O1": [6, 7, 8, 9, 0, 1, 2, 3],
    "QK": [4, 5, 6, 7],
    "VB": [8, 9, 2, 3, 4, 5, 6, 7],
}
FIRST = [("W0", 0), ("W1", 0), ("G", 0), ("VA", 0), ("QK", 0), ("VB", 0)]
EACH = ["VA", "O0", "O1", "QK", "VB"]


def plan_chunks():
    stages = FIRST + [(s, p) for p in range(1, PAIRS) for s in EACH] + [("O0", PAIRS), ("O1", PAIRS)]
    first, before, held, n = {}, {}, {}, 0
    for stage in stages:
        first[stage] = n
        for k, slot in enumerate(SLOTS[stage[0]]):
            before[stage, k] = held.get(slot, -1)
            held[slot] = n
            n += 1
    return first, before


CHUNK_FIRST, CHUNK_BEFORE = plan_chunks()
PER_PAIR = sum(len(SLOTS[s]) for s in EACH)


def chunk_number(stage, p, k):
    if isinstance(p, int):
        return CHUNK_FIRST[stage, p] + k
    return (CHUNK_FIRST[stage, 1] - PER_PAIR + k) + p * PER_PAIR


def chunk_raw(stage, p, k):
    if isinstance(p, int):
        n = CHUNK_FIRST[stage, p] + k
        return n % RAW, n // RAW + 1
    n = CHUNK_FIRST[stage, 1] + k
    return n % RAW, p * (PER_PAIR // RAW) + (n // RAW + 1 - PER_PAIR // RAW)


def chunk_before(stage, p, k):
    if isinstance(p, int):
        return CHUNK_BEFORE[(stage, p), k] + 1
    gap = CHUNK_FIRST[stage, 1] + k - CHUNK_BEFORE[(stage, 1), k]
    for q in range(2, PAIRS):
        assert gap == CHUNK_FIRST[stage, q] + k - CHUNK_BEFORE[(stage, q), k] or stage == "VA"
    if stage == "VA":
        gap = min(CHUNK_FIRST[stage, q] + k - CHUNK_BEFORE[(stage, q), k] for q in range(1, PAIRS))
    return chunk_number(stage, p, k) - gap + 1


assert PER_PAIR % RAW == 0


def wait(engine, semaphore, value):
    if not isinstance(value, int) or value > 0:
        engine.wait_ge(semaphore, value)


def build(nc, x, src, dst, gnn_w, gnn_b, w_q, w_k, w_gate, value_experts, output_experts, out):
    with ExitStack() as ctx:
        def sem(name):
            return ctx.enter_context(nc.semaphore(name))

        base = (nc.sbuf_base + 63) // 64 * 64
        limit = nc.sbuf_usable_end

        def at(name, offset, shape, dtype):
            size = mybir.dt.size(dtype)
            for s in shape[1:]:
                size *= s
            assert base + offset + size <= limit, (name, base + offset + size, limit)
            return nc.alloc_sbuf_tensor_at(name, shape, dtype, offset=base + offset)

        class Region:
            def __init__(self, start):
                self.next = start

            def put(self, name, shape, dtype):
                t = at(name, self.next, shape, dtype)
                size = mybir.dt.size(dtype)
                for s in shape[1:]:
                    size *= s
                self.next += -(-size // 32) * 32
                return t

        r = Region(0)
        wide_at = 0
        xT_hi = r.put("xT_hi", [P, KT, NP], F32R)
        xT_lo = r.put("xT_lo", [P, KT, NP], F32R)
        ring_hi = r.put("ring_hi", [P, RING, HALF], F32R)
        ring_lo = r.put("ring_lo", [P, RING, HALF], F32R)
        raw = r.put("raw", [P, RAW, HALF], F32)
        ident = r.put("ident", [P, P], F32)
        ident_b = r.put("ident_b", [P, P], BF16)
        causal = r.put("causal", [P, 2, 2 * P], BF16)
        rank = r.put("rank", [P, EXPERTS], F32)
        ones = r.put("ones", [P, P], F32)
        mv = r.put("mv", [P, TILES, 2], F32)
        rstd = r.put("rstd", [P, TILES], F32)
        nt = r.put("nt", [P, 4, TILES], F32)
        stats = r.put("stats", [P, 2, 6], F32)
        dinv = r.put("dinv", [P, TILES], F32)
        rowstat = r.put("rowstat", [P, 4, 2], F32)
        scratch = r.put("scratch", [P, 8], F32)
        z = r.next

        a_f = at("a_f", wide_at, [P, TILES, NP], F32)
        r = Region(z)
        h_at = z
        h = r.put("h", [P, TILES, D], F32)
        a_at = r.next
        a_u16 = r.put("a_u16", [P, TILES, NP], U16)
        oh_at = r.next
        onehot = r.put("onehot", [P, OH_SLOTS, PART, P + KEYS], BF16)
        iota = r.put("iota", [P, KEYS], FP16)
        keyT = r.put("keyT", [P, GROUPS, SUB], F32)
        modT = r.put("modT", [P, GROUPS, SUB], F32)
        krel = r.put("krel", [P, SUB], F32)
        srel = r.put("srel", [P, SUB], F32)
        zeros_b = r.put("zeros_b", [P, KEYS], BF16)
        key_offset = r.put("key_offset", [P, BLOCKS], F32)
        table_row = r.put("table_row", [1, BLOCKS * 3], I32)
        r = Region(h_at)
        e_dst = r.put("e_dst", [GROUPS, GROUP], I32)
        e_dst_hi = r.put("e_dst_hi", [GROUPS, GROUP], I32)
        e_src = r.put("e_src", [GROUPS, GROUP], I32)
        e_t0 = r.put("e_t0", [GROUPS, GROUP], I32)
        e_t1 = r.put("e_t1", [GROUPS, GROUP], I32)
        f_dst = r.put("f_dst", [GROUPS, GROUP], F32)
        f_dst_hi = r.put("f_dst_hi", [GROUPS, GROUP], F32)
        f_src = r.put("f_src", [GROUPS, GROUP], F32)
        f_key = r.put("f_key", [GROUPS, GROUP], F32)
        f_hi = r.put("f_hi", [GROUPS, GROUP], F32)
        minmax = r.put("minmax", [GROUPS, 2], F32)
        diag = r.put("diag", [GROUPS, 2 * GROUPS], F32)
        block_lo = r.put("block_lo", [P, 1], F32)
        group_no = r.put("group_no", [P, GROUPS], F32)
        before_tri = r.put("before_tri", [P, BLOCKS], F32)
        over = r.put("over", [BLOCKS, GROUPS], F32)
        over_t = r.put("over_t", [BLOCKS, 2, GROUPS], F32)
        table_f = r.put("table_f", [BLOCKS, 3], F32)
        table_i = r.put("table_i", [BLOCKS, 3], I32)
        iota_f = r.put("iota_f", [P, KEYS], F32)
        assert r.next <= a_at
        r = Region(a_at)
        xin = r.put("xin", [P, 3, D], F32)
        r = Region(a_at)
        xres = r.put("xres", [P, 2, D], F32)
        y = r.put("y", [P, D], F32)
        bias = r.put("bias", [P, D], F32)
        assert r.next <= oh_at
        r = Region(oh_at)
        a_sum = r.put("a_sum", [P, NP], F32)

        r = Region(z)
        q_st = [r.put(f"q_st{s}", [P, NP], F32R) for s in range(2)]
        kh_st = [r.put(f"kh_st{s}", [P, NP], F32R) for s in range(2)]
        kl_st = [r.put(f"kl_st{s}", [P, NP], F32R) for s in range(2)]
        v_hi = r.put("v_hi", [P, TILES, P], F32R)
        v_lo = r.put("v_lo", [P, TILES, P], F32R)
        v_raw = r.put("v_raw", [P, TILES, DH], F32)
        oT = r.put("oT", [P, NP], F32)
        top = r.put("top", [P, TILES, HEADS * EXPERTS], F32)
        gate = r.put("gate", [P, TILES, HEADS], F32)
        shared_at = r.next
        picked = r.put("picked", [P, 2, HALF], F32)
        prob = r.put("prob", [P, 2, NP], F32)
        pT_hi = r.put("pT_hi", [P, 2, HALF], F32R)
        pT_lo = r.put("pT_lo", [P, 2, HALF], F32R)
        r = Region(shared_at)
        masked = r.put("masked", [P, 4, P], F32)
        m_hi = r.put("m_hi", [P, 4, 4, P], F32R)
        m_lo = r.put("m_lo", [P, 4, 4, P], F32R)
        mask = r.put("mask", [P, 2, EXPERTS, P], BF16)
        acc = r.put("acc", [P, 2, HALF], F32)
        r = Region(shared_at)
        q_lo = r.put("q_lo", [P, NP], F32R)
        r = Region(z)
        x2in = r.put("x2in", [P, 3, D], F32)
        logitT = r.put("logitT", [HEADS * EXPERTS, NP], F32)
        g_all = r.put("g_all", [P, TILES * HEADS, EXPERTS], F32)
        g_t = r.put("g_t", [P, TILES * HEADS, EXPERTS], F32)
        g_m = r.put("g_m", [P, TILES * HEADS], F32)
        topT = r.put("topT", [HEADS * EXPERTS, NP], BF16)

        bank = ctx.enter_context(nc.psum_tensor("bank", [P, 8, HALF], F32))

        table_dram = nc.dram_tensor("table_dram", [BLOCKS * 3], I32).ap()
        x1_dram = nc.dram_tensor("x1_dram", [NP, D], F32).ap()
        topT_dram = nc.dram_tensor("topT_dram", [HEADS * EXPERTS, NP], BF16).ap()

        consts = sem("consts")
        filled = sem("filled")
        edges_in = sem("edges_in")
        table_step = sem("table_step")
        table_ready = sem("table_ready")
        table_pe = sem("table_pe")
        table_done = sem("table_done")
        table_out = sem("table_out")
        table_in = sem("table_in")
        raw_in = [sem(f"raw_in{i}") for i in range(RAW)]
        chunk_hi = sem("chunk_hi")
        chunk_lo = sem("chunk_lo")
        chunk_used = sem("chunk_used")
        xin_in = [sem(f"xin_in{i}") for i in range(3)]
        ln_step = sem("ln_step")
        ln_var = sem("ln_var")
        ln_sqrt = sem("ln_sqrt")
        ln_done = sem("ln_done")
        xT_pe = sem("xT_pe")
        xT_hi_done = sem("xT_hi_done")
        xT_lo_done = sem("xT_lo_done")
        h_pe = sem("h_pe")
        h_done = sem("h_done")
        key_ready = sem("key_ready")
        dst_ready = sem("dst_ready")
        held = sem("held")
        srel_ready = sem("srel_ready")
        src_ready = sem("src_ready")
        onehot_used = sem("onehot_used")
        block_pe = sem("block_pe")
        block_done = sem("block_done")
        a_ready = sem("a_ready")
        a_diag = sem("a_diag")
        a_step = sem("a_step")
        a_summed = sem("a_summed")
        deg_pe = sem("deg_pe")
        h_scaled = sem("h_scaled")
        agg_pe = sem("agg_pe")
        agg_read = sem("agg_read")
        xres_in = [sem(f"xres_in{i}") for i in range(2)]
        bias_in = sem("bias_in")
        x1_ready = sem("x1_ready")
        x1_out = [sem(f"x1_out{i}") for i in range(2)]
        x2_in = [sem(f"x2_in{i}") for i in range(3)]
        gate_pe = sem("gate_pe")
        gate_act = sem("gate_act")
        gate_step = sem("gate_step")
        topT_out = sem("topT_out")

        values_pe = sem("values_pe")
        picked_done = sem("picked_done")
        value_done = sem("value_done")
        v_step = sem("v_step")
        qk_hi = sem("qk_hi")
        qk_lo = sem("qk_lo")
        qk_in = sem("qk_in")
        sim_pe = sem("sim_pe")
        max_done = sem("max_done")
        neg_done = sem("neg_done")
        exp_done = sem("exp_done")
        inv_done = sem("inv_done")
        norm_done = sem("norm_done")
        prob_done = sem("prob_done")
        pT_pe = sem("pT_pe")
        pT_hi_done = sem("pT_hi_done")
        pT_lo_done = sem("pT_lo_done")
        pv_pe = sem("pv_pe")
        o_done = sem("o_done")
        mask_in = [sem(f"mask_in{i}") for i in range(2)]
        masked_done = sem("masked_done")
        m_hi_done = sem("m_hi_done")
        m_lo_done = sem("m_lo_done")
        m_used = sem("m_used")
        acc_in = [sem(f"acc_in{i}") for i in range(2)]
        acc_done = sem("acc_done")

        block = ctx.enter_context(nc.Block())

        def cols(t, width=P):
            return slice(t * width, (t + 1) * width)

        def load_chunks(eng, stage, p, begin=0, end=KT):
            for k in range(begin, min(end, len(SLOTS[stage]))):
                slot, times = chunk_raw(stage, p, k)
                wait(eng, chunk_lo, chunk_number(stage, p, k) - RAW + 1)
                to = raw[:, slot, :]
                if stage in ("W0", "W1"):
                    n = int(stage[1])
                    of = gnn_w[cols(k), cols(n, HALF)]
                elif stage == "G":
                    to = to.rearrange("p (k c) -> p k c", k=KT)
                    of = w_gate.rearrange("(k p) c -> p k c", p=P)
                elif stage in ("VA", "VB"):
                    head = 2 * p + (stage == "VB")
                    to = to.rearrange("p (e c) -> p e c", e=EXPERTS)
                    of = value_experts[:, bass.ds(head, 1), cols(k), :].rearrange("e h d c -> d (e h) c")
                elif stage in ("O0", "O1"):
                    pair = p - 1
                    of = output_experts[k, bass.ds(2 * pair, 2), :, cols(int(stage[1]), HALF)].rearrange("h c n -> (h c) n")
                else:
                    w = (w_q, w_k)[k // 2]
                    to = to.rearrange("p (k c) -> p k c", k=4)
                    of = w.rearrange("(k p) c -> p k c", p=P)[:, 4 * (k % 2):4 * (k % 2) + 4, bass.ds(P * p, P)]
                eng.dma_start(to, of).then_inc(raw_in[slot], 16)

        def wait_dense(eng, done, stage, p, n, t):
            if t < TILES - 1:
                eng.wait_ge(done, (TILES - 1) * n + t + 1)
            else:
                eng.wait_ge(chunk_used, chunk_number(stage, p, KT - 1) + 1)

        def split_hi(act, stage, p):
            for k, place in enumerate(SLOTS[stage]):
                slot, times = chunk_raw(stage, p, k)
                wait(act, raw_in[slot], times * 16)
                wait(act, chunk_used, chunk_before(stage, p, k))
                act.activation(ring_hi[:, place, :], raw[:, slot, :], ACT.Copy).then_inc(chunk_hi, 1)

        def split_lo(dve, stage, p):
            for k, place in enumerate(SLOTS[stage]):
                slot, times = chunk_raw(stage, p, k)
                wait(dve, chunk_hi, chunk_number(stage, p, k) + 1)
                dve.tensor_tensor(ring_lo[:, place, :], raw[:, slot, :], ring_hi[:, place, :],
                                  ALU.subtract).then_inc(chunk_lo, 1)

        def three(pe, acc_ap, w_hi, w_lo, m_hi_ap, m_lo_ap, start, stop):
            return [pe.matmul(acc_ap, w_hi, m_hi_ap, start=start, stop=False),
                    pe.matmul(acc_ap, w_hi, m_lo_ap, start=False, stop=False),
                    pe.matmul(acc_ap, w_lo, m_hi_ap, start=False, stop=stop)]

        @block.sync
        def _(sp):
            sp.wait_ge(filled, 3)
            for to, of in ((e_dst, dst), (e_dst_hi, dst), (e_src, src)):
                sp.dma_start(to[0:FULL_GROUPS, :], of[0:FULL_GROUPS * GROUP].rearrange("(g q) -> g q", q=GROUP)).then_inc(edges_in, 16)
                sp.dma_start(to[FULL_GROUPS:GROUPS, 0:REST], of[FULL_GROUPS * GROUP:E].rearrange("(g q) -> g q", g=1)).then_inc(edges_in, 16)

            def load_x(t):
                if t >= 3:
                    sp.wait_ge(xT_pe, t - 2)
                if t < TILES - 1:
                    sp.dma_start(xin[:, t % 3, :], x[cols(t), :]).then_inc(xin_in[t % 3], 16)
                else:
                    sp.wait_ge(filled, 4)
                    sp.dma_start(xin[0:LAST, t % 3, :], x[t * P:N, :]).then_inc(xin_in[t % 3], 16)

            for t in range(3):
                load_x(t)
            load_chunks(sp, "W0", 0)
            sp.wait_ge(table_done, 1)
            sp.dma_start(table_dram.rearrange("(b c) -> b c", c=3), table_i[:, :]).then_inc(table_out, 16)
            sp.wait_ge(table_out, 16)
            sp.dma_start(table_row[:, :], table_dram.rearrange("(a n) -> a n", a=1)).then_inc(table_in, 16)
            for t in range(3, TILES):
                load_x(t)
            load_chunks(sp, "W1", 0)
            load_chunks(sp, "G", 0)
            sp.wait_ge(a_summed, 1)
            sp.wait_ge(a_ready, TILES)
            sp.dma_start(bias[:, :], gnn_b.rearrange("(a n) -> a n", a=1).broadcast_to([P, D])).then_inc(bias_in, 16)

            def store_x1(t):
                sp.wait_ge(x1_ready, t + 1)
                sp.dma_start(x1_dram[cols(t), :], xres[:, t % 2, :]).then_inc(x1_out[t % 2], 16)

            for t in range(TILES):
                if t >= 2:
                    store_x1(t - 2)
                    sp.wait_ge(x1_out[t % 2], 16 * (t // 2))
                    sp.wait_ge(ln_var, TILES + t)
                if t < TILES - 1:
                    sp.dma_start(xres[:, t % 2, :], x[cols(t), :]).then_inc(xres_in[t % 2], 16)
                else:
                    sp.wait_ge(filled, 5)
                    sp.dma_start(xres[0:LAST, t % 2, :], x[t * P:N, :]).then_inc(xres_in[t % 2], 16)
            store_x1(TILES - 2)
            store_x1(TILES - 1)
            for i in range(2):
                sp.wait_ge(x1_out[i], 16 * TILES // 2)
            sp.wait_ge(agg_pe, TILES)
            for t in range(TILES):
                if t >= 3:
                    sp.wait_ge(xT_pe, TILES + t - 2)
                sp.dma_start(x2in[:, t % 3, :], x1_dram[cols(t), :]).then_inc(x2_in[t % 3], 16)

            def moe_in(p, m):
                t, n = m % TILES, m // TILES
                sp.wait_ge(masked_done, (20 * p + m - 1) * 2)
                for s in range(2):
                    rows = topT_dram[bass.ds((2 * (p - 1) + s) * EXPERTS, EXPERTS), cols(t)]
                    sp.dma_start(mask[s * DH:(s + 1) * DH, t % 2, :, :],
                                 rows.unsqueeze(0).broadcast_to([DH, EXPERTS, P])).then_inc(mask_in[t % 2], 16)
                sp.wait_ge(x1_out[t % 2], (5 + (p - 1) * 10 + m // 2) * 16)
                rows = LAST if t == TILES - 1 else P
                sp.dma_start(acc[0:rows, t % 2, :], x1_dram[t * P:t * P + rows, cols(n, HALF)]).then_inc(acc_in[t % 2], 16)

            def moe_out(p, m, to):
                t, n = m % TILES, m // TILES
                rows = LAST if t == TILES - 1 else P
                sp.wait_ge(acc_done, 20 * p + m + 1)
                sp.dma_start(to[t * P:t * P + rows, cols(n, HALF)], acc[0:rows, t % 2, :]).then_inc(x1_out[t % 2], 16)

            def moe(p, to):
                load_chunks(sp, "O0", p, 0, RAW)
                sp.wait_ge(pv_pe, (2 * p) * 15)
                if not (isinstance(p, int) and p == PAIRS):
                    sp.wait_ge(v_step, (2 * p + 1) * 3)
                moe_in(p, 0)
                load_chunks(sp, "O0", p, RAW)
                load_chunks(sp, "O1", p, 0, RAW)
                for m in range(2 * TILES):
                    if m < 2 * TILES - 1:
                        moe_in(p, m + 1)
                    if m == TILES - 1:
                        load_chunks(sp, "O1", p, RAW)
                    moe_out(p, m, to)

            load_chunks(sp, "VA", 0)
            load_chunks(sp, "QK", 0)
            load_chunks(sp, "VB", 0)
            sp.wait_ge(topT_out, 16)
            with sp.Fori(1, PAIRS) as p:
                load_chunks(sp, "VA", p)
                moe(p, x1_dram)
                load_chunks(sp, "QK", p)
                load_chunks(sp, "VB", p)
            moe(PAIRS, out)
            for i in range(2):
                sp.wait_ge(x1_out[i], (5 + PAIRS * 10) * 16)

        @block.gpsimd
        def _(pool):
            exact = dict(channel_multiplier=0, base=0, allow_small_or_imprecise_dtypes=True)
            pool.iota(iota_f[:, :], [[1, KEYS]], **exact).then_inc(consts, 1)
            pool.iota(group_no[:, :], [[1, GROUPS]], **exact).then_inc(consts, 1)
            pool.iota(key_offset[:, :], [[-BLOCK_KEY, BLOCKS]], **exact).then_inc(consts, 1)
            pool.iota(block_lo[:, :], [[0, 1]], base=0, channel_multiplier=BLOCK,
                      allow_small_or_imprecise_dtypes=True).then_inc(consts, 1)
            pool.iota(rank[:, :], [[-1, EXPERTS]], base=EXPERTS, channel_multiplier=0,
                      allow_small_or_imprecise_dtypes=True).then_inc(consts, 1)
            pool.memset(ident[:, :], 0.0).then_inc(consts, 1)
            pool.memset(ident_b[:, :], 0.0).then_inc(consts, 1)
            pool.memset(causal[:, :, :], 0.0).then_inc(consts, 1)
            pool.memset(before_tri[:, :], 1.0).then_inc(consts, 1)
            pool.wait_ge(consts, 9)
            for m in (ident, ident_b):
                pool.affine_select(out=m[:, :], in_=m[:, :], compare_op=ALU.not_equal, fill=1.0, base=0,
                                   pattern=[[-1, P]], channel_multiplier=1).then_inc(consts, 1)
            for i in range(2):
                pool.affine_select(out=causal[:, i, :], in_=causal[:, i, :], compare_op=ALU.is_ge, fill=NEG,
                                   base=P * i, pattern=[[-1, 2 * P]], channel_multiplier=1).then_inc(consts, 1)
            pool.affine_select(out=before_tri[:, :], in_=before_tri[:, :], compare_op=ALU.is_gt, fill=0.0, base=0,
                               pattern=[[1, BLOCKS]], channel_multiplier=-1).then_inc(consts, 1)

            def hold(i):
                return pool.tensor_tensor(scratch[:, i:i + 1], ident[:, 0:1], ident[:, 0:1], ALU.add)

            pool.wait_ge(consts, 14)
            for i, (semaphore, start) in enumerate((
                    (masked_done, 40), (m_hi_done, 40), (m_lo_done, 40), (m_used, 40),
                    (acc_done, 20))):
                pool.memset(scratch[:, 3 + i:4 + i], 0.0).then_inc(semaphore, start)

            pool.wait_ge(table_in, 16)
            for b in range(BLOCKS):
                first = pool.value_load(table_row[0:1, 3 * b:3 * b + 1], min_val=0, max_val=GROUPS - 1)
                count = pool.value_load(table_row[0:1, 3 * b + 1:3 * b + 2], min_val=1, max_val=GROUPS)
                past = pool.value_load(table_row[0:1, 3 * b + 2:3 * b + 3], min_val=0, max_val=GROUPS * BLOCKS)
                with pool.Fori(0, count) as i:
                    g = (first + i).with_bounds(min_val=0, max_val=GROUPS - 1)
                    pool.wait_ge(src_ready, OH_SLOTS * (past + i) + 1)
                    pool.tensor_copy(srel[:, :], modT[:, bass.ds(g, 1), :].rearrange("p a s -> p (a s)")).then_inc(srel_ready, 1)
                    for slot in range(OH_SLOTS):
                        pool.wait_ge(srel_ready, past + i + 1)
                        pool.wait_ge(onehot_used, OH_SLOTS * (past + i) + slot + 1)
                        hold(slot)
                        for s in range(POOL_SUBS):
                            last = pool.tensor_scalar(onehot[:, slot, s, 0:P], iota[:, 0:P],
                                                      srel[:, PART * slot + s:PART * slot + s + 1], None, ALU.is_equal)
                        last.then_inc(src_ready, 1)

            def stack_halves(p):
                pool.wait_ge(qk_lo, 4 * p + 4)
                if not isinstance(p, int):
                    pool.wait_ge(held, p)
                hold(OH_SLOTS).then_inc(held, 1)
                low, high = slice(0, DH), slice(DH, P)
                for to, of in (
                    (q_st[0][high, :], q_lo[low, :]), (kh_st[0][high, :], kh_st[0][low, :]),
                    (kl_st[0][high, :], kl_st[0][low, :]), (q_st[1][low, :], q_lo[high, :]),
                    (kh_st[1][low, :], kh_st[1][high, :]), (kl_st[1][low, :], kl_st[1][high, :]),
                ):
                    pool.dma_start(to, of).then_inc(qk_in, 16)

            stack_halves(0)
            with pool.Fori(1, PAIRS) as p:
                stack_halves(p)

        @block.scalar
        def _(act):
            def sqrt_of(w, n):
                act.wait_ge(ln_var, n)
                act.activation(nt[:, 1, 0:w], nt[:, 0, 0:w], ACT.Sqrt).then_inc(ln_sqrt, 1)

            def xT_hi_part(t, n):
                act.wait_ge(xT_pe, n + 1)
                b = 2 * (n % 2)
                act.activation(xT_hi[:, :, cols(t)], bank[:, b:b + 2, :].rearrange("p b (k c) -> p (b k) c", c=P),
                               ACT.Copy).then_inc(xT_hi_done, 1)

            def h_part(n, t):
                u = n * TILES + t
                wait_dense(act, h_pe, f"W{n}", 0, n, t)
                act.activation(h[:, t, cols(n, HALF)], bank[:, 4 + u % 2, :], ACT.Copy).then_inc(h_done, 1)

            split_hi(act, "W0", 0)
            act.wait_ge(table_done, 1)
            act.wait_ge(table_out, 16)
            for t in range(TILES):
                sqrt_of(1, t + 1)
                xT_hi_part(t, t)
                if t >= 1:
                    h_part(0, t - 1)
            h_part(0, TILES - 1)
            split_hi(act, "W1", 0)
            for t in range(TILES):
                h_part(1, t)
                for b in range(t * BLOCKS // TILES, (t + 1) * BLOCKS // TILES):
                    act.wait_ge(block_pe, b + 1)
                    act.activation(a_u16[:, :, cols(b, BLOCK)],
                                   bank[:, 6 + b % 2, 0:KEYS].rearrange("p (d s) -> p s d", s=TILES),
                                   ACT.Copy).then_inc(block_done, 1)
            act.wait_ge(block_done, BLOCKS)
            for t in range(TILES):
                act.activation(a_f[:, t, :], a_u16[:, t, :], ACT.Copy).then_inc(a_ready, 1)
            sqrt_of(TILES, TILES + 1)
            for t in range(TILES):
                sqrt_of(1, TILES + 2 + t)
            split_hi(act, "G", 0)
            for t in range(TILES):
                xT_hi_part(t, TILES + t)
            act.wait_ge(gate_pe, 1)
            act.activation(logitT[:, :], bank[0:HEADS * EXPERTS, 2:5, :].rearrange("p b c -> p (b c)")[:, 0:NP],
                           ACT.Copy).then_inc(gate_act, 1)
            act.wait_ge(gate_pe, 2)
            act.activation(g_all[:, :, :].rearrange("p a e -> p (a e)"),
                           bank[:, 5:7, :].rearrange("p b c -> p (b c)")[:, 0:TILES * HEADS * EXPERTS],
                           ACT.Sigmoid).then_inc(gate_act, 1)
            act.wait_ge(gate_pe, 3)
            act.activation(topT[:, :], bank[0:HEADS * EXPERTS, 2:5, :].rearrange("p b c -> p (b c)")[:, 0:NP],
                           ACT.Copy).then_inc(gate_act, 1)
            act.wait_ge(gate_act, 3)
            act.dma_start(topT_dram, topT[:, :]).then_inc(topT_out, 16)
            split_hi(act, "VA", 0)

            def exps(g, i, w):
                n = 10 * g + i
                act.wait_ge(neg_done, n + 1)
                wait(act, pT_pe, 15 * g + (i // 2) * (i // 2 + 1) // 2)
                act.activation(prob[:, i % 2, 0:w], bank[:, 2:5, :].rearrange("p b c -> p (b c)")[:, 0:w], ACT.Exp,
                               bias=rowstat[:, 0, i % 2:i % 2 + 1], scale=SCALE,
                               accum_out=rowstat[:, 1, i % 2:i % 2 + 1]).then_inc(exp_done, 1)

            def pT_hi_parts(g, s, q):
                for j in range(q + 1):
                    n = 15 * g + q * (q + 1) // 2 + j
                    b = (15 * s + q * (q + 1) // 2 + j) % 2
                    act.wait_ge(pT_pe, n + 1)
                    wait(act, pv_pe, n - 1)
                    act.activation(pT_hi[:, b, :], bank[:, 5 + b, :], ACT.Copy).then_inc(pT_hi_done, 1)
                act.wait_ge(pv_pe, 15 * g + (q + 1) * (q + 2) // 2)
                part = slice(s * DH, (s + 1) * DH)
                side = (s + q) % 2
                act.activation(oT[part, cols(q, 2 * P)], bank[part, 7, cols(side, 2 * P)], ACT.Copy).then_inc(o_done, 1)

            def attention(g, s):
                if s == 0:
                    act.wait_ge(masked_done, 20 * g + 40)
                    act.wait_ge(m_used, 20 * g + 40)
                    act.wait_ge(qk_in, 48 * g + 96)
                for i in range(TILES):
                    exps(g, i, (i // 2 + 1) * 2 * P)
                    if i % 2:
                        pT_hi_parts(g, s, i // 2)

            def qk_hi_parts(p):
                for m in range(2):
                    act.wait_ge(chunk_used, chunk_number("QK", p, 2 * m + 1) + 1)
                    b = 2 + 3 * m
                    for s in range(2):
                        part = slice(s * DH, (s + 1) * DH)
                        to = (q_st, kh_st)[m][s]
                        act.activation(to[part, :], bank[part, b:b + 3, :].rearrange("p b c -> p (b c)")[:, 0:NP],
                                       ACT.Copy).then_inc(qk_hi, 1)

            def pair(p):
                if not isinstance(p, int):
                    attention(2 * p - 1, 1)
                    split_hi(act, "O0", p)
                    moe_hi_half(p, 0)
                    split_hi(act, "O1", p)
                    moe_hi_half(p, 1)
                split_hi(act, "QK", p)
                qk_hi_parts(p)
                split_hi(act, "VB", p)
                attention(2 * p, 0)

            def moe_hi_half(p, half):
                for n in range(20 * half, 20 * half + 20):
                    G = 40 * p + n
                    act.wait_ge(masked_done, G + 1)
                    act.wait_ge(m_used, G - 3)
                    act.activation(m_hi[:, n % 4, :, :], masked[:, :, :], ACT.Copy).then_inc(m_hi_done, 1)

            pair(0)
            with act.Fori(1, PAIRS) as p:
                split_hi(act, "VA", p)
                pair(p)
            attention(2 * PAIRS - 1, 1)
            split_hi(act, "O0", PAIRS)
            moe_hi_half(PAIRS, 0)
            split_hi(act, "O1", PAIRS)
            moe_hi_half(PAIRS, 1)

        @block.tensor
        def _(pe):
            def transposes(n, tiles_in):
                pe.wait_ge(ln_done, n + 1)
                if n >= 2:
                    pe.wait_ge(xT_lo_done, n - 1)
                b = 2 * (n % 2)
                for k in range(KT):
                    last = pe.transpose(bank[:, b + k // 4, cols(k % 4)], tiles_in[:, (n % TILES) % 3, cols(k)], ident[:, :])
                last.then_inc(xT_pe, 1)

            def dense(stage, p, t, acc_ap, done):
                for k, place in enumerate(SLOTS[stage]):
                    if t == 0:
                        pe.wait_ge(chunk_lo, chunk_number(stage, p, k) + 1)
                    last = three(pe, acc_ap, xT_hi[:, k, cols(t)], xT_lo[:, k, cols(t)],
                                 ring_hi[:, place, :], ring_lo[:, place, :], k == 0, k == KT - 1)[-1]
                    if t == TILES - 1:
                        last.then_inc(chunk_used, 1)
                if t < TILES - 1:
                    last.then_inc(done, 1)

            pe.wait_ge(consts, 14)
            pe.wait_ge(table_ready, 1)
            for n, of in enumerate((f_key, f_src)):
                for s in range(SUB):
                    last = pe.transpose(bank[:, 4 + n, cols(s, GROUPS)], of[:, cols(s)], ident[0:GROUPS, 0:GROUPS])
                last.then_inc(table_pe, 1)
            pe.matmul(bank[0:BLOCKS, 6, 0:2 * GROUPS], ones[0:GROUPS, 0:BLOCKS], diag[:, :],
                      start=True, stop=True).then_inc(table_pe, 1)
            pe.wait_ge(table_ready, 2)
            pe.matmul(bank[0:BLOCKS, 7, 0:1], before_tri[0:BLOCKS, :], table_f[:, 1:2],
                      start=True, stop=True).then_inc(table_pe, 1)
            pe.wait_ge(table_done, 1)

            def h_unit(n, t):
                u = n * TILES + t
                pe.wait_ge(xT_lo_done, t + 1)
                if u >= 2:
                    pe.wait_ge(h_done, u - 1)
                dense(f"W{n}", 0, t, bank[:, 4 + u % 2, :], h_pe)

            for t in range(TILES + 1):
                if t < TILES:
                    transposes(t, xin)
                if t >= 1:
                    h_unit(0, t - 1)
            pe.wait_ge(table_in, 16)
            for t in range(TILES):
                h_unit(1, t)
                for b in range(t * BLOCKS // TILES, (t + 1) * BLOCKS // TILES):
                    count = pe.value_load(table_row[0:1, 3 * b + 1:3 * b + 2], min_val=1, max_val=GROUPS)
                    past = pe.value_load(table_row[0:1, 3 * b + 2:3 * b + 3], min_val=0, max_val=GROUPS * BLOCKS)
                    counts = bank[:, 6 + b % 2, 0:KEYS]
                    if b >= 2:
                        pe.wait_ge(block_done, b - 1)
                    free = dict(skip_group_check=True)
                    pe.matmul(counts, zeros_b[:, 0:P], zeros_b[:, :], start=True, stop=False, **free)
                    with pe.Fori(0, count) as i:
                        for slot in range(OH_SLOTS):
                            pe.wait_ge(dst_ready, OH_SLOTS * (past + i) + slot + 2)
                            pe.wait_ge(src_ready, OH_SLOTS * (past + i) + slot + 2)
                            for s in range(PART):
                                last = pe.matmul(counts, onehot[:, slot, s, 0:P], onehot[:, slot, s, P:P + KEYS],
                                                 start=False, stop=False, **free)
                            last.then_inc(onehot_used, 1)
                    pe.matmul(counts, zeros_b[:, 0:P], zeros_b[:, :], start=False, stop=True, **free).then_inc(block_pe, 1)
            pe.wait_ge(a_summed, 1)
            for t in range(TILES):
                last = pe.matmul(bank[:, 4, t:t + 1], a_sum[:, cols(t)], ones[:, 0:1], start=True, stop=True)
            last.then_inc(deg_pe, 1)
            pe.wait_ge(a_diag, TILES)
            pe.wait_ge(h_scaled, TILES)
            for t in range(TILES):
                if t >= 2:
                    pe.wait_ge(agg_read, t - 1)
                for u in range(TILES):
                    for n in range(2):
                        last = pe.matmul(bank[:, 2 * (t % 2) + n, :], a_f[:, u, cols(t)], h[:, u, cols(n, HALF)],
                                         start=(u == 0), stop=(u == TILES - 1))
                last.then_inc(agg_pe, 1)
            pe.wait_ge(agg_read, TILES)
            for t in range(TILES):
                transposes(TILES + t, x2in)
            pe.wait_ge(xT_lo_done, 2 * TILES)
            pe.wait_ge(chunk_lo, chunk_number("G", 0, 0) + 1)
            GE = HEADS * EXPERTS
            place = SLOTS["G"][0]
            for k in range(KT):
                for c, w in ((0, HALF), (HALF, HALF), (2 * HALF, NP - 2 * HALF)):
                    last = three(pe, bank[0:GE, 2 + c // HALF, 0:w], ring_hi[:, place, cols(k, GE)],
                                 ring_lo[:, place, cols(k, GE)], xT_hi[:, k, c:c + w], xT_lo[:, k, c:c + w],
                                 k == 0, k == KT - 1)[-1]
            last.then_inc(gate_pe, 1)
            pe.wait_ge(gate_act, 1)
            for t in range(TILES):
                last = pe.transpose(bank[:, 5 + t // 8, cols(t % 8, GE)], logitT[:, cols(t)], ident[0:GE, 0:GE])
                if t == 0:
                    last.then_inc(chunk_used, 1)
            last.then_inc(gate_pe, 1)
            pe.wait_ge(gate_step, 5)
            for t in range(TILES):
                last = pe.transpose(bank[0:GE, 2 + t // 4, cols(t % 4)], top[:, t, :], ident[:, :])
            last.then_inc(gate_pe, 1)
            pe.wait_ge(gate_act, 3)

            def values_tile(g, stage, p, t):
                n = 10 * g + t
                wait(pe, picked_done, n - 1)
                dense(stage, p, t, bank[:, t % 2, :], values_pe)

            def sim_row(g, s, i):
                n = 10 * g + i
                w = (i // 2 + 1) * 2 * P
                if i == 0:
                    if s == 0:
                        pe.wait_ge(qk_in, 48 * g + 96)
                wait(pe, exp_done, n)
                for c in range(0, w, HALF):
                    e = min(w, c + HALF)
                    to = bank[:, 2 + c // HALF, 0:e - c]
                    lhs = q_st[s][:, cols(i)]
                    pe.matmul(to, lhs, kh_st[s][:, c:e], start=True, stop=False)
                    last = pe.matmul(to, lhs, kl_st[s][:, c:e], start=False, stop=True)
                    if e == w:
                        edge = bank[:, 2 + c // HALF, e - c - 2 * P:e - c]
                        last = pe.matmul(edge, ident_b[:, :], causal[:, i % 2, :], start=False, stop=True,
                                         skip_group_check=True)
                last.then_inc(sim_pe, 1)

            def attend(g, s, q):
                pe.wait_ge(prob_done, 10 * g + 2 * q + 2)
                side = (s + q) % 2
                rows = slice(0, DH) if s == 0 else slice(0, P)
                o = bank[rows, 7, cols(side, 2 * P)]

                def products(j):
                    n = 15 * g + q * (q + 1) // 2 + j
                    b = (15 * s + q * (q + 1) // 2 + j) % 2
                    pe.wait_ge(pT_lo_done, n + 1)
                    for jj in range(2):
                        u = 2 * j + jj
                        last = three(pe, o, v_hi[:, u, rows], v_lo[:, u, rows], pT_hi[:, b, cols(jj, 2 * P)],
                                     pT_lo[:, b, cols(jj, 2 * P)], u == 0, u == 2 * q + 1)[-1]
                    last.then_inc(pv_pe, 1)

                for j in range(q + 1):
                    n = 15 * g + q * (q + 1) // 2 + j
                    b = (15 * s + q * (q + 1) // 2 + j) % 2
                    wait(pe, pT_lo_done, n - 1)
                    for jj in range(2):
                        for i in range(2):
                            last = pe.transpose(bank[:, 5 + b, (2 * jj + i) * P:(2 * jj + i + 1) * P],
                                                prob[:, i, cols(2 * j + jj)], ident[:, :])
                    last.then_inc(pT_pe, 1)
                    if j == 0:
                        pe.wait_ge(v_step, 3 * g + 3)
                        wait(pe, o_done, 5 * g + q - 1)
                    else:
                        products(j - 1)
                products(q)

            def values_and_attention(gv, stage, p, ga, sa):
                for t in range(TILES):
                    if ga is not None:
                        sim_row(ga, sa, t)
                    values_tile(gv, stage, p, t)
                    if ga is not None and t % 2:
                        attend(ga, sa, t // 2)

            def qk(p):
                for m in range(2):
                    b = 2 + 3 * m
                    if m == 0:
                        wait(pe, exp_done, 20 * p)
                        wait(pe, pT_lo_done, 30 * p)
                        wait(pe, o_done, 10 * p)
                    for j in range(2):
                        place = SLOTS["QK"][2 * m + j]
                        pe.wait_ge(chunk_lo, chunk_number("QK", p, 2 * m + j) + 1)
                        for kk in range(4):
                            k = 4 * j + kk
                            for c, w in ((0, HALF), (HALF, HALF), (2 * HALF, NP - 2 * HALF)):
                                last = three(pe, bank[:, b + c // HALF, 0:w], ring_hi[:, place, cols(kk)],
                                             ring_lo[:, place, cols(kk)], xT_hi[:, k, c:c + w], xT_lo[:, k, c:c + w],
                                             k == 0, k == KT - 1)[-1]
                        last.then_inc(chunk_used, 1)

            def moe(p):
                for n in range(2):
                    stage = f"O{n}"
                    for t in range(TILES):
                        m = 20 * p + TILES * n + t
                        pe.wait_ge(acc_done, m - 1)
                        for e in range(EXPERTS):
                            G = 2 * m + e // 4
                            u = (2 * (TILES * n + t) + e // 4) % 4
                            place = SLOTS[stage][e]
                            if t == 0:
                                pe.wait_ge(chunk_lo, chunk_number(stage, p, e) + 1)
                            if e % 4 == 0:
                                pe.wait_ge(m_lo_done, G + 1)
                            of_three = three(pe, bank[:, t % 2, :], m_hi[:, u, e % 4, :], m_lo[:, u, e % 4, :],
                                             ring_hi[:, place, :], ring_lo[:, place, :], e == 0, e == EXPERTS - 1)
                            last = of_three[-1]
                            if t == TILES - 1 and e == 4:
                                of_three[0].then_inc(chunk_used, 1)
                            if e % 4 == 3:
                                last.then_inc(m_used, 1)
                            elif t == TILES - 1:
                                last.then_inc(chunk_used, 1)
                        if t == TILES - 1:
                            pe.drain().then_inc(chunk_used, 1)

            values_and_attention(0, "VA", 0, None, None)
            qk(0)
            values_and_attention(1, "VB", 0, 0, 0)
            with pe.Fori(1, PAIRS) as p:
                values_and_attention(2 * p, "VA", p, 2 * p - 1, 1)
                moe(p)
                qk(p)
                values_and_attention(2 * p + 1, "VB", p, 2 * p, 0)
            for i in range(TILES):
                sim_row(2 * PAIRS - 1, 1, i)
                if i % 2:
                    attend(2 * PAIRS - 1, 1, i // 2)
            moe(PAIRS)

        @block.vector
        def _(dve):
            dve.memset(e_dst[:, :], -(1 << 20)).then_inc(filled, 1)
            dve.memset(e_dst_hi[:, :], 1 << 20).then_inc(filled, 1)
            dve.memset(e_src[:, :], 0).then_inc(filled, 1)
            steps = {}

            def chain(ins, semaphore=table_step):
                steps[id(semaphore)] = steps.get(id(semaphore), 0) + 1
                ins.then_inc(semaphore, 1)
                dve.wait_ge(semaphore, steps[id(semaphore)])

            dve.memset(ones[:, :], 1.0).then_inc(table_step, 1)
            dve.memset(krel[:, :], 0.0).then_inc(dst_ready, 1)
            dve.memset(srel[:, :], 0.0).then_inc(src_ready, 1)
            dve.memset(zeros_b[:, :], 0.0).then_inc(onehot_used, OH_SLOTS)
            steps[id(table_step)] = 1
            split_lo(dve, "W0", 0)
            dve.wait_ge(consts, 14)
            dve.wait_ge(edges_in, 96)
            chain(dve.tensor_copy(iota[:, :], iota_f[:, :]))
            chain(dve.tensor_single_scalar(e_t0[:, :], e_dst[:, :], 5, ALU.arith_shift_right))
            chain(dve.tensor_single_scalar(e_t1[:, :], e_src[:, :], 7, ALU.arith_shift_right))
            for to, of in ((f_dst, e_dst), (f_dst_hi, e_dst_hi), (f_src, e_src), (f_key, e_t0), (f_hi, e_t1)):
                chain(dve.tensor_copy(to[:, :], of[:, :]))
            chain(dve.tensor_reduce(minmax[:, 0:1], f_dst_hi[:, :], AX_X, ALU.min))
            chain(dve.tensor_reduce(minmax[:, 1:2], f_dst[:, :], AX_X, ALU.max))
            chain(dve.tensor_scalar(f_dst_hi[:, :], f_dst[:, :], float(TILES), None, ALU.mult))
            chain(dve.scalar_tensor_tensor(out=f_key[:, :], in0=f_key[:, :], scalar=float(BLOCK_KEY - TILES * BLOCK),
                                           in1=f_dst_hi[:, :], op0=ALU.mult, op1=ALU.add))
            chain(dve.tensor_tensor(f_key[:, :], f_key[:, :], f_hi[:, :], ALU.add))
            chain(dve.scalar_tensor_tensor(out=f_src[:, :], in0=f_hi[:, :], scalar=-float(P), in1=f_src[:, :],
                                           op0=ALU.mult, op1=ALU.add))
            for i in range(2):
                last = dve.tensor_scalar(diag[:, cols(i, GROUPS)], ident[0:GROUPS, 0:GROUPS], minmax[:, i:i + 1], None,
                                         ALU.mult)
            last.then_inc(table_ready, 1)
            dve.wait_ge(table_pe, 3)
            chain(dve.tensor_copy(keyT[:, :, :].rearrange("p g s -> p s g"),
                                  bank[:, 4, 0:SUB * GROUPS].rearrange("p (s g) -> p s g", s=SUB)))
            chain(dve.tensor_copy(modT[:, :, :].rearrange("p g s -> p s g"),
                                  bank[:, 5, 0:SUB * GROUPS].rearrange("p (s g) -> p s g", s=SUB)))
            least, greatest = bank[0:BLOCKS, 6, 0:GROUPS], bank[0:BLOCKS, 6, GROUPS:2 * GROUPS]
            chain(dve.tensor_scalar(over_t[:, 0, :], least, -float(BLOCK - 1), block_lo[0:BLOCKS, :], ALU.add, ALU.is_le))
            chain(dve.tensor_scalar(over_t[:, 1, :], greatest, block_lo[0:BLOCKS, :], None, ALU.is_ge))
            chain(dve.tensor_tensor(over[:, :], over_t[:, 0, :], over_t[:, 1, :], ALU.mult))
            chain(dve.scalar_tensor_tensor(out=over_t[:, 0, :], in0=over[:, :], scalar=-1000.0,
                                           in1=group_no[0:BLOCKS, :], op0=ALU.mult, op1=ALU.add))
            chain(dve.tensor_reduce(table_f[:, 0:1], over_t[:, 0, :], AX_X, ALU.min))
            chain(dve.tensor_scalar(table_f[:, 0:1], table_f[:, 0:1], 1000.0, float(GROUPS - 1), ALU.add, ALU.min))
            chain(dve.scalar_tensor_tensor(out=over_t[:, 1, :], in0=group_no[0:BLOCKS, :], scalar=1.0,
                                           in1=over[:, :], op0=ALU.add, op1=ALU.mult))
            chain(dve.tensor_reduce(table_f[:, 1:2], over_t[:, 1, :], AX_X, ALU.max))
            chain(dve.tensor_tensor(table_f[:, 1:2], table_f[:, 1:2], table_f[:, 0:1], ALU.subtract))
            dve.tensor_scalar(table_f[:, 1:2], table_f[:, 1:2], 1.0, None, ALU.max).then_inc(table_ready, 1)
            dve.wait_ge(table_ready, 2)
            dve.wait_ge(table_pe, 4)
            chain(dve.tensor_copy(table_f[:, 2:3], bank[0:BLOCKS, 7, 0:1]))
            dve.tensor_copy(table_i[:, :], table_f[:, :]).then_inc(table_done, 1)

            ln = [0]

            def ln_chain(ins):
                ln[0] += 1
                ins.then_inc(ln_step, 1)
                dve.wait_ge(ln_step, ln[0])

            roots = [0]

            def rsqrt(to, w):
                roots[0] += 1
                dve.wait_ge(ln_sqrt, roots[0])
                ln_chain(dve.reciprocal(nt[:, 2, 0:w], nt[:, 1, 0:w]))
                ln_chain(dve.tensor_tensor(nt[:, 3, 0:w], nt[:, 2, 0:w], nt[:, 2, 0:w], ALU.mult))
                ln_chain(dve.tensor_tensor(nt[:, 3, 0:w], nt[:, 3, 0:w], nt[:, 0, 0:w], ALU.mult))
                ln_chain(dve.tensor_scalar(nt[:, 3, 0:w], nt[:, 3, 0:w], -0.5, 1.5, ALU.mult, ALU.add))
                ln_chain(dve.tensor_tensor(to, nt[:, 2, 0:w], nt[:, 3, 0:w], ALU.mult))

            def statistics(tile, t):
                for n in range(2):
                    dve.bn_stats(stats[:, n, :], tile[:, cols(n, HALF)]).then_inc(ln_step, 1)
                ln[0] += 2
                dve.wait_ge(ln_step, ln[0])
                ln_chain(dve.bn_aggr(mv[:, t, :], stats[:, :, :]))
                dve.tensor_scalar(nt[:, 0, 0:1], mv[:, t, 1:2], LN_EPS, None, ALU.add).then_inc(ln_var, 1)
                rsqrt(rstd[:, t:t + 1], 1)

            def normalise(tile, t):
                dve.tensor_scalar(tile, tile, mv[:, t, 0:1], rstd[:, t:t + 1], ALU.subtract, ALU.mult).then_inc(ln_done, 1)

            def xT_lo_part(t, n):
                dve.wait_ge(xT_hi_done, n + 1)
                b = 2 * (n % 2)
                dve.tensor_tensor(xT_lo[:, :, cols(t)], bank[:, b:b + 2, :].rearrange("p b (k c) -> p (b k) c", c=P),
                                  xT_hi[:, :, cols(t)], ALU.subtract).then_inc(xT_lo_done, 1)

            for t in range(TILES):
                if t == TILES - 1:
                    dve.wait_ge(xT_pe, TILES - 3)
                    dve.memset(xin[96:P, t % 3, :], 0.0).then_inc(filled, 1)
                    dve.wait_ge(filled, 4)
                dve.wait_ge(xin_in[t % 3], 16 * (t // 3 + 1))
                tile = xin[:, t % 3, :]
                statistics(tile, t)
                normalise(tile, t)
                xT_lo_part(t, t)
            split_lo(dve, "W1", 0)
            dve.wait_ge(table_in, 16)
            for b in range(BLOCKS):
                first = dve.value_load(table_row[0:1, 3 * b:3 * b + 1], min_val=0, max_val=GROUPS - 1)
                count = dve.value_load(table_row[0:1, 3 * b + 1:3 * b + 2], min_val=1, max_val=GROUPS)
                past = dve.value_load(table_row[0:1, 3 * b + 2:3 * b + 3], min_val=0, max_val=GROUPS * BLOCKS)
                with dve.Fori(0, count) as i:
                    g = (first + i).with_bounds(min_val=0, max_val=GROUPS - 1)
                    dve.wait_ge(dst_ready, OH_SLOTS * (past + i) + 1)
                    dve.tensor_scalar(krel[:, :], keyT[:, bass.ds(g, 1), :].rearrange("p a s -> p (a s)"),
                                      key_offset[:, b:b + 1], None, ALU.add).then_inc(key_ready, 1)
                    for slot in range(OH_SLOTS):
                        dve.wait_ge(onehot_used, OH_SLOTS * (past + i) + slot + 1)
                        for s in range(POOL_SUBS, PART):
                            dve.tensor_scalar(onehot[:, slot, s, 0:P], iota[:, 0:P],
                                              modT[:, bass.ds(g, 1), PART * slot + s], None, ALU.is_equal)
                        dve.wait_ge(key_ready, past + i + 1)
                        for s in range(PART):
                            last = dve.tensor_scalar(onehot[:, slot, s, P:P + KEYS], iota[:, :],
                                                     krel[:, PART * slot + s:PART * slot + s + 1], None, ALU.is_equal)
                        last.then_inc(dst_ready, 1)
            dve.wait_ge(block_done, BLOCKS)
            dve.wait_ge(block_pe, BLOCKS)
            sums = [0]

            def a_chain(ins):
                sums[0] += 1
                ins.then_inc(a_step, 1)
                dve.wait_ge(a_step, sums[0])

            a_chain(dve.tensor_tensor(a_sum[:, :], a_u16[:, 0, :], a_u16[:, 1, :], ALU.add))
            for u in range(2, TILES - 1):
                a_chain(dve.tensor_tensor(a_sum[:, :], a_sum[:, :], a_u16[:, u, :], ALU.add))
            dve.tensor_tensor(a_sum[:, :], a_sum[:, :], a_u16[:, TILES - 1, :], ALU.add).then_inc(a_summed, 1)
            for t in range(TILES):
                dve.wait_ge(a_ready, t + 1)
                dve.tensor_tensor(a_f[:, t, cols(t)], a_f[:, t, cols(t)], ident[:, :], ALU.add).then_inc(a_diag, 1)
            dve.wait_ge(deg_pe, 1)
            dve.tensor_scalar(nt[:, 0, :], bank[:, 4, 0:TILES], 1.0, None, ALU.add).then_inc(ln_var, 1)
            rsqrt(dinv[:, :], TILES)
            dve.wait_ge(h_done, 2 * TILES)
            for t in range(TILES):
                dve.tensor_scalar(h[:, t, :], h[:, t, :], dinv[:, t:t + 1], None, ALU.mult).then_inc(h_scaled, 1)
            dve.wait_ge(a_summed, 1)
            dve.wait_ge(bias_in, 16)
            for t in range(TILES):
                tile = xres[:, t % 2, :]
                if t == TILES - 1:
                    dve.wait_ge(x1_out[t % 2], 16 * (t // 2))
                    dve.memset(xres[96:P, t % 2, :], 0.0).then_inc(filled, 1)
                    dve.wait_ge(filled, 5)
                dve.wait_ge(agg_pe, t + 1)
                b = 2 * (t % 2)
                dve.scalar_tensor_tensor(out=y[:, :], in0=bank[:, b:b + 2, :].rearrange("p b c -> p (b c)"),
                                         scalar=dinv[:, t:t + 1], in1=bias[:, :], op0=ALU.mult,
                                         op1=ALU.add).then_inc(agg_read, 1)
                dve.wait_ge(agg_read, t + 1)
                dve.wait_ge(xres_in[t % 2], 16 * (t // 2 + 1))
                dve.scalar_tensor_tensor(out=tile, in0=y[:, :], scalar=0.0, in1=tile, op0=ALU.max,
                                         op1=ALU.add).then_inc(x1_ready, 1)
                dve.wait_ge(x1_ready, t + 1)
                statistics(tile, t)
            split_lo(dve, "G", 0)
            for t in range(TILES):
                dve.wait_ge(x2_in[t % 3], 16 * (t // 3 + 1))
                normalise(x2in[:, t % 3, :], t)
                xT_lo_part(t, TILES + t)
            steps[id(gate_step)] = 0
            dve.wait_ge(gate_act, 2)
            flat = [P, TILES * HEADS, EXPERTS]
            of_max = gate[:, :, :].rearrange("p t h -> p (t h)").unsqueeze(2).broadcast_to(flat)
            ranks = rank[:, :].unsqueeze(1).broadcast_to(flat)
            top_v = top[:, :, :].rearrange("p t (h e) -> p (t h) e", e=EXPERTS)
            chain(dve.tensor_reduce(gate[:, :, :].rearrange("p t h -> p (t h)"), g_all[:, :, :], AX_X, ALU.max), gate_step)
            chain(dve.tensor_tensor(g_t[:, :, :], g_all[:, :, :], of_max, ALU.is_equal), gate_step)
            chain(dve.tensor_tensor(g_t[:, :, :], g_t[:, :, :], ranks, ALU.mult), gate_step)
            chain(dve.tensor_reduce(g_m[:, :], g_t[:, :, :], AX_X, ALU.max), gate_step)
            chain(dve.tensor_tensor(top_v, g_t[:, :, :], g_m[:, :].unsqueeze(2).broadcast_to(flat), ALU.is_equal), gate_step)
            split_lo(dve, "VA", 0)
            dve.wait_ge(topT_out, 16)

            def pick(g, t, stage, p):
                n = 10 * g + t
                wait_dense(dve, values_pe, stage, p, g, t)
                wait(dve, value_done, n - 1)
                hot = top[:, t, bass.ds(g * EXPERTS, EXPERTS)].unsqueeze(2).broadcast_to([P, EXPERTS, DH])
                mul = picked[:, t % 2, :].rearrange("p (e c) -> p e c", e=EXPERTS)
                dve.tensor_tensor(mul, bank[:, t % 2, :].rearrange("p (e c) -> p e c", e=EXPERTS), hot,
                                  ALU.mult).then_inc(picked_done, 1)
                dve.wait_ge(picked_done, n + 1)
                wait(dve, v_step, 3 * g)
                dve.tensor_reduce(v_raw[:, t, :], mul.rearrange("p e c -> p c e"), AX_X, ALU.add).then_inc(value_done, 1)

            def finish_values(g, s):
                dve.wait_ge(value_done, 10 * g + 10)
                if s == 0:
                    wait(dve, pv_pe, 15 * g)
                mine = slice(s * DH, (s + 1) * DH)
                gates = gate[:, :, bass.ds(g, 1)].broadcast_to([P, TILES, DH])
                dve.tensor_tensor(v_raw[:, :, :], v_raw[:, :, :], gates, ALU.mult).then_inc(v_step, 1)
                dve.wait_ge(v_step, 3 * g + 1)
                dve.tensor_copy(v_hi[:, :, mine], v_raw[:, :, :]).then_inc(v_step, 1)
                dve.wait_ge(v_step, 3 * g + 2)
                dve.tensor_tensor(v_lo[:, :, mine], v_raw[:, :, :], v_hi[:, :, mine], ALU.subtract).then_inc(v_step, 1)

            def row_max(g, i, w):
                n = 10 * g + i
                dve.wait_ge(sim_pe, n + 1)
                wait(dve, norm_done, n - 1)
                dve.tensor_reduce(rowstat[:, 2, i % 2:i % 2 + 1],
                                  bank[:, 2:5, :].rearrange("p b c -> p (b c)")[:, 0:w], AX_X, ALU.max).then_inc(max_done, 1)
                dve.wait_ge(max_done, n + 1)
                wait(dve, exp_done, n - 1)
                dve.tensor_scalar(rowstat[:, 0, i % 2:i % 2 + 1], rowstat[:, 2, i % 2:i % 2 + 1], -SCALE, None,
                                  ALU.mult).then_inc(neg_done, 1)

            def row_norm(g, i, w):
                n = 10 * g + i
                one = slice(i % 2, i % 2 + 1)
                dve.wait_ge(exp_done, n + 1)
                dve.wait_ge(neg_done, n + 1)
                dve.reciprocal(rowstat[:, 2, one], rowstat[:, 1, one]).then_inc(inv_done, 1)
                dve.wait_ge(inv_done, n + 1)
                wait(dve, prob_done, n - 1)
                dve.tensor_tensor(rowstat[:, 3, one], rowstat[:, 2, one], gate[:, i, bass.ds(g, 1)],
                                  ALU.mult).then_inc(norm_done, 1)
                dve.wait_ge(norm_done, n + 1)
                dve.tensor_scalar(prob[:, i % 2, 0:w], prob[:, i % 2, 0:w], rowstat[:, 3, one], None,
                                  ALU.mult).then_inc(prob_done, 1)

            def pT_lo_parts(g, s, q):
                for j in range(q + 1):
                    n = 15 * g + q * (q + 1) // 2 + j
                    b = (15 * s + q * (q + 1) // 2 + j) % 2
                    dve.wait_ge(pT_hi_done, n + 1)
                    dve.tensor_tensor(pT_lo[:, b, :], bank[:, 5 + b, :], pT_hi[:, b, :], ALU.subtract).then_inc(pT_lo_done, 1)

            def values_and_attention(gv, sv, p, ga, sa):
                stage = ("VA", "VB")[sv]
                for t in range(TILES):
                    if ga is not None:
                        w = (t // 2 + 1) * 2 * P
                        row_max(ga, t, w)
                        if t >= 1:
                            pick(gv, t - 1, stage, p)
                        row_norm(ga, t, w)
                        if t % 2:
                            pT_lo_parts(ga, sa, t // 2)
                    elif t >= 1:
                        pick(gv, t - 1, stage, p)
                pick(gv, TILES - 1, stage, p)
                finish_values(gv, sv)

            def qk_lo_parts(p):
                for m in range(2):
                    for s in range(2):
                        part = slice(s * DH, (s + 1) * DH)
                        dve.wait_ge(qk_hi, 4 * p + 2 * m + s + 1)
                        if m == 0:
                            dve.wait_ge(m_used, 40 * p + 40)
                        hi, lo = ((q_st[s], q_lo), (kh_st[s], kl_st[s]))[m]
                        b = 2 + 3 * m
                        dve.tensor_tensor(lo[part, :], bank[part, b:b + 3, :].rearrange("p b c -> p (b c)")[:, 0:NP],
                                          hi[part, :], ALU.subtract).then_inc(qk_lo, 1)

            def moe_half(p, half):
                def make(m):
                    for u in range(2):
                        n = 2 * m + u
                        G = 40 * p + n
                        if u == 0:
                            dve.wait_ge(mask_in[m % 2], 32 * ((p - 1) * 10 + m // 2 + 1))
                            dve.wait_ge(o_done, 10 * p)
                        dve.wait_ge(m_hi_done, G)
                        dve.wait_ge(m_lo_done, G)
                        t = m % TILES
                        dve.tensor_tensor(masked[:, :, :], oT[:, cols(t)].unsqueeze(1).broadcast_to([P, 4, P]),
                                          mask[:, t % 2, 4 * u:4 * u + 4, :], ALU.mult).then_inc(masked_done, 1)
                        dve.wait_ge(m_hi_done, G + 1)
                        dve.tensor_tensor(m_lo[:, n % 4, :, :], masked[:, :, :], m_hi[:, n % 4, :, :],
                                          ALU.subtract).then_inc(m_lo_done, 1)

                def add(m):
                    t = m % TILES
                    M = 20 * p + m
                    rows = LAST if t == TILES - 1 else P
                    dve.wait_ge(m_used, 2 * M + 2)
                    dve.wait_ge(acc_in[t % 2], 16 * ((p - 1) * 10 + m // 2 + 1))
                    dve.tensor_tensor(acc[0:rows, t % 2, :], acc[0:rows, t % 2, :], bank[0:rows, t % 2, :],
                                      ALU.add).then_inc(acc_done, 1)

                for t in range(TILES):
                    m = half * TILES + t
                    make(m)
                    if t >= 1:
                        add(m - 1)
                add(half * TILES + TILES - 1)

            values_and_attention(0, 0, 0, None, None)
            split_lo(dve, "QK", 0)
            qk_lo_parts(0)
            split_lo(dve, "VB", 0)
            values_and_attention(1, 1, 0, 0, 0)
            with dve.Fori(1, PAIRS) as p:
                split_lo(dve, "VA", p)
                values_and_attention(2 * p, 0, p, 2 * p - 1, 1)
                split_lo(dve, "O0", p)
                moe_half(p, 0)
                split_lo(dve, "O1", p)
                moe_half(p, 1)
                split_lo(dve, "QK", p)
                qk_lo_parts(p)
                split_lo(dve, "VB", p)
                values_and_attention(2 * p + 1, 1, p, 2 * p, 0)
            for i in range(TILES):
                w = (i // 2 + 1) * 2 * P
                row_max(2 * PAIRS - 1, i, w)
                row_norm(2 * PAIRS - 1, i, w)
                if i % 2:
                    pT_lo_parts(2 * PAIRS - 1, 1, i // 2)
            split_lo(dve, "O0", PAIRS)
            moe_half(PAIRS, 0)
            split_lo(dve, "O1", PAIRS)
            moe_half(PAIRS, 1)


_INS = ["x", "src", "dst", "L0_gnn_W", "L0_gnn_b", "L0_ffn_w_q", "L0_ffn_w_k", "L0_ffn_w_gate",
        "L0_ffn_value_experts", "L0_ffn_output_experts"]


def kernel(**inputs):
    import numpy as _np
    import concourse.bacc as _bacc
    from concourse import mybir as _mybir
    from concourse.bass_utils import run_bass_kernel_spmd as _run

    nc = _bacc.Bacc("TRN2", target_bir_lowering=False, num_devices=1)
    arrays, args = {}, []
    for name in _INS:
        a = _np.ascontiguousarray(inputs[name])
        arrays[f"in_{name}_dram"] = a
        args.append(nc.dram_tensor(f"in_{name}_dram", a.shape, _mybir.dt.from_np(a.dtype), kind="ExternalInput").ap())
    out = nc.dram_tensor("out_0_dram", (N, D), F32, kind="ExternalOutput").ap()
    build(nc, *args, out)
    r = _run(nc, [arrays], core_ids=[0])
    return r.results[0]["out_0_dram"]
```

```python
from contextlib import ExitStack

import concourse.bass as bass
from concourse import mybir

F32 = mybir.dt.float32
F32R = mybir.dt.float32r
BF16 = mybir.dt.bfloat16
FP16 = mybir.dt.float16
I32 = mybir.dt.int32
U16 = mybir.dt.uint16
ALU = mybir.AluOpType
ACT = mybir.ActivationFunctionType
AX_X = mybir.AxisListType.X

P = 128
N = 1250
D = 1024
E = 40000
HEADS, DH, EXPERTS = 8, 64, 8
PAIRS = HEADS // 2
TILES = -(-N // P)
NP = TILES * P
QUADS = TILES // 2
LAST = N - (TILES - 1) * P
KT = D // P
HALF = 512
SCALE = DH ** -0.5
LN_EPS = 1e-5
NEG = -3.0e38

GROUP = 512
SUB = GROUP // P
GROUPS = -(-E // GROUP)
FULL_GROUPS = E // GROUP
REST = E - FULL_GROUPS * GROUP
BLOCK = 32
BLOCKS = NP // BLOCK
KEYS = BLOCK * TILES
BLOCK_KEY = 1024
OH_SLOTS = 2
PART = SUB // OH_SLOTS
POOL_SUBS = 1

M_SLOTS = 3
RING, RAW = 10, 4

SLOTS = {
    "W0": [0, 1, 2, 3, 4, 5, 6, 7],
    "W1": [8, 9, 0, 1, 2, 3, 4, 5],
    "G": [6],
    "VA": [4, 5, 0, 1, 2, 3, 6, 7],
    "QK": [8, 9, 4, 5],
    "O0": [0, 1, 2, 3, 6, 7, 8, 9],
    "O1": [4, 5, 0, 1, 2, 3, 6, 7],
    "VB": [8, 9, 0, 1, 2, 3, 6, 7],
}
FIRST = [("W0", 0), ("W1", 0), ("G", 0), ("VA", 0), ("QK", 0), ("VB", 0)]
EACH = ["VA", "QK", "O0", "O1", "VB"]


def plan_chunks():
    stages = FIRST + [(s, p) for p in range(1, PAIRS) for s in EACH] + [("O0", PAIRS), ("O1", PAIRS)]
    first, before, held, n = {}, {}, {}, 0
    for stage in stages:
        first[stage] = n
        for k, slot in enumerate(SLOTS[stage[0]]):
            before[stage, k] = held.get(slot, -1)
            held[slot] = n
            n += 1
    return first, before


CHUNK_FIRST, CHUNK_BEFORE = plan_chunks()
PER_PAIR = sum(len(SLOTS[s]) for s in EACH)


def chunk_number(stage, p, k):
    if isinstance(p, int):
        return CHUNK_FIRST[stage, p] + k
    return (CHUNK_FIRST[stage, 1] - PER_PAIR + k) + p * PER_PAIR


def chunk_raw(stage, p, k):
    if isinstance(p, int):
        n = CHUNK_FIRST[stage, p] + k
        return n % RAW, n // RAW + 1
    n = CHUNK_FIRST[stage, 1] + k
    return n % RAW, p * (PER_PAIR // RAW) + (n // RAW + 1 - PER_PAIR // RAW)


def chunk_before(stage, p, k):
    if isinstance(p, int):
        return CHUNK_BEFORE[(stage, p), k] + 1
    gap = CHUNK_FIRST[stage, 1] + k - CHUNK_BEFORE[(stage, 1), k]
    gap = min(CHUNK_FIRST[stage, q] + k - CHUNK_BEFORE[(stage, q), k] for q in range(1, PAIRS))
    return chunk_number(stage, p, k) - gap + 1


assert PER_PAIR % RAW == 0


def wait(engine, semaphore, value):
    if not isinstance(value, int) or value > 0:
        engine.wait_ge(semaphore, value)


def build(nc, x, src, dst, gnn_w, gnn_b, w_q, w_k, w_gate, value_experts, output_experts, out):
    with ExitStack() as ctx:
        def sem(name):
            return ctx.enter_context(nc.semaphore(name))

        base = (nc.sbuf_base + 63) // 64 * 64
        limit = nc.sbuf_usable_end

        def at(name, offset, shape, dtype):
            size = mybir.dt.size(dtype)
            for s in shape[1:]:
                size *= s
            assert base + offset + size <= limit, (name, base + offset + size, limit)
            return nc.alloc_sbuf_tensor_at(name, shape, dtype, offset=base + offset)

        class Region:
            def __init__(self, start):
                self.next = start

            def put(self, name, shape, dtype):
                t = at(name, self.next, shape, dtype)
                size = mybir.dt.size(dtype)
                for s in shape[1:]:
                    size *= s
                self.next += -(-size // 32) * 32
                return t

        r = Region(0)
        wide_at = 0
        xT_hi = r.put("xT_hi", [P, KT, NP], F32R)
        xT_lo = r.put("xT_lo", [P, KT, NP], F32R)
        ring_hi = r.put("ring_hi", [P, RING, HALF], F32R)
        ring_lo = r.put("ring_lo", [P, RING, HALF], F32R)
        raw = r.put("raw", [P, RAW, HALF], F32)
        ident = r.put("ident", [P, P], F32)
        ident_b = r.put("ident_b", [P, P], BF16)
        causal = r.put("causal", [P, 2, 2 * P], BF16)
        rank = r.put("rank", [P, EXPERTS], F32)
        ones = r.put("ones", [P, BLOCKS], F32)
        mv = r.put("mv", [P, TILES, 2], F32)
        rstd = r.put("rstd", [P, TILES], F32)
        nt = r.put("nt", [P, 4, TILES], F32)
        stats = r.put("stats", [P, 2, 6], F32)
        dinv = r.put("dinv", [P, TILES], F32)
        rowstat = r.put("rowstat", [P, 4, 2], F32)
        scratch = r.put("scratch", [P, 8], F32)
        z = r.next

        a_f = at("a_f", wide_at, [P, TILES, NP], F32)
        r = Region(z)
        h_at = z
        h = r.put("h", [P, TILES, D], F32)
        a_at = r.next
        a_u16 = r.put("a_u16", [P, TILES, NP], U16)
        oh_at = r.next
        onehot = r.put("onehot", [P, OH_SLOTS, PART, P + KEYS], BF16)
        iota = r.put("iota", [P, KEYS], FP16)
        keyT = r.put("keyT", [P, GROUPS, SUB], F32)
        modT = r.put("modT", [P, GROUPS, SUB], F32)
        krel = r.put("krel", [P, SUB], F32)
        srel = r.put("srel", [P, SUB], F32)
        zeros_b = r.put("zeros_b", [P, KEYS], BF16)
        key_offset = r.put("key_offset", [P, BLOCKS], F32)
        table_row = r.put("table_row", [1, BLOCKS * 3], I32)
        r = Region(h_at)
        e_dst = r.put("e_dst", [GROUPS, GROUP], I32)
        e_dst_hi = r.put("e_dst_hi", [GROUPS, GROUP], I32)
        e_src = r.put("e_src", [GROUPS, GROUP], I32)
        e_t0 = r.put("e_t0", [GROUPS, GROUP], I32)
        e_t1 = r.put("e_t1", [GROUPS, GROUP], I32)
        f_dst = r.put("f_dst", [GROUPS, GROUP], F32)
        f_dst_hi = r.put("f_dst_hi", [GROUPS, GROUP], F32)
        f_src = r.put("f_src", [GROUPS, GROUP], F32)
        f_key = r.put("f_key", [GROUPS, GROUP], F32)
        f_hi = r.put("f_hi", [GROUPS, GROUP], F32)
        minmax = r.put("minmax", [GROUPS, 2], F32)
        diag = r.put("diag", [GROUPS, 2 * GROUPS], F32)
        block_lo = r.put("block_lo", [P, 1], F32)
        group_no = r.put("group_no", [P, GROUPS], F32)
        before_tri = r.put("before_tri", [P, BLOCKS], F32)
        over = r.put("over", [BLOCKS, GROUPS], F32)
        over_t = r.put("over_t", [BLOCKS, 2, GROUPS], F32)
        table_f = r.put("table_f", [BLOCKS, 3], F32)
        table_i = r.put("table_i", [BLOCKS, 3], I32)
        iota_f = r.put("iota_f", [P, KEYS], F32)
        assert r.next <= a_at
        r = Region(a_at)
        xin = r.put("xin", [P, 3, D], F32)
        r = Region(a_at)
        xres = r.put("xres", [P, 2, D], F32)
        y = r.put("y", [P, D], F32)
        bias = r.put("bias", [P, D], F32)
        assert r.next <= oh_at
        r = Region(oh_at)
        a_sum = r.put("a_sum", [P, NP], F32)

        r = Region(z)
        q_st = [r.put(f"q_st{s}", [P, NP], F32R) for s in range(2)]
        kh_st = [r.put(f"kh_st{s}", [P, NP], F32R) for s in range(2)]
        kl_st = [r.put(f"kl_st{s}", [P, NP], F32R) for s in range(2)]
        v_hi = r.put("v_hi", [P, TILES, P], F32R)
        v_lo = r.put("v_lo", [P, TILES, P], F32R)
        v_raw = r.put("v_raw", [P, TILES, DH], F32)
        oT_hi = r.put("oT_hi", [P, NP], F32R)
        oT_lo = r.put("oT_lo", [P, NP], F32R)
        top = r.put("top", [P, TILES, HEADS * EXPERTS], F32)
        gate = r.put("gate", [P, TILES, HEADS], F32)
        shared_at = r.next
        picked = r.put("picked", [P, 2, HALF], F32)
        prob = r.put("prob", [P, 2, NP], F32)
        pT_hi = r.put("pT_hi", [P, 2, HALF], F32R)
        pT_lo = r.put("pT_lo", [P, 2, HALF], F32R)
        r = Region(shared_at)
        m_hi = r.put("m_hi", [P, M_SLOTS, 4, P], F32R)
        m_lo = r.put("m_lo", [P, M_SLOTS, 4, P], F32R)
        mask = r.put("mask", [P, 2, EXPERTS, P], BF16)
        q_lo_at = r.next
        acc = r.put("acc", [P, 2, HALF], F32)
        r = Region(q_lo_at)
        q_lo = r.put("q_lo", [P, NP], F32R)
        r = Region(z)
        x2in = r.put("x2in", [P, 3, D], F32)
        logitT = r.put("logitT", [HEADS * EXPERTS, NP], F32)
        g_all = r.put("g_all", [P, TILES * HEADS, EXPERTS], F32)
        g_t = r.put("g_t", [P, TILES * HEADS, EXPERTS], F32)
        g_m = r.put("g_m", [P, TILES * HEADS], F32)
        topT = r.put("topT", [HEADS * EXPERTS, NP], BF16)

        bank = ctx.enter_context(nc.psum_tensor("bank", [P, 8, HALF], F32))

        table_dram = nc.dram_tensor("table_dram", [BLOCKS * 3], I32).ap()
        x1_dram = nc.dram_tensor("x1_dram", [NP, D], F32).ap()
        topT_dram = nc.dram_tensor("topT_dram", [HEADS * EXPERTS, NP], BF16).ap()

        consts = sem("consts")
        filled = sem("filled")
        edges_in = sem("edges_in")
        table_step = sem("table_step")
        table_ready = sem("table_ready")
        table_pe = sem("table_pe")
        table_done = sem("table_done")
        table_out = sem("table_out")
        table_in = sem("table_in")
        raw_in = [sem(f"raw_in{i}") for i in range(RAW)]
        chunk_hi = sem("chunk_hi")
        chunk_lo = sem("chunk_lo")
        chunk_used = sem("chunk_used")
        xin_in = [sem(f"xin_in{i}") for i in range(3)]
        ln_step = sem("ln_step")
        ln_var = sem("ln_var")
        ln_sqrt = sem("ln_sqrt")
        ln_done = sem("ln_done")
        xT_pe = sem("xT_pe")
        xT_hi_done = sem("xT_hi_done")
        xT_lo_done = sem("xT_lo_done")
        h_pe = sem("h_pe")
        h_done = sem("h_done")
        key_ready = sem("key_ready")
        dst_ready = sem("dst_ready")
        held = sem("held")
        srel_ready = sem("srel_ready")
        src_ready = sem("src_ready")
        onehot_used = sem("onehot_used")
        block_pe = sem("block_pe")
        block_done = sem("block_done")
        a_ready = sem("a_ready")
        a_diag = sem("a_diag")
        a_step = sem("a_step")
        a_summed = sem("a_summed")
        deg_pe = sem("deg_pe")
        h_scaled = sem("h_scaled")
        agg_pe = sem("agg_pe")
        agg_read = sem("agg_read")
        xres_in = [sem(f"xres_in{i}") for i in range(2)]
        bias_in = sem("bias_in")
        x1_ready = sem("x1_ready")
        x1_out = [sem(f"x1_out{i}") for i in range(2)]
        x2_in = [sem(f"x2_in{i}") for i in range(3)]
        gate_pe = sem("gate_pe")
        gate_act = sem("gate_act")
        gate_step = sem("gate_step")
        topT_out = sem("topT_out")

        values_pe = sem("values_pe")
        picked_done = sem("picked_done")
        value_done = sem("value_done")
        v_step = sem("v_step")
        qk_hi = sem("qk_hi")
        qk_lo = sem("qk_lo")
        q_in = sem("q_in")
        k_in = sem("k_in")
        sim_pe = sem("sim_pe")
        max_done = sem("max_done")
        neg_done = sem("neg_done")
        exp_done = sem("exp_done")
        inv_done = sem("inv_done")
        norm_done = sem("norm_done")
        prob_done = sem("prob_done")
        pT_pe = sem("pT_pe")
        pT_hi_done = sem("pT_hi_done")
        pT_lo_done = sem("pT_lo_done")
        pv_pe = sem("pv_pe")
        o_hi = sem("o_hi")
        o_done = sem("o_done")
        mask_in = [sem(f"mask_in{i}") for i in range(2)]
        m_hi_done = sem("m_hi_done")
        m_lo_done = sem("m_lo_done")
        m_used = sem("m_used")
        acc_in = [sem(f"acc_in{i}") for i in range(2)]
        acc_done = sem("acc_done")

        block = ctx.enter_context(nc.Block())

        def cols(t, width=P):
            return slice(t * width, (t + 1) * width)

        def load_chunks(eng, stage, p, begin=0, end=KT):
            for k in range(begin, min(end, len(SLOTS[stage]))):
                slot, times = chunk_raw(stage, p, k)
                wait(eng, chunk_lo, chunk_number(stage, p, k) - RAW + 1)
                to = raw[:, slot, :]
                if stage in ("W0", "W1"):
                    n = int(stage[1])
                    of = gnn_w[cols(k), cols(n, HALF)]
                elif stage == "G":
                    to = to.rearrange("p (k c) -> p k c", k=KT)
                    of = w_gate.rearrange("(k p) c -> p k c", p=P)
                elif stage in ("VA", "VB"):
                    head = 2 * p + (stage == "VB")
                    to = to.rearrange("p (e c) -> p e c", e=EXPERTS)
                    of = value_experts[:, bass.ds(head, 1), cols(k), :].rearrange("e h d c -> d (e h) c")
                elif stage in ("O0", "O1"):
                    pair = p - 1
                    of = output_experts[k, bass.ds(2 * pair, 2), :, cols(int(stage[1]), HALF)].rearrange("h c n -> (h c) n")
                else:
                    w = (w_q, w_k)[k // 2]
                    to = to.rearrange("p (k c) -> p k c", k=4)
                    of = w.rearrange("(k p) c -> p k c", p=P)[:, 4 * (k % 2):4 * (k % 2) + 4, bass.ds(P * p, P)]
                eng.dma_start(to, of).then_inc(raw_in[slot], 16)

        def wait_dense(eng, done, stage, p, n, t):
            if t < TILES - 1:
                eng.wait_ge(done, (TILES - 1) * n + t + 1)
            else:
                eng.wait_ge(chunk_used, chunk_number(stage, p, KT - 1) + 1)

        def split_hi(act, stage, p, begin=0, end=KT):
            for k, place in list(enumerate(SLOTS[stage]))[begin:end]:
                slot, times = chunk_raw(stage, p, k)
                wait(act, raw_in[slot], times * 16)
                wait(act, chunk_used, chunk_before(stage, p, k))
                act.activation(ring_hi[:, place, :], raw[:, slot, :], ACT.Copy).then_inc(chunk_hi, 1)

        def split_lo(dve, stage, p, begin=0, end=KT):
            for k, place in list(enumerate(SLOTS[stage]))[begin:end]:
                slot, times = chunk_raw(stage, p, k)
                wait(dve, chunk_hi, chunk_number(stage, p, k) + 1)
                dve.tensor_tensor(ring_lo[:, place, :], raw[:, slot, :], ring_hi[:, place, :],
                                  ALU.subtract).then_inc(chunk_lo, 1)

        def due(g, s, i):
            if i % 2 == 0 and i >= 2:
                return g, s, i // 2 - 1
            if i == 0 and s == 1:
                return g - 1, 0, QUADS - 1
            return None

        def three(pe, acc_ap, w_hi, w_lo, m_hi_ap, m_lo_ap, start, stop):
            return [pe.matmul(acc_ap, w_hi, m_hi_ap, start=start, stop=False),
                    pe.matmul(acc_ap, w_hi, m_lo_ap, start=False, stop=False),
                    pe.matmul(acc_ap, w_lo, m_hi_ap, start=False, stop=stop)]

        @block.sync
        def _(sp):
            sp.wait_ge(filled, 3)
            for to, of in ((e_dst, dst), (e_dst_hi, dst), (e_src, src)):
                sp.dma_start(to[0:FULL_GROUPS, :], of[0:FULL_GROUPS * GROUP].rearrange("(g q) -> g q", q=GROUP)).then_inc(edges_in, 16)
                sp.dma_start(to[FULL_GROUPS:GROUPS, 0:REST], of[FULL_GROUPS * GROUP:E].rearrange("(g q) -> g q", g=1)).then_inc(edges_in, 16)

            def load_x(t):
                if t >= 3:
                    sp.wait_ge(xT_pe, t - 2)
                if t < TILES - 1:
                    sp.dma_start(xin[:, t % 3, :], x[cols(t), :]).then_inc(xin_in[t % 3], 16)
                else:
                    sp.wait_ge(filled, 4)
                    sp.dma_start(xin[0:LAST, t % 3, :], x[t * P:N, :]).then_inc(xin_in[t % 3], 16)

            for t in range(3):
                load_x(t)
            load_chunks(sp, "W0", 0)
            sp.wait_ge(table_done, 1)
            sp.dma_start(table_dram.rearrange("(b c) -> b c", c=3), table_i[:, :]).then_inc(table_out, 16)
            sp.wait_ge(table_out, 16)
            sp.dma_start(table_row[:, :], table_dram.rearrange("(a n) -> a n", a=1)).then_inc(table_in, 16)
            for t in range(3, TILES):
                load_x(t)
            load_chunks(sp, "W1", 0)
            load_chunks(sp, "G", 0)
            sp.wait_ge(a_summed, 1)
            sp.wait_ge(a_ready, TILES)
            sp.dma_start(bias[:, :], gnn_b.rearrange("(a n) -> a n", a=1).broadcast_to([P, D])).then_inc(bias_in, 16)

            def store_x1(t):
                sp.wait_ge(x1_ready, t + 1)
                sp.dma_start(x1_dram[cols(t), :], xres[:, t % 2, :]).then_inc(x1_out[t % 2], 16)

            for t in range(TILES):
                if t >= 2:
                    store_x1(t - 2)
                    sp.wait_ge(x1_out[t % 2], 16 * (t // 2))
                    sp.wait_ge(ln_var, TILES + t)
                if t < TILES - 1:
                    sp.dma_start(xres[:, t % 2, :], x[cols(t), :]).then_inc(xres_in[t % 2], 16)
                else:
                    sp.wait_ge(filled, 5)
                    sp.dma_start(xres[0:LAST, t % 2, :], x[t * P:N, :]).then_inc(xres_in[t % 2], 16)
            store_x1(TILES - 2)
            store_x1(TILES - 1)
            for i in range(2):
                sp.wait_ge(x1_out[i], 16 * TILES // 2)
            sp.wait_ge(agg_pe, TILES)
            for t in range(TILES):
                if t >= 3:
                    sp.wait_ge(xT_pe, TILES + t - 2)
                sp.dma_start(x2in[:, t % 3, :], x1_dram[cols(t), :]).then_inc(x2_in[t % 3], 16)

            def sums_in(p, m):
                t, n = m % TILES, m // TILES
                if m == 0:
                    sp.wait_ge(pv_pe, (2 * p) * 15)
                if m == 0 and not isinstance(p, int):
                    sp.wait_ge(q_in, 32 * p + 32)
                sp.wait_ge(x1_out[t % 2], (5 + (p - 1) * 10 + m // 2) * 16)
                rows = LAST if t == TILES - 1 else P
                sp.dma_start(acc[0:rows, t % 2, :], x1_dram[t * P:t * P + rows, cols(n, HALF)]).then_inc(acc_in[t % 2], 16)

            def sums_out(p, m, to):
                t, n = m % TILES, m // TILES
                rows = LAST if t == TILES - 1 else P
                sp.wait_ge(acc_done, 20 * p + m + 1)
                sp.dma_start(to[t * P:t * P + rows, cols(n, HALF)], acc[0:rows, t % 2, :]).then_inc(x1_out[t % 2], 16)

            def moe(p, to):
                last = isinstance(p, int)
                load_chunks(sp, "O0", p)
                load_chunks(sp, "O1", p, 0, RAW)
                sums_in(p, 0)
                for m in range(2 * TILES):
                    if m + 1 < 2 * TILES:
                        sums_in(p, m + 1)
                    if m == TILES - 1:
                        load_chunks(sp, "O1", p, RAW)
                    if not last and m == TILES:
                        load_chunks(sp, "VB", p, 0, RAW)
                    if not last and m == 2 * TILES - 1:
                        load_chunks(sp, "VB", p, RAW)
                    sums_out(p, m, to)

            load_chunks(sp, "VA", 0)
            load_chunks(sp, "QK", 0)
            load_chunks(sp, "VB", 0)
            sp.wait_ge(topT_out, 16)
            with sp.Fori(1, PAIRS) as p:
                load_chunks(sp, "VA", p)
                load_chunks(sp, "QK", p)
                moe(p, x1_dram)
            moe(PAIRS, out)
            for i in range(2):
                sp.wait_ge(x1_out[i], (5 + PAIRS * 10) * 16)

        @block.gpsimd
        def _(pool):
            exact = dict(channel_multiplier=0, base=0, allow_small_or_imprecise_dtypes=True)
            pool.iota(iota_f[:, :], [[1, KEYS]], **exact).then_inc(consts, 1)
            pool.iota(group_no[:, :], [[1, GROUPS]], **exact).then_inc(consts, 1)
            pool.iota(key_offset[:, :], [[-BLOCK_KEY, BLOCKS]], **exact).then_inc(consts, 1)
            pool.iota(block_lo[:, :], [[0, 1]], base=0, channel_multiplier=BLOCK,
                      allow_small_or_imprecise_dtypes=True).then_inc(consts, 1)
            pool.iota(rank[:, :], [[-1, EXPERTS]], base=EXPERTS, channel_multiplier=0,
                      allow_small_or_imprecise_dtypes=True).then_inc(consts, 1)
            pool.memset(ident[:, :], 0.0).then_inc(consts, 1)
            pool.memset(ident_b[:, :], 0.0).then_inc(consts, 1)
            pool.memset(causal[:, :, :], 0.0).then_inc(consts, 1)
            pool.memset(before_tri[:, :], 1.0).then_inc(consts, 1)
            pool.wait_ge(consts, 9)
            for m in (ident, ident_b):
                pool.affine_select(out=m[:, :], in_=m[:, :], compare_op=ALU.not_equal, fill=1.0, base=0,
                                   pattern=[[-1, P]], channel_multiplier=1).then_inc(consts, 1)
            for i in range(2):
                pool.affine_select(out=causal[:, i, :], in_=causal[:, i, :], compare_op=ALU.is_ge, fill=NEG,
                                   base=P * i, pattern=[[-1, 2 * P]], channel_multiplier=1).then_inc(consts, 1)
            pool.affine_select(out=before_tri[:, :], in_=before_tri[:, :], compare_op=ALU.is_gt, fill=0.0, base=0,
                               pattern=[[1, BLOCKS]], channel_multiplier=-1).then_inc(consts, 1)

            def hold(i):
                return pool.tensor_tensor(scratch[:, i:i + 1], ident[:, 0:1], ident[:, 0:1], ALU.add)

            pool.wait_ge(consts, 14)
            for i, (semaphore, start) in enumerate((
                    (m_hi_done, 40), (m_lo_done, 40), (m_used, 40),
                    (acc_done, 20))):
                pool.memset(scratch[:, 3 + i:4 + i], 0.0).then_inc(semaphore, start)

            pool.wait_ge(table_in, 16)
            for b in range(BLOCKS):
                first = pool.value_load(table_row[0:1, 3 * b:3 * b + 1], min_val=0, max_val=GROUPS - 1)
                count = pool.value_load(table_row[0:1, 3 * b + 1:3 * b + 2], min_val=1, max_val=GROUPS)
                past = pool.value_load(table_row[0:1, 3 * b + 2:3 * b + 3], min_val=0, max_val=GROUPS * BLOCKS)
                with pool.Fori(0, count) as i:
                    g = (first + i).with_bounds(min_val=0, max_val=GROUPS - 1)
                    pool.wait_ge(src_ready, OH_SLOTS * (past + i) + 1)
                    pool.tensor_copy(srel[:, :], modT[:, bass.ds(g, 1), :].rearrange("p a s -> p (a s)")).then_inc(srel_ready, 1)
                    for slot in range(OH_SLOTS):
                        pool.wait_ge(srel_ready, past + i + 1)
                        pool.wait_ge(onehot_used, OH_SLOTS * (past + i) + slot + 1)
                        hold(slot)
                        for s in range(POOL_SUBS):
                            last = pool.tensor_scalar(onehot[:, slot, s, 0:P], iota[:, 0:P],
                                                      srel[:, PART * slot + s:PART * slot + s + 1], None, ALU.is_equal)
                        last.then_inc(src_ready, 1)

            def stack_halves(p):
                low, high = slice(0, DH), slice(DH, P)
                for m, copies in enumerate((
                    ((q_st[0][high, :], q_lo[low, :]), (q_st[1][low, :], q_lo[high, :])),
                    ((kh_st[0][high, :], kh_st[0][low, :]), (kl_st[0][high, :], kl_st[0][low, :]),
                     (kh_st[1][low, :], kh_st[1][high, :]), (kl_st[1][low, :], kl_st[1][high, :])))):
                    pool.wait_ge(qk_lo, 4 * p + 2 * m + 2)
                    if not isinstance(p, int):
                        pool.wait_ge(held, 2 * p + m)
                    elif m == 1:
                        pool.wait_ge(held, 1)
                    hold(OH_SLOTS).then_inc(held, 1)
                    for to, of in copies:
                        pool.dma_start(to, of).then_inc((q_in, k_in)[m], 16)

            stack_halves(0)
            with pool.Fori(1, PAIRS) as p:
                stack_halves(p)

        @block.scalar
        def _(act):
            def sqrt_of(w, n):
                act.wait_ge(ln_var, n)
                act.activation(nt[:, 1, 0:w], nt[:, 0, 0:w], ACT.Sqrt).then_inc(ln_sqrt, 1)

            def xT_hi_part(t, n):
                act.wait_ge(xT_pe, n + 1)
                b = 2 * (n % 2)
                act.activation(xT_hi[:, :, cols(t)], bank[:, b:b + 2, :].rearrange("p b (k c) -> p (b k) c", c=P),
                               ACT.Copy).then_inc(xT_hi_done, 1)

            def h_part(n, t):
                u = n * TILES + t
                wait_dense(act, h_pe, f"W{n}", 0, n, t)
                act.activation(h[:, t, cols(n, HALF)], bank[:, 4 + u % 2, :], ACT.Copy).then_inc(h_done, 1)

            split_hi(act, "W0", 0)
            act.wait_ge(table_done, 1)
            act.wait_ge(table_out, 16)
            for t in range(TILES):
                sqrt_of(1, t + 1)
                xT_hi_part(t, t)
                if t >= 1:
                    h_part(0, t - 1)
            h_part(0, TILES - 1)
            split_hi(act, "W1", 0)
            for t in range(TILES):
                h_part(1, t)
                for b in range(t * BLOCKS // TILES, (t + 1) * BLOCKS // TILES):
                    act.wait_ge(block_pe, b + 1)
                    act.activation(a_u16[:, :, cols(b, BLOCK)],
                                   bank[:, 6 + b % 2, 0:KEYS].rearrange("p (d s) -> p s d", s=TILES),
                                   ACT.Copy).then_inc(block_done, 1)
            act.wait_ge(block_done, BLOCKS)
            for t in range(TILES):
                act.activation(a_f[:, t, :], a_u16[:, t, :], ACT.Copy).then_inc(a_ready, 1)
            sqrt_of(TILES, TILES + 1)
            for t in range(TILES):
                sqrt_of(1, TILES + 2 + t)
            split_hi(act, "G", 0)
            for t in range(TILES):
                xT_hi_part(t, TILES + t)
            act.wait_ge(gate_pe, 1)
            act.activation(logitT[:, :], bank[0:HEADS * EXPERTS, 2:5, :].rearrange("p b c -> p (b c)")[:, 0:NP],
                           ACT.Copy).then_inc(gate_act, 1)
            act.wait_ge(gate_pe, 2)
            act.activation(g_all[:, :, :].rearrange("p a e -> p (a e)"),
                           bank[:, 5:7, :].rearrange("p b c -> p (b c)")[:, 0:TILES * HEADS * EXPERTS],
                           ACT.Sigmoid).then_inc(gate_act, 1)
            act.wait_ge(gate_pe, 3)
            act.activation(topT[:, :], bank[0:HEADS * EXPERTS, 2:5, :].rearrange("p b c -> p (b c)")[:, 0:NP],
                           ACT.Copy).then_inc(gate_act, 1)
            act.wait_ge(gate_act, 3)
            act.dma_start(topT_dram, topT[:, :]).then_inc(topT_out, 16)
            split_hi(act, "VA", 0)

            def exps(g, i, w):
                n = 10 * g + i
                act.wait_ge(neg_done, n + 1)
                wait(act, pT_pe, 15 * g + (i // 2) * (i // 2 + 1) // 2)
                act.activation(prob[:, i % 2, 0:w], bank[:, 2:5, :].rearrange("p b c -> p (b c)")[:, 0:w], ACT.Exp,
                               bias=rowstat[:, 0, i % 2:i % 2 + 1], scale=SCALE,
                               accum_out=rowstat[:, 1, i % 2:i % 2 + 1]).then_inc(exp_done, 1)

            def pT_hi_parts(g, s, q):
                for j in range(q + 1):
                    n = 15 * g + q * (q + 1) // 2 + j
                    b = (15 * s + q * (q + 1) // 2 + j) % 2
                    if s == 0 and q == 0:
                        for i in range(2):
                            act.wait_ge(x1_out[i], (5 * g + 5) * 16)
                    act.wait_ge(pT_pe, n + 1)
                    wait(act, pv_pe, n - 1)
                    act.activation(pT_hi[:, b, :], bank[:, 5 + b, :], ACT.Copy).then_inc(pT_hi_done, 1)

            def o_hi_part(g, s, q):
                act.wait_ge(pv_pe, 15 * g + (q + 1) * (q + 2) // 2)
                if s == 0 and q == 0:
                    act.wait_ge(m_lo_done, 20 * g + 40)
                part = slice(s * DH, (s + 1) * DH)
                side = (s + q) % 2
                act.activation(oT_hi[part, cols(q, 2 * P)], bank[part, 7, cols(side, 2 * P)], ACT.Copy).then_inc(o_hi, 1)

            def attention(g, s, beside=None):
                for i in range(TILES):
                    ready = due(g, s, i)
                    if ready:
                        pT_hi_parts(*ready)
                    if i == 0 and s == 0:
                        act.wait_ge(m_used, 20 * g + 40)
                        act.wait_ge(acc_done, 10 * g + 20)
                    exps(g, i, (i // 2 + 1) * 2 * P)
                    if ready:
                        o_hi_part(*ready)
                    if i == TILES - 2 and beside:
                        split_hi(act, *beside, 0, 2)
                if beside:
                    split_hi(act, *beside, 2)

            def qk_hi_parts(p, m):
                act.wait_ge(chunk_used, chunk_number("QK", p, 2 * m + 1) + 1)
                b = 2 + 3 * m
                for s in range(2):
                    part = slice(s * DH, (s + 1) * DH)
                    to = (q_st, kh_st)[m][s]
                    act.activation(to[part, :], bank[part, b:b + 3, :].rearrange("p b c -> p (b c)")[:, 0:NP],
                                   ACT.Copy).then_inc(qk_hi, 1)

            def masks_in(p, m):
                t = m % TILES
                act.wait_ge(m_lo_done, (20 * p + m - 1) * 2)
                for s in range(2):
                    rows = topT_dram[bass.ds((2 * (p - 1) + s) * EXPERTS, EXPERTS), cols(t)]
                    act.dma_start(mask[s * DH:(s + 1) * DH, t % 2, :, :],
                                 rows.unsqueeze(0).broadcast_to([DH, EXPERTS, P])).then_inc(mask_in[t % 2], 16)

            def first_masks(p):
                act.wait_ge(pv_pe, (2 * p) * 15)
                if not isinstance(p, int):
                    act.wait_ge(v_step, (2 * p + 1) * 3)
                for m in range(2):
                    masks_in(p, m)

            def moe(p, following=None):
                for m in range(2, TILES + 2):
                    masks_in(p, m)
                    if m == TILES:
                        split_hi(act, "O1", p, 0, 2)
                split_hi(act, "O1", p, 2)
                for m in range(TILES + 2, 2 * TILES):
                    masks_in(p, m)
                if following:
                    split_hi(act, *following)

            split_hi(act, "QK", 0)
            qk_hi_parts(0, 0)
            qk_hi_parts(0, 1)
            split_hi(act, "VB", 0)
            attention(0, 0)
            with act.Fori(1, PAIRS) as p:
                split_hi(act, "VA", p)
                attention(2 * p - 1, 1, ("QK", p))
                pT_hi_parts(2 * p - 1, 1, QUADS - 1)
                o_hi_part(2 * p - 1, 1, QUADS - 1)
                split_hi(act, "O0", p, 0, 6)
                qk_hi_parts(p, 0)
                split_hi(act, "O0", p, 6)
                first_masks(p)
                qk_hi_parts(p, 1)
                moe(p, ("VB", p))
                attention(2 * p, 0)
            attention(2 * PAIRS - 1, 1)
            pT_hi_parts(2 * PAIRS - 1, 1, QUADS - 1)
            o_hi_part(2 * PAIRS - 1, 1, QUADS - 1)
            first_masks(PAIRS)
            split_hi(act, "O0", PAIRS)
            moe(PAIRS)

        @block.tensor
        def _(pe):
            def transposes(n, tiles_in):
                pe.wait_ge(ln_done, n + 1)
                if n >= 2:
                    pe.wait_ge(xT_lo_done, n - 1)
                b = 2 * (n % 2)
                for k in range(KT):
                    last = pe.transpose(bank[:, b + k // 4, cols(k % 4)], tiles_in[:, (n % TILES) % 3, cols(k)], ident[:, :])
                last.then_inc(xT_pe, 1)

            def dense(stage, p, t, acc_ap, done, ready=None):
                for k, place in enumerate(SLOTS[stage]):
                    attend_step(ready, k)
                    if t == 0:
                        pe.wait_ge(chunk_lo, chunk_number(stage, p, k) + 1)
                    last = three(pe, acc_ap, xT_hi[:, k, cols(t)], xT_lo[:, k, cols(t)],
                                 ring_hi[:, place, :], ring_lo[:, place, :], k == 0, k == KT - 1)[-1]
                    if t == TILES - 1:
                        last.then_inc(chunk_used, 1)
                if t < TILES - 1:
                    last.then_inc(done, 1)

            def attend_step(ready, k):
                if ready is None:
                    return
                g, s, q = ready
                if k <= q:
                    n = 15 * g + q * (q + 1) // 2 + k
                    b = (15 * s + q * (q + 1) // 2 + k) % 2
                    if k == 0:
                        pe.wait_ge(prob_done, 10 * g + 2 * q + 2)
                if 2 <= k <= q + 2:
                    side = (s + q) % 2
                    rows = slice(0, DH) if s == 0 else slice(0, P)
                    o = bank[rows, 7, cols(side, 2 * P)]
                    j = k - 2
                    nj = 15 * g + q * (q + 1) // 2 + j
                    bj = (15 * s + q * (q + 1) // 2 + j) % 2
                    if j == 0:
                        pe.wait_ge(v_step, 3 * g + 3)
                        wait(pe, o_done, 5 * g + q - 1)
                    pe.wait_ge(pT_lo_done, nj + 1)
                    for jj in range(2):
                        u = 2 * j + jj
                        last = three(pe, o, v_hi[:, u, rows], v_lo[:, u, rows], pT_hi[:, bj, cols(jj, 2 * P)],
                                     pT_lo[:, bj, cols(jj, 2 * P)], u == 0, u == 2 * q + 1)[-1]
                    last.then_inc(pv_pe, 1)
                if k <= q:
                    wait(pe, pT_lo_done, n - 1)
                    for jj in range(2):
                        for i in range(2):
                            last = pe.transpose(bank[:, 5 + b, (2 * jj + i) * P:(2 * jj + i + 1) * P],
                                                prob[:, i, cols(2 * k + jj)], ident[:, :])
                    last.then_inc(pT_pe, 1)

            pe.wait_ge(consts, 14)
            pe.wait_ge(table_ready, 1)
            for n, of in enumerate((f_key, f_src)):
                for s in range(SUB):
                    last = pe.transpose(bank[:, 4 + n, cols(s, GROUPS)], of[:, cols(s)], ident[0:GROUPS, 0:GROUPS])
                last.then_inc(table_pe, 1)
            pe.matmul(bank[0:BLOCKS, 6, 0:2 * GROUPS], ones[0:GROUPS, 0:BLOCKS], diag[:, :],
                      start=True, stop=True).then_inc(table_pe, 1)
            pe.wait_ge(table_ready, 2)
            pe.matmul(bank[0:BLOCKS, 7, 0:1], before_tri[0:BLOCKS, :], table_f[:, 1:2],
                      start=True, stop=True).then_inc(table_pe, 1)
            pe.wait_ge(table_done, 1)

            def h_unit(n, t):
                u = n * TILES + t
                pe.wait_ge(xT_lo_done, t + 1)
                if u >= 2:
                    pe.wait_ge(h_done, u - 1)
                dense(f"W{n}", 0, t, bank[:, 4 + u % 2, :], h_pe)

            for t in range(TILES + 1):
                if t < TILES:
                    transposes(t, xin)
                if t >= 1:
                    h_unit(0, t - 1)
            pe.wait_ge(table_in, 16)
            for t in range(TILES):
                h_unit(1, t)
                for b in range(t * BLOCKS // TILES, (t + 1) * BLOCKS // TILES):
                    count = pe.value_load(table_row[0:1, 3 * b + 1:3 * b + 2], min_val=1, max_val=GROUPS)
                    past = pe.value_load(table_row[0:1, 3 * b + 2:3 * b + 3], min_val=0, max_val=GROUPS * BLOCKS)
                    counts = bank[:, 6 + b % 2, 0:KEYS]
                    if b >= 2:
                        pe.wait_ge(block_done, b - 1)
                    free = dict(skip_group_check=True)
                    pe.matmul(counts, zeros_b[:, 0:P], zeros_b[:, :], start=True, stop=False, **free)
                    with pe.Fori(0, count) as i:
                        for slot in range(OH_SLOTS):
                            pe.wait_ge(dst_ready, OH_SLOTS * (past + i) + slot + 2)
                            pe.wait_ge(src_ready, OH_SLOTS * (past + i) + slot + 2)
                            for s in range(PART):
                                last = pe.matmul(counts, onehot[:, slot, s, 0:P], onehot[:, slot, s, P:P + KEYS],
                                                 start=False, stop=False, **free)
                            last.then_inc(onehot_used, 1)
                    pe.matmul(counts, zeros_b[:, 0:P], zeros_b[:, :], start=False, stop=True, **free).then_inc(block_pe, 1)
            pe.wait_ge(a_summed, 1)
            for t in range(TILES):
                last = pe.matmul(bank[:, 4, t:t + 1], a_sum[:, cols(t)], ones[:, 0:1], start=True, stop=True)
            last.then_inc(deg_pe, 1)
            pe.wait_ge(a_diag, TILES)
            pe.wait_ge(h_scaled, TILES)
            for t in range(TILES):
                if t >= 2:
                    pe.wait_ge(agg_read, t - 1)
                for u in range(TILES):
                    for n in range(2):
                        last = pe.matmul(bank[:, 2 * (t % 2) + n, :], a_f[:, u, cols(t)], h[:, u, cols(n, HALF)],
                                         start=(u == 0), stop=(u == TILES - 1))
                last.then_inc(agg_pe, 1)
            pe.wait_ge(agg_read, TILES)
            for t in range(TILES):
                transposes(TILES + t, x2in)
            pe.wait_ge(xT_lo_done, 2 * TILES)
            pe.wait_ge(chunk_lo, chunk_number("G", 0, 0) + 1)
            GE = HEADS * EXPERTS
            place = SLOTS["G"][0]
            for k in range(KT):
                for c, w in ((0, HALF), (HALF, HALF), (2 * HALF, NP - 2 * HALF)):
                    last = three(pe, bank[0:GE, 2 + c // HALF, 0:w], ring_hi[:, place, cols(k, GE)],
                                 ring_lo[:, place, cols(k, GE)], xT_hi[:, k, c:c + w], xT_lo[:, k, c:c + w],
                                 k == 0, k == KT - 1)[-1]
            last.then_inc(gate_pe, 1)
            pe.wait_ge(gate_act, 1)
            for t in range(TILES):
                last = pe.transpose(bank[:, 5 + t // 8, cols(t % 8, GE)], logitT[:, cols(t)], ident[0:GE, 0:GE])
                if t == 0:
                    last.then_inc(chunk_used, 1)
            last.then_inc(gate_pe, 1)
            pe.wait_ge(gate_step, 5)
            for t in range(TILES):
                last = pe.transpose(bank[0:GE, 2 + t // 4, cols(t % 4)], top[:, t, :], ident[:, :])
            last.then_inc(gate_pe, 1)
            pe.wait_ge(gate_act, 3)

            def values_tile(g, stage, p, t, ready):
                n = 10 * g + t
                wait(pe, picked_done, n - 1)
                if stage == "VB" and t < 2:
                    pe.wait_ge(acc_done, 20 * p + 19 + t)
                dense(stage, p, t, bank[:, t % 2, :], values_pe, ready)

            def sim_row(g, s, i):
                n = 10 * g + i
                w = (i // 2 + 1) * 2 * P
                if i == 0 and s == 0:
                    pe.wait_ge(q_in, 16 * g + 32)
                    pe.wait_ge(k_in, 32 * g + 64)
                wait(pe, exp_done, n)
                for c in range(0, w, HALF):
                    e = min(w, c + HALF)
                    to = bank[:, 2 + c // HALF, 0:e - c]
                    lhs = q_st[s][:, cols(i)]
                    pe.matmul(to, lhs, kh_st[s][:, c:e], start=True, stop=False)
                    last = pe.matmul(to, lhs, kl_st[s][:, c:e], start=False, stop=True)
                    if e == w:
                        edge = bank[:, 2 + c // HALF, e - c - 2 * P:e - c]
                        last = pe.matmul(edge, ident_b[:, :], causal[:, i % 2, :], start=False, stop=True,
                                         skip_group_check=True)
                last.then_inc(sim_pe, 1)

            def values_and_attention(gv, stage, p, ga, sa):
                for t in range(TILES):
                    if ga is not None:
                        sim_row(ga, sa, t)
                    values_tile(gv, stage, p, t, due(ga, sa, t) if ga is not None else None)

            def qk(p, ready=None):
                for m in range(2):
                    b = 2 + 3 * m
                    if m == 0:
                        wait(pe, exp_done, 20 * p)
                    else:
                        wait(pe, pT_lo_done, 30 * p)
                        wait(pe, o_done, 10 * p)
                    for j in range(2):
                        place = SLOTS["QK"][2 * m + j]
                        pe.wait_ge(chunk_lo, chunk_number("QK", p, 2 * m + j) + 1)
                        for kk in range(4):
                            k = 4 * j + kk
                            if m == 0:
                                attend_step(ready, k)
                            for c, w in ((0, HALF), (HALF, HALF), (2 * HALF, NP - 2 * HALF)):
                                last = three(pe, bank[:, b + c // HALF, 0:w], ring_hi[:, place, cols(kk)],
                                             ring_lo[:, place, cols(kk)], xT_hi[:, k, c:c + w], xT_lo[:, k, c:c + w],
                                             k == 0, k == KT - 1)[-1]
                        last.then_inc(chunk_used, 1)

            def moe(p):
                pe.wait_ge(picked_done, 2 * TILES * PAIRS if isinstance(p, int) else 20 * p + 10)
                for n in range(2):
                    stage = f"O{n}"
                    for t in range(TILES):
                        m = 20 * p + TILES * n + t
                        pe.wait_ge(acc_done, m - 1)
                        for e in range(EXPERTS):
                            G = 2 * m + e // 4
                            u = (2 * (TILES * n + t) + e // 4) % M_SLOTS
                            place = SLOTS[stage][e]
                            if t == 0:
                                pe.wait_ge(chunk_lo, chunk_number(stage, p, e) + 1)
                            if e % 4 == 0:
                                pe.wait_ge(m_lo_done, G + 1)
                            of_three = three(pe, bank[:, t % 2, :], m_hi[:, u, e % 4, :], m_lo[:, u, e % 4, :],
                                             ring_hi[:, place, :], ring_lo[:, place, :], e == 0, e == EXPERTS - 1)
                            last = of_three[-1]
                            if t == TILES - 1 and e == 4:
                                of_three[0].then_inc(chunk_used, 1)
                            if e % 4 == 3:
                                last.then_inc(m_used, 1)
                            elif t == TILES - 1:
                                last.then_inc(chunk_used, 1)
                        if t == TILES - 1:
                            pe.drain().then_inc(chunk_used, 1)

            values_and_attention(0, "VA", 0, None, None)
            qk(0)
            values_and_attention(1, "VB", 0, 0, 0)
            with pe.Fori(1, PAIRS) as p:
                values_and_attention(2 * p, "VA", p, 2 * p - 1, 1)
                qk(p, (2 * p - 1, 1, QUADS - 1))
                moe(p)
                values_and_attention(2 * p + 1, "VB", p, 2 * p, 0)
            for i in range(TILES + 1):
                if i < TILES:
                    sim_row(2 * PAIRS - 1, 1, i)
                ready = due(2 * PAIRS - 1, 1, i)
                for k in range(QUADS + 2):
                    attend_step(ready, k)
            moe(PAIRS)

        @block.vector
        def _(dve):
            dve.memset(e_dst[:, :], -(1 << 20)).then_inc(filled, 1)
            dve.memset(e_dst_hi[:, :], 1 << 20).then_inc(filled, 1)
            dve.memset(e_src[:, :], 0).then_inc(filled, 1)
            steps = {}

            def chain(ins, semaphore=table_step):
                steps[id(semaphore)] = steps.get(id(semaphore), 0) + 1
                ins.then_inc(semaphore, 1)
                dve.wait_ge(semaphore, steps[id(semaphore)])

            dve.memset(ones[:, :], 1.0).then_inc(table_step, 1)
            dve.memset(krel[:, :], 0.0).then_inc(dst_ready, 1)
            dve.memset(srel[:, :], 0.0).then_inc(src_ready, 1)
            dve.memset(zeros_b[:, :], 0.0).then_inc(onehot_used, OH_SLOTS)
            steps[id(table_step)] = 1
            split_lo(dve, "W0", 0)
            dve.wait_ge(consts, 14)
            dve.wait_ge(edges_in, 96)
            chain(dve.tensor_copy(iota[:, :], iota_f[:, :]))
            chain(dve.tensor_single_scalar(e_t0[:, :], e_dst[:, :], 5, ALU.arith_shift_right))
            chain(dve.tensor_single_scalar(e_t1[:, :], e_src[:, :], 7, ALU.arith_shift_right))
            for to, of in ((f_dst, e_dst), (f_dst_hi, e_dst_hi), (f_src, e_src), (f_key, e_t0), (f_hi, e_t1)):
                chain(dve.tensor_copy(to[:, :], of[:, :]))
            chain(dve.tensor_reduce(minmax[:, 0:1], f_dst_hi[:, :], AX_X, ALU.min))
            chain(dve.tensor_reduce(minmax[:, 1:2], f_dst[:, :], AX_X, ALU.max))
            chain(dve.tensor_scalar(f_dst_hi[:, :], f_dst[:, :], float(TILES), None, ALU.mult))
            chain(dve.scalar_tensor_tensor(out=f_key[:, :], in0=f_key[:, :], scalar=float(BLOCK_KEY - TILES * BLOCK),
                                           in1=f_dst_hi[:, :], op0=ALU.mult, op1=ALU.add))
            chain(dve.tensor_tensor(f_key[:, :], f_key[:, :], f_hi[:, :], ALU.add))
            chain(dve.scalar_tensor_tensor(out=f_src[:, :], in0=f_hi[:, :], scalar=-float(P), in1=f_src[:, :],
                                           op0=ALU.mult, op1=ALU.add))
            for i in range(2):
                last = dve.tensor_scalar(diag[:, cols(i, GROUPS)], ident[0:GROUPS, 0:GROUPS], minmax[:, i:i + 1], None,
                                         ALU.mult)
            last.then_inc(table_ready, 1)
            dve.wait_ge(table_pe, 3)
            chain(dve.tensor_copy(keyT[:, :, :].rearrange("p g s -> p s g"),
                                  bank[:, 4, 0:SUB * GROUPS].rearrange("p (s g) -> p s g", s=SUB)))
            chain(dve.tensor_copy(modT[:, :, :].rearrange("p g s -> p s g"),
                                  bank[:, 5, 0:SUB * GROUPS].rearrange("p (s g) -> p s g", s=SUB)))
            least, greatest = bank[0:BLOCKS, 6, 0:GROUPS], bank[0:BLOCKS, 6, GROUPS:2 * GROUPS]
            chain(dve.tensor_scalar(over_t[:, 0, :], least, -float(BLOCK - 1), block_lo[0:BLOCKS, :], ALU.add, ALU.is_le))
            chain(dve.tensor_scalar(over_t[:, 1, :], greatest, block_lo[0:BLOCKS, :], None, ALU.is_ge))
            chain(dve.tensor_tensor(over[:, :], over_t[:, 0, :], over_t[:, 1, :], ALU.mult))
            chain(dve.scalar_tensor_tensor(out=over_t[:, 0, :], in0=over[:, :], scalar=-1000.0,
                                           in1=group_no[0:BLOCKS, :], op0=ALU.mult, op1=ALU.add))
            chain(dve.tensor_reduce(table_f[:, 0:1], over_t[:, 0, :], AX_X, ALU.min))
            chain(dve.tensor_scalar(table_f[:, 0:1], table_f[:, 0:1], 1000.0, float(GROUPS - 1), ALU.add, ALU.min))
            chain(dve.scalar_tensor_tensor(out=over_t[:, 1, :], in0=group_no[0:BLOCKS, :], scalar=1.0,
                                           in1=over[:, :], op0=ALU.add, op1=ALU.mult))
            chain(dve.tensor_reduce(table_f[:, 1:2], over_t[:, 1, :], AX_X, ALU.max))
            chain(dve.tensor_tensor(table_f[:, 1:2], table_f[:, 1:2], table_f[:, 0:1], ALU.subtract))
            dve.tensor_scalar(table_f[:, 1:2], table_f[:, 1:2], 1.0, None, ALU.max).then_inc(table_ready, 1)
            dve.wait_ge(table_ready, 2)
            dve.wait_ge(table_pe, 4)
            chain(dve.tensor_copy(table_f[:, 2:3], bank[0:BLOCKS, 7, 0:1]))
            dve.tensor_copy(table_i[:, :], table_f[:, :]).then_inc(table_done, 1)

            ln = [0]

            def ln_chain(ins):
                ln[0] += 1
                ins.then_inc(ln_step, 1)
                dve.wait_ge(ln_step, ln[0])

            roots = [0]

            def rsqrt(to, w):
                roots[0] += 1
                dve.wait_ge(ln_sqrt, roots[0])
                ln_chain(dve.reciprocal(nt[:, 2, 0:w], nt[:, 1, 0:w]))
                ln_chain(dve.tensor_tensor(nt[:, 3, 0:w], nt[:, 2, 0:w], nt[:, 2, 0:w], ALU.mult))
                ln_chain(dve.tensor_tensor(nt[:, 3, 0:w], nt[:, 3, 0:w], nt[:, 0, 0:w], ALU.mult))
                ln_chain(dve.tensor_scalar(nt[:, 3, 0:w], nt[:, 3, 0:w], -0.5, 1.5, ALU.mult, ALU.add))
                ln_chain(dve.tensor_tensor(to, nt[:, 2, 0:w], nt[:, 3, 0:w], ALU.mult))

            def statistics(tile, t):
                for n in range(2):
                    dve.bn_stats(stats[:, n, :], tile[:, cols(n, HALF)]).then_inc(ln_step, 1)
                ln[0] += 2
                dve.wait_ge(ln_step, ln[0])
                ln_chain(dve.bn_aggr(mv[:, t, :], stats[:, :, :]))
                dve.tensor_scalar(nt[:, 0, 0:1], mv[:, t, 1:2], LN_EPS, None, ALU.add).then_inc(ln_var, 1)
                rsqrt(rstd[:, t:t + 1], 1)

            def normalise(tile, t):
                dve.tensor_scalar(tile, tile, mv[:, t, 0:1], rstd[:, t:t + 1], ALU.subtract, ALU.mult).then_inc(ln_done, 1)

            def xT_lo_part(t, n):
                dve.wait_ge(xT_hi_done, n + 1)
                b = 2 * (n % 2)
                dve.tensor_tensor(xT_lo[:, :, cols(t)], bank[:, b:b + 2, :].rearrange("p b (k c) -> p (b k) c", c=P),
                                  xT_hi[:, :, cols(t)], ALU.subtract).then_inc(xT_lo_done, 1)

            for t in range(TILES):
                if t == TILES - 1:
                    dve.wait_ge(xT_pe, TILES - 3)
                    dve.memset(xin[96:P, t % 3, :], 0.0).then_inc(filled, 1)
                    dve.wait_ge(filled, 4)
                dve.wait_ge(xin_in[t % 3], 16 * (t // 3 + 1))
                tile = xin[:, t % 3, :]
                statistics(tile, t)
                normalise(tile, t)
                xT_lo_part(t, t)
            split_lo(dve, "W1", 0)
            dve.wait_ge(table_in, 16)
            for b in range(BLOCKS):
                first = dve.value_load(table_row[0:1, 3 * b:3 * b + 1], min_val=0, max_val=GROUPS - 1)
                count = dve.value_load(table_row[0:1, 3 * b + 1:3 * b + 2], min_val=1, max_val=GROUPS)
                past = dve.value_load(table_row[0:1, 3 * b + 2:3 * b + 3], min_val=0, max_val=GROUPS * BLOCKS)
                with dve.Fori(0, count) as i:
                    g = (first + i).with_bounds(min_val=0, max_val=GROUPS - 1)
                    dve.wait_ge(dst_ready, OH_SLOTS * (past + i) + 1)
                    dve.tensor_scalar(krel[:, :], keyT[:, bass.ds(g, 1), :].rearrange("p a s -> p (a s)"),
                                      key_offset[:, b:b + 1], None, ALU.add).then_inc(key_ready, 1)
                    for slot in range(OH_SLOTS):
                        dve.wait_ge(onehot_used, OH_SLOTS * (past + i) + slot + 1)
                        for s in range(POOL_SUBS, PART):
                            dve.tensor_scalar(onehot[:, slot, s, 0:P], iota[:, 0:P],
                                              modT[:, bass.ds(g, 1), PART * slot + s], None, ALU.is_equal)
                        dve.wait_ge(key_ready, past + i + 1)
                        for s in range(PART):
                            last = dve.tensor_scalar(onehot[:, slot, s, P:P + KEYS], iota[:, :],
                                                     krel[:, PART * slot + s:PART * slot + s + 1], None, ALU.is_equal)
                        last.then_inc(dst_ready, 1)
            dve.wait_ge(block_done, BLOCKS)
            dve.wait_ge(block_pe, BLOCKS)
            sums = [0]

            def a_chain(ins):
                sums[0] += 1
                ins.then_inc(a_step, 1)
                dve.wait_ge(a_step, sums[0])

            a_chain(dve.tensor_tensor(a_sum[:, :], a_u16[:, 0, :], a_u16[:, 1, :], ALU.add))
            for u in range(2, TILES - 1):
                a_chain(dve.tensor_tensor(a_sum[:, :], a_sum[:, :], a_u16[:, u, :], ALU.add))
            dve.tensor_tensor(a_sum[:, :], a_sum[:, :], a_u16[:, TILES - 1, :], ALU.add).then_inc(a_summed, 1)
            for t in range(TILES):
                dve.wait_ge(a_ready, t + 1)
                dve.tensor_tensor(a_f[:, t, cols(t)], a_f[:, t, cols(t)], ident[:, :], ALU.add).then_inc(a_diag, 1)
            dve.wait_ge(deg_pe, 1)
            dve.tensor_scalar(nt[:, 0, :], bank[:, 4, 0:TILES], 1.0, None, ALU.add).then_inc(ln_var, 1)
            rsqrt(dinv[:, :], TILES)
            dve.wait_ge(h_done, 2 * TILES)
            for t in range(TILES):
                dve.tensor_scalar(h[:, t, :], h[:, t, :], dinv[:, t:t + 1], None, ALU.mult).then_inc(h_scaled, 1)
            dve.wait_ge(a_summed, 1)
            dve.wait_ge(bias_in, 16)
            for t in range(TILES):
                tile = xres[:, t % 2, :]
                if t == TILES - 1:
                    dve.wait_ge(x1_out[t % 2], 16 * (t // 2))
                    dve.memset(xres[96:P, t % 2, :], 0.0).then_inc(filled, 1)
                    dve.wait_ge(filled, 5)
                dve.wait_ge(agg_pe, t + 1)
                b = 2 * (t % 2)
                dve.scalar_tensor_tensor(out=y[:, :], in0=bank[:, b:b + 2, :].rearrange("p b c -> p (b c)"),
                                         scalar=dinv[:, t:t + 1], in1=bias[:, :], op0=ALU.mult,
                                         op1=ALU.add).then_inc(agg_read, 1)
                dve.wait_ge(agg_read, t + 1)
                dve.wait_ge(xres_in[t % 2], 16 * (t // 2 + 1))
                dve.scalar_tensor_tensor(out=tile, in0=y[:, :], scalar=0.0, in1=tile, op0=ALU.max,
                                         op1=ALU.add).then_inc(x1_ready, 1)
                dve.wait_ge(x1_ready, t + 1)
                statistics(tile, t)
            split_lo(dve, "G", 0)
            for t in range(TILES):
                dve.wait_ge(x2_in[t % 3], 16 * (t // 3 + 1))
                normalise(x2in[:, t % 3, :], t)
                xT_lo_part(t, TILES + t)
            steps[id(gate_step)] = 0
            dve.wait_ge(gate_act, 2)
            flat = [P, TILES * HEADS, EXPERTS]
            of_max = gate[:, :, :].rearrange("p t h -> p (t h)").unsqueeze(2).broadcast_to(flat)
            ranks = rank[:, :].unsqueeze(1).broadcast_to(flat)
            top_v = top[:, :, :].rearrange("p t (h e) -> p (t h) e", e=EXPERTS)
            chain(dve.tensor_reduce(gate[:, :, :].rearrange("p t h -> p (t h)"), g_all[:, :, :], AX_X, ALU.max), gate_step)
            chain(dve.tensor_tensor(g_t[:, :, :], g_all[:, :, :], of_max, ALU.is_equal), gate_step)
            chain(dve.tensor_tensor(g_t[:, :, :], g_t[:, :, :], ranks, ALU.mult), gate_step)
            chain(dve.tensor_reduce(g_m[:, :], g_t[:, :, :], AX_X, ALU.max), gate_step)
            chain(dve.tensor_tensor(top_v, g_t[:, :, :], g_m[:, :].unsqueeze(2).broadcast_to(flat), ALU.is_equal), gate_step)
            split_lo(dve, "VA", 0)
            dve.wait_ge(topT_out, 16)

            def pick(g, t, stage, p):
                n = 10 * g + t
                if stage == "VB" and t == TILES - 1 and not isinstance(p, int):
                    dve.wait_ge(chunk_used, chunk_number("VA", p + 1, 0))
                else:
                    wait_dense(dve, values_pe, stage, p, g, t)
                wait(dve, value_done, n - 1)
                hot = top[:, t, bass.ds(g * EXPERTS, EXPERTS)].unsqueeze(2).broadcast_to([P, EXPERTS, DH])
                mul = picked[:, t % 2, :].rearrange("p (e c) -> p e c", e=EXPERTS)
                dve.tensor_tensor(mul, bank[:, t % 2, :].rearrange("p (e c) -> p e c", e=EXPERTS), hot,
                                  ALU.mult).then_inc(picked_done, 1)
                dve.wait_ge(picked_done, n + 1)
                wait(dve, v_step, 3 * g)
                dve.tensor_reduce(v_raw[:, t, :], mul.rearrange("p e c -> p c e"), AX_X, ALU.add).then_inc(value_done, 1)

            def finish_values(g, s):
                dve.wait_ge(value_done, 10 * g + 10)
                if s == 0:
                    wait(dve, pv_pe, 15 * g)
                mine = slice(s * DH, (s + 1) * DH)
                gates = gate[:, :, bass.ds(g, 1)].broadcast_to([P, TILES, DH])
                dve.tensor_tensor(v_raw[:, :, :], v_raw[:, :, :], gates, ALU.mult).then_inc(v_step, 1)
                dve.wait_ge(v_step, 3 * g + 1)
                dve.tensor_copy(v_hi[:, :, mine], v_raw[:, :, :]).then_inc(v_step, 1)
                dve.wait_ge(v_step, 3 * g + 2)
                dve.tensor_tensor(v_lo[:, :, mine], v_raw[:, :, :], v_hi[:, :, mine], ALU.subtract).then_inc(v_step, 1)

            def row_max(g, i, w):
                n = 10 * g + i
                dve.wait_ge(sim_pe, n + 1)
                wait(dve, norm_done, n - 1)
                dve.tensor_reduce(rowstat[:, 2, i % 2:i % 2 + 1],
                                  bank[:, 2:5, :].rearrange("p b c -> p (b c)")[:, 0:w], AX_X, ALU.max).then_inc(max_done, 1)
                dve.wait_ge(max_done, n + 1)
                wait(dve, exp_done, n - 1)
                dve.tensor_scalar(rowstat[:, 0, i % 2:i % 2 + 1], rowstat[:, 2, i % 2:i % 2 + 1], -SCALE, None,
                                  ALU.mult).then_inc(neg_done, 1)

            def row_norm(g, i, w):
                n = 10 * g + i
                one = slice(i % 2, i % 2 + 1)
                dve.wait_ge(exp_done, n + 1)
                dve.wait_ge(neg_done, n + 1)
                dve.reciprocal(rowstat[:, 2, one], rowstat[:, 1, one]).then_inc(inv_done, 1)
                dve.wait_ge(inv_done, n + 1)
                wait(dve, prob_done, n - 1)
                dve.tensor_tensor(rowstat[:, 3, one], rowstat[:, 2, one], gate[:, i, bass.ds(g, 1)],
                                  ALU.mult).then_inc(norm_done, 1)
                dve.wait_ge(norm_done, n + 1)
                dve.tensor_scalar(prob[:, i % 2, 0:w], prob[:, i % 2, 0:w], rowstat[:, 3, one], None,
                                  ALU.mult).then_inc(prob_done, 1)

            def pT_lo_part(g, s, q, j):
                n = 15 * g + q * (q + 1) // 2 + j
                b = (15 * s + q * (q + 1) // 2 + j) % 2
                dve.wait_ge(pT_hi_done, n + 1)
                dve.tensor_tensor(pT_lo[:, b, :], bank[:, 5 + b, :], pT_hi[:, b, :], ALU.subtract).then_inc(pT_lo_done, 1)

            def o_lo_part(g, s, q):
                part = slice(s * DH, (s + 1) * DH)
                side = (s + q) % 2
                dve.wait_ge(o_hi, 5 * g + q + 1)
                dve.tensor_tensor(oT_lo[part, cols(q, 2 * P)], bank[part, 7, cols(side, 2 * P)],
                                  oT_hi[part, cols(q, 2 * P)], ALU.subtract).then_inc(o_done, 1)

            def attention(g, s, values=None, following=None):
                for i in range(TILES):
                    w = (i // 2 + 1) * 2 * P
                    row_max(g, i, w)
                    ready = due(g, s, i)
                    if ready:
                        pT_lo_part(*ready, 0)
                    if values and i >= 1:
                        pick(values[0], i - 1, *values[1:])
                    if ready:
                        for j in range(1, ready[2] + 1):
                            pT_lo_part(*ready, j)
                    row_norm(g, i, w)
                    if ready:
                        o_lo_part(*ready)
                    if i == TILES - 2 and following:
                        split_lo(dve, *following, 0, 2)
                if following:
                    split_lo(dve, *following, 2)

            def last_rows(g):
                for j in range(QUADS):
                    pT_lo_part(g, 1, QUADS - 1, j)
                o_lo_part(g, 1, QUADS - 1)

            def qk_lo_parts(p, m):
                for s in range(2):
                    part = slice(s * DH, (s + 1) * DH)
                    dve.wait_ge(qk_hi, 4 * p + 2 * m + s + 1)
                    hi, lo = ((q_st[s], q_lo), (kh_st[s], kl_st[s]))[m]
                    b = 2 + 3 * m
                    dve.tensor_tensor(lo[part, :], bank[part, b:b + 3, :].rearrange("p b c -> p (b c)")[:, 0:NP],
                                      hi[part, :], ALU.subtract).then_inc(qk_lo, 1)

            def moe_half(p, half, following=None):
                def make(m):
                    t = m % TILES
                    for u in range(2):
                        n = 2 * m + u
                        G = 40 * p + n
                        if u == 0:
                            dve.wait_ge(mask_in[m % 2], 32 * ((p - 1) * 10 + m // 2 + 1))
                        if n == 0:
                            dve.wait_ge(o_done, 10 * p)
                        dve.wait_ge(m_used, G if n == 0 else G - M_SLOTS + 1)
                        for oT, to, done in ((oT_hi, m_hi, m_hi_done), (oT_lo, m_lo, m_lo_done)):
                            dve.tensor_tensor(to[:, n % M_SLOTS, :, :], oT[:, cols(t)].unsqueeze(1).broadcast_to([P, 4, P]),
                                              mask[:, t % 2, 4 * u:4 * u + 4, :], ALU.mult).then_inc(done, 1)

                def add(m):
                    t = m % TILES
                    M = 20 * p + m
                    rows = LAST if t == TILES - 1 else P
                    dve.wait_ge(m_used, 2 * M + 2)
                    dve.wait_ge(acc_in[t % 2], 16 * ((p - 1) * 10 + m // 2 + 1))
                    dve.tensor_tensor(acc[0:rows, t % 2, :], acc[0:rows, t % 2, :], bank[0:rows, t % 2, :],
                                      ALU.add).then_inc(acc_done, 1)

                for t in range(TILES):
                    m = half * TILES + t
                    if m == 0:
                        make(m)
                    if m < 2 * TILES - 1:
                        make(m + 1)
                    if t >= 1:
                        add(m - 1)
                    if t == TILES - 2 and following:
                        split_lo(dve, *following, 0, 2)
                if following:
                    split_lo(dve, *following, 2)
                add(half * TILES + TILES - 1)

            for t in range(TILES):
                pick(0, t, "VA", 0)
            finish_values(0, 0)
            split_lo(dve, "QK", 0)
            qk_lo_parts(0, 0)
            qk_lo_parts(0, 1)
            split_lo(dve, "VB", 0)
            attention(0, 0, (1, "VB", 0))
            with dve.Fori(1, PAIRS) as p:
                split_lo(dve, "VA", p)
                pick(2 * p - 1, TILES - 1, "VB", p - 1)
                finish_values(2 * p - 1, 1)
                attention(2 * p - 1, 1, (2 * p, "VA", p), ("QK", p))
                pick(2 * p, TILES - 1, "VA", p)
                last_rows(2 * p - 1)
                split_lo(dve, "O0", p, 0, 6)
                qk_lo_parts(p, 0)
                finish_values(2 * p, 0)
                split_lo(dve, "O0", p, 6)
                qk_lo_parts(p, 1)
                moe_half(p, 0, ("O1", p))
                moe_half(p, 1, ("VB", p))
                attention(2 * p, 0, (2 * p + 1, "VB", p))
            pick(2 * PAIRS - 1, TILES - 1, "VB", PAIRS - 1)
            finish_values(2 * PAIRS - 1, 1)
            attention(2 * PAIRS - 1, 1)
            last_rows(2 * PAIRS - 1)
            split_lo(dve, "O0", PAIRS)
            moe_half(PAIRS, 0, ("O1", PAIRS))
            moe_half(PAIRS, 1)


_INS = ["x", "src", "dst", "L0_gnn_W", "L0_gnn_b", "L0_ffn_w_q", "L0_ffn_w_k", "L0_ffn_w_gate",
        "L0_ffn_value_experts", "L0_ffn_output_experts"]


def kernel(**inputs):
    import numpy as _np
    import concourse.bacc as _bacc
    from concourse import mybir as _mybir
    from concourse.bass_utils import run_bass_kernel_spmd as _run

    nc = _bacc.Bacc("TRN2", target_bir_lowering=False, num_devices=1)
    arrays, args = {}, []
    for name in _INS:
        a = _np.ascontiguousarray(inputs[name])
        arrays[f"in_{name}_dram"] = a
        args.append(nc.dram_tensor(f"in_{name}_dram", a.shape, _mybir.dt.from_np(a.dtype), kind="ExternalInput").ap())
    out = nc.dram_tensor("out_0_dram", (N, D), F32, kind="ExternalOutput").ap()
    build(nc, *args, out)
    r = _run(nc, [arrays], core_ids=[0])
    return r.results[0]["out_0_dram"]
```

```python
from contextlib import ExitStack

import concourse.bass as bass
from concourse import mybir

F32 = mybir.dt.float32
F32R = mybir.dt.float32r
BF16 = mybir.dt.bfloat16
FP16 = mybir.dt.float16
I32 = mybir.dt.int32
U16 = mybir.dt.uint16
ALU = mybir.AluOpType
ACT = mybir.ActivationFunctionType
AX_X = mybir.AxisListType.X

P = 128
N = 1250
D = 1024
E = 40000
HEADS, DH, EXPERTS = 8, 64, 8
PAIRS = HEADS // 2
TILES = -(-N // P)
NP = TILES * P
QUADS = TILES // 2
LAST = N - (TILES - 1) * P
KT = D // P
HALF = 512
SCALE = DH ** -0.5
LN_EPS = 1e-5
NEG = -3.0e38

GROUP = 512
SUB = GROUP // P
GROUPS = -(-E // GROUP)
FULL_GROUPS = E // GROUP
REST = E - FULL_GROUPS * GROUP
BLOCK = 32
BLOCKS = NP // BLOCK
KEYS = BLOCK * TILES
BLOCK_KEY = 1024
OH_SLOTS = 2
PART = SUB // OH_SLOTS

M_SLOTS = 3
RING, RAW = 10, 4

SLOTS = {
    "W0": [0, 1, 2, 3, 4, 5, 6, 7],
    "W1": [8, 9, 0, 1, 2, 3, 4, 5],
    "G": [6],
    "VA": [4, 5, 0, 1, 2, 3, 6, 7],
    "QK": [8, 9, 4, 5],
    "O0": [0, 1, 2, 3, 6, 7, 8, 9],
    "O1": [4, 5, 0, 1, 2, 3, 6, 7],
    "VB": [8, 9, 0, 1, 2, 3, 6, 7],
}
FIRST = [("W0", 0), ("W1", 0), ("G", 0), ("QK", 0), ("VA", 0), ("VB", 0)]
EACH = ["VA", "QK", "O0", "O1", "VB"]


def plan_chunks():
    stages = FIRST + [(s, p) for p in range(1, PAIRS) for s in EACH] + [("O0", PAIRS), ("O1", PAIRS)]
    first, before, held, n = {}, {}, {}, 0
    for stage in stages:
        first[stage] = n
        for k, slot in enumerate(SLOTS[stage[0]]):
            before[stage, k] = held.get(slot, -1)
            held[slot] = n
            n += 1
    return first, before


CHUNK_FIRST, CHUNK_BEFORE = plan_chunks()
PER_PAIR = sum(len(SLOTS[s]) for s in EACH)


def chunk_number(stage, p, k):
    if isinstance(p, int):
        return CHUNK_FIRST[stage, p] + k
    return (CHUNK_FIRST[stage, 1] - PER_PAIR + k) + p * PER_PAIR


def chunk_raw(stage, p, k):
    if isinstance(p, int):
        n = CHUNK_FIRST[stage, p] + k
        return n % RAW, n // RAW + 1
    n = CHUNK_FIRST[stage, 1] + k
    return n % RAW, p * (PER_PAIR // RAW) + (n // RAW + 1 - PER_PAIR // RAW)


def chunk_before(stage, p, k):
    if isinstance(p, int):
        return CHUNK_BEFORE[(stage, p), k] + 1
    gap = CHUNK_FIRST[stage, 1] + k - CHUNK_BEFORE[(stage, 1), k]
    gap = min(CHUNK_FIRST[stage, q] + k - CHUNK_BEFORE[(stage, q), k] for q in range(1, PAIRS))
    return chunk_number(stage, p, k) - gap + 1


assert PER_PAIR % RAW == 0


def past_pairs(p):
    return isinstance(p, int) and p == PAIRS


def wait(engine, semaphore, value):
    if not isinstance(value, int) or value > 0:
        engine.wait_ge(semaphore, value)


def build(nc, x, src, dst, gnn_w, gnn_b, w_q, w_k, w_gate, value_experts, output_experts, out):
    with ExitStack() as ctx:
        def sem(name):
            return ctx.enter_context(nc.semaphore(name))

        base = (nc.sbuf_base + 63) // 64 * 64
        limit = nc.sbuf_usable_end

        def at(name, offset, shape, dtype):
            size = mybir.dt.size(dtype)
            for s in shape[1:]:
                size *= s
            assert base + offset + size <= limit, (name, base + offset + size, limit)
            return nc.alloc_sbuf_tensor_at(name, shape, dtype, offset=base + offset)

        class Region:
            def __init__(self, start):
                self.next = start

            def put(self, name, shape, dtype):
                t = at(name, self.next, shape, dtype)
                size = mybir.dt.size(dtype)
                for s in shape[1:]:
                    size *= s
                self.next += -(-size // 32) * 32
                return t

        r = Region(0)
        xT_hi = r.put("xT_hi", [P, KT, NP], F32R)
        xT_lo = r.put("xT_lo", [P, KT, NP], F32R)
        ring_hi_at = r.next
        ring_hi = r.put("ring_hi", [P, RING, HALF], F32R)
        ring_lo_at = r.next
        ring_lo = r.put("ring_lo", [P, RING, HALF], F32R)
        raw = r.put("raw", [P, RAW, HALF], F32)
        ident = r.put("ident", [P, P], F32)
        ident_b = r.put("ident_b", [P, P], BF16)
        causal = r.put("causal", [P, 2, 2 * P], BF16)
        rank = r.put("rank", [P, EXPERTS], F32)
        ones = r.put("ones", [P, BLOCKS], F32)
        mv = r.put("mv", [P, TILES, 2], F32)
        rstd = r.put("rstd", [P, TILES], F32)
        nt = r.put("nt", [P, 4, TILES], F32)
        stats = r.put("stats", [P, 2, 6], F32)
        dinv = r.put("dinv", [P, TILES], F32)
        most = r.put("most", [P, 2], F32)
        many = r.put("many", [1, 1], I32)
        rowstat = r.put("rowstat", [P, 4, 2], F32)
        scratch = r.put("scratch", [P, 8], F32)
        z = r.next

        h_hi = at("h_hi", 0, [P, TILES, D], F32R)
        h_lo = at("h_lo", 4 * TILES * D, [P, TILES, D], F32R)
        xin_place = (RING - 2) * HALF * 4
        xin = [at("xin0", ring_hi_at + xin_place, [P, D], F32), at("xin1", ring_lo_at + xin_place, [P, D], F32)]
        r = Region(ring_hi_at)
        a_hi = r.put("a_hi", [P, 2, TILES, P], F32R)
        a_lo = r.put("a_lo", [P, 2, TILES, P], F32R)
        assert r.next <= ring_lo_at
        a_sum_f = at("a_sum_f", ring_lo_at, [P, NP], F32)
        r = Region(ring_lo_at)
        xres = r.put("xres", [P, 2, D], F32)
        y = r.put("y", [P, D], F32)
        bias = r.put("bias", [P, D], F32)
        r = Region(z)
        h_at = z
        h = r.put("h", [P, TILES, D], F32)
        a_at = r.next
        a_u16 = r.put("a_u16", [P, TILES, NP], U16)
        oh_at = r.next
        onehot = r.put("onehot", [P, OH_SLOTS, PART, P + KEYS], BF16)
        iota = r.put("iota", [P, KEYS], FP16)
        keyT = r.put("keyT", [P, GROUPS, SUB], F32)
        modT = r.put("modT", [P, GROUPS, SUB], F32)
        pool_src = r.put("pool_src", [P, OH_SLOTS], F32)
        zeros_b = r.put("zeros_b", [P, KEYS], BF16)
        key_offset = r.put("key_offset", [P, BLOCKS], F32)
        table_row = r.put("table_row", [1, BLOCKS], I32)
        a_sum = r.put("a_sum", [P, NP], U16)
        r = Region(h_at)
        e_dst = r.put("e_dst", [GROUPS, GROUP], I32)
        e_dst_hi = r.put("e_dst_hi", [GROUPS, GROUP], I32)
        e_src = r.put("e_src", [GROUPS, GROUP], I32)
        e_t0 = r.put("e_t0", [GROUPS, GROUP], I32)
        e_t1 = r.put("e_t1", [GROUPS, GROUP], I32)
        f_dst = r.put("f_dst", [GROUPS, GROUP], F32)
        f_dst_hi = r.put("f_dst_hi", [GROUPS, GROUP], F32)
        f_src = r.put("f_src", [GROUPS, GROUP], F32)
        f_key = r.put("f_key", [GROUPS, GROUP], F32)
        f_hi = r.put("f_hi", [GROUPS, GROUP], F32)
        minmax = r.put("minmax", [GROUPS, 2], F32)
        diag = r.put("diag", [GROUPS, 2 * GROUPS], F32)
        block_lo = r.put("block_lo", [P, 1], F32)
        group_no = r.put("group_no", [P, GROUPS], F32)
        over = r.put("over", [BLOCKS, GROUPS], F32)
        over_t = r.put("over_t", [BLOCKS, 2, GROUPS], F32)
        table_f = r.put("table_f", [BLOCKS, 2], F32)
        table_i = r.put("table_i", [BLOCKS, 1], I32)
        iota_f = r.put("iota_f", [P, KEYS], F32)
        assert r.next <= a_at
        r = Region(z)
        q_st = [r.put(f"q_st{s}", [P, NP], F32R) for s in range(2)]
        kh_st = [r.put(f"kh_st{s}", [P, NP], F32R) for s in range(2)]
        kl_st = [r.put(f"kl_st{s}", [P, NP], F32R) for s in range(2)]
        v_hi = r.put("v_hi", [P, TILES, P], F32R)
        v_lo = r.put("v_lo", [P, TILES, P], F32R)
        v_raw = r.put("v_raw", [P, TILES, DH], F32)
        oT_hi = r.put("oT_hi", [P, NP], F32R)
        oT_lo = r.put("oT_lo", [P, NP], F32R)
        top = r.put("top", [P, TILES, HEADS * EXPERTS], F32)
        gate = r.put("gate", [P, TILES, HEADS], F32)
        shared_at = r.next
        picked = r.put("picked", [P, 2, HALF], F32)
        prob = r.put("prob", [P, 2, NP], F32)
        pT_hi = r.put("pT_hi", [P, 2, HALF], F32R)
        pT_lo = r.put("pT_lo", [P, 2, HALF], F32R)
        r = Region(shared_at)
        m_hi = r.put("m_hi", [P, M_SLOTS, 4, P], F32R)
        m_lo = r.put("m_lo", [P, M_SLOTS, 4, P], F32R)
        mask = r.put("mask", [P, 2, EXPERTS, P], BF16)
        q_lo_at = r.next
        acc = r.put("acc", [P, 2, HALF], F32)
        r = Region(q_lo_at)
        q_lo = r.put("q_lo", [P, NP], F32R)
        r = Region(shared_at + 4 * 2 * HALF)
        logitT = r.put("logitT", [HEADS * EXPERTS, NP], F32)
        g_all = r.put("g_all", [P, TILES * HEADS, EXPERTS], F32)
        g_t = r.put("g_t", [P, TILES * HEADS, EXPERTS], F32)
        g_m = r.put("g_m", [P, TILES * HEADS], F32)
        assert r.next <= q_lo_at
        topT = at("topT", shared_at + 4 * 2 * HALF, [HEADS * EXPERTS, NP], BF16)

        bank = ctx.enter_context(nc.psum_tensor("bank", [P, 8, HALF], F32))

        table_dram = nc.dram_tensor("table_dram", [BLOCKS], I32).ap()
        x1_dram = nc.dram_tensor("x1_dram", [NP, D], F32).ap()
        topT_dram = nc.dram_tensor("topT_dram", [HEADS * EXPERTS, NP], BF16).ap()

        consts = sem("consts")
        filled = sem("filled")
        edges_in = sem("edges_in")
        table_step = sem("table_step")
        table_ready = sem("table_ready")
        table_pe = sem("table_pe")
        table_done = sem("table_done")
        table_out = sem("table_out")
        table_in = sem("table_in")
        raw_in = [sem(f"raw_in{i}") for i in range(RAW)]
        chunk_hi = sem("chunk_hi")
        chunk_lo = sem("chunk_lo")
        chunk_used = sem("chunk_used")
        xin_in = [sem(f"xin_in{i}") for i in range(2)]
        ln_step = sem("ln_step")
        ln_var = sem("ln_var")
        ln_sqrt = sem("ln_sqrt")
        ln_done = sem("ln_done")
        xT_pe = sem("xT_pe")
        xT_hi_done = sem("xT_hi_done")
        xT_lo_done = sem("xT_lo_done")
        h_pe = sem("h_pe")
        h_done = sem("h_done")
        dst_ready = sem("dst_ready")
        held = sem("held")
        pool_src_ready = sem("pool_src_ready")
        src_ready = sem("src_ready")
        onehot_used = sem("onehot_used")
        block_pe = sem("block_pe")
        block_done = sem("block_done")
        a_loops = sem("a_loops")
        a_summed = sem("a_summed")
        sum_ready = sem("sum_ready")
        h_hi_done = sem("h_hi_done")
        h_lo_done = sem("h_lo_done")
        a_hi_done = sem("a_hi_done")
        a_lo_done = sem("a_lo_done")
        deg_pe = sem("deg_pe")
        most_ready = sem("most_ready")
        most_pe = sem("most_pe")
        many_ready = sem("many_ready")
        dinv_done = sem("dinv_done")
        agg_pe = sem("agg_pe")
        agg_read = sem("agg_read")
        xres_in = [sem(f"xres_in{i}") for i in range(2)]
        bias_in = sem("bias_in")
        x1_ready = sem("x1_ready")
        x1_out = [sem(f"x1_out{i}") for i in range(2)]
        gate_pe = sem("gate_pe")
        gate_act = sem("gate_act")
        gate_step = sem("gate_step")
        topT_out = sem("topT_out")

        values_pe = sem("values_pe")
        picked_done = sem("picked_done")
        value_done = sem("value_done")
        v_step = sem("v_step")
        qk_hi = sem("qk_hi")
        qk_lo = sem("qk_lo")
        q_in = sem("q_in")
        k_in = sem("k_in")
        sim_pe = sem("sim_pe")
        max_done = sem("max_done")
        neg_done = sem("neg_done")
        exp_done = sem("exp_done")
        inv_done = sem("inv_done")
        norm_done = sem("norm_done")
        prob_done = sem("prob_done")
        pT_pe = sem("pT_pe")
        pT_hi_done = sem("pT_hi_done")
        pT_lo_done = sem("pT_lo_done")
        pv_pe = sem("pv_pe")
        o_hi = sem("o_hi")
        o_done = sem("o_done")
        mask_in = [sem(f"mask_in{i}") for i in range(2)]
        m_hi_done = sem("m_hi_done")
        m_lo_done = sem("m_lo_done")
        m_used = sem("m_used")
        acc_in = [sem(f"acc_in{i}") for i in range(2)]
        acc_done = sem("acc_done")

        block = ctx.enter_context(nc.Block())

        def block_range(eng, b):
            word = eng.value_load(table_row[0:1, b:b + 1], min_val=2 * 128, max_val=GROUPS * 128 + GROUPS)
            first = eng.snap((word % 128).with_bounds(min_val=0, max_val=GROUPS - 2))
            end = eng.snap((word // 128).with_bounds(min_val=2, max_val=GROUPS))
            return first, end

        def counter(eng, name, start):
            register = eng.alloc_register(name)
            eng.reg_mov(register, start)
            return register

        def cols(t, width=P):
            return slice(t * width, (t + 1) * width)

        def load_chunks(eng, stage, p, begin=0, end=KT):
            for k in range(begin, min(end, len(SLOTS[stage]))):
                slot, _ = chunk_raw(stage, p, k)
                wait(eng, chunk_lo, chunk_number(stage, p, k) - RAW + 1)
                to = raw[:, slot, :]
                if stage in ("W0", "W1"):
                    n = int(stage[1])
                    of = gnn_w[cols(k), cols(n, HALF)]
                elif stage == "G":
                    to = to.rearrange("p (k c) -> p k c", k=KT)
                    of = w_gate.rearrange("(k p) c -> p k c", p=P)
                elif stage in ("VA", "VB"):
                    head = 2 * p + (stage == "VB")
                    to = to.rearrange("p (e c) -> p e c", e=EXPERTS)
                    of = value_experts[:, bass.ds(head, 1), cols(k), :].rearrange("e h d c -> d (e h) c")
                elif stage in ("O0", "O1"):
                    pair = p - 1
                    of = output_experts[k, bass.ds(2 * pair, 2), :, cols(int(stage[1]), HALF)].rearrange("h c n -> (h c) n")
                else:
                    w = (w_q, w_k)[k // 2]
                    to = to.rearrange("p (k c) -> p k c", k=4)
                    of = w.rearrange("(k p) c -> p k c", p=P)[:, 4 * (k % 2):4 * (k % 2) + 4, bass.ds(P * p, P)]
                eng.dma_start(to, of).then_inc(raw_in[slot], 16)

        def wait_dense(eng, done, stage, p, n, t):
            if t < TILES - 1:
                eng.wait_ge(done, (TILES - 1) * n + t + 1)
            else:
                eng.wait_ge(chunk_used, chunk_number(stage, p, KT - 1) + 1)

        def split_hi(act, stage, p, begin=0, end=KT):
            for k, place in list(enumerate(SLOTS[stage]))[begin:end]:
                slot, times = chunk_raw(stage, p, k)
                wait(act, raw_in[slot], times * 16)
                wait(act, chunk_used, chunk_before(stage, p, k))
                act.activation(ring_hi[:, place, :], raw[:, slot, :], ACT.Copy).then_inc(chunk_hi, 1)

        def split_lo(dve, stage, p, begin=0, end=KT):
            for k, place in list(enumerate(SLOTS[stage]))[begin:end]:
                slot, _ = chunk_raw(stage, p, k)
                wait(dve, chunk_hi, chunk_number(stage, p, k) + 1)
                dve.tensor_tensor(ring_lo[:, place, :], raw[:, slot, :], ring_hi[:, place, :],
                                  ALU.subtract).then_inc(chunk_lo, 1)

        def xT_bank(n):
            return 2 * (n % 2) if n < TILES else 2 * (n % 4)

        def due(g, s, i):
            if i % 2 == 0 and i >= 2:
                return g, s, i // 2 - 1
            if i == 0 and s == 1:
                return g - 1, 0, QUADS - 1
            return None

        def three(pe, acc_ap, w_hi, w_lo, m_hi_ap, m_lo_ap, start, stop):
            return [pe.matmul(acc_ap, w_hi, m_hi_ap, start=start, stop=False),
                    pe.matmul(acc_ap, w_hi, m_lo_ap, start=False, stop=False),
                    pe.matmul(acc_ap, w_lo, m_hi_ap, start=False, stop=stop)]

        @block.sync
        def _(sp):
            sp.wait_ge(filled, 3)
            for to, of in ((e_dst, dst), (e_dst_hi, dst), (e_src, src)):
                sp.dma_start(to[0:FULL_GROUPS, :], of[0:FULL_GROUPS * GROUP].rearrange("(g q) -> g q", q=GROUP)).then_inc(edges_in, 16)
                sp.dma_start(to[FULL_GROUPS:GROUPS, 0:REST], of[FULL_GROUPS * GROUP:E].rearrange("(g q) -> g q", g=1)).then_inc(edges_in, 16)

            def load_x(t):
                if t >= 2:
                    sp.wait_ge(xT_pe, t - 1)
                if t < TILES - 1:
                    sp.dma_start(xin[t % 2][:, :], x[cols(t), :]).then_inc(xin_in[t % 2], 16)
                else:
                    sp.wait_ge(filled, 4)
                    sp.dma_start(xin[t % 2][0:LAST, :], x[t * P:N, :]).then_inc(xin_in[t % 2], 16)

            for t in range(2):
                load_x(t)
            load_chunks(sp, "W0", 0)
            sp.wait_ge(table_done, 1)
            sp.dma_start(table_dram.rearrange("(b c) -> b c", c=1), table_i[:, :]).then_inc(table_out, 16)
            sp.wait_ge(table_out, 16)
            sp.dma_start(table_row[:, :], table_dram.rearrange("(a n) -> a n", a=1)).then_inc(table_in, 16)
            for t in range(2, TILES):
                load_x(t)
            load_chunks(sp, "W1", 0)
            load_chunks(sp, "G", 0)
            load_chunks(sp, "QK", 0, 0, 3)
            sp.wait_ge(chunk_used, CHUNK_FIRST["G", 0])
            sp.wait_ge(deg_pe, 1)
            sp.dma_start(bias[:, :], gnn_b.rearrange("(a n) -> a n", a=1).broadcast_to([P, D])).then_inc(bias_in, 16)

            def store_x1(t):
                sp.wait_ge(x1_ready, t + 1)
                sp.dma_start(x1_dram[cols(t), :], xres[:, t % 2, :]).then_inc(x1_out[t % 2], 16)

            for t in range(TILES):
                if t >= 2:
                    store_x1(t - 2)
                    sp.wait_ge(x1_out[t % 2], 16 * (t // 2))
                    sp.wait_ge(ln_done, TILES + t - 1)
                if t < TILES - 1:
                    sp.dma_start(xres[:, t % 2, :], x[cols(t), :]).then_inc(xres_in[t % 2], 16)
                else:
                    sp.wait_ge(filled, 5)
                    sp.dma_start(xres[0:LAST, t % 2, :], x[t * P:N, :]).then_inc(xres_in[t % 2], 16)
            store_x1(TILES - 2)
            store_x1(TILES - 1)
            for i in range(2):
                sp.wait_ge(x1_out[i], 16 * TILES // 2)

            def sums_in(p, m):
                t, n = m % TILES, m // TILES
                if m == 0:
                    sp.wait_ge(pv_pe, (2 * p) * 15)
                if m == 0 and not past_pairs(p):
                    sp.wait_ge(q_in, 32 * p + 32)
                sp.wait_ge(x1_out[t % 2], (5 + (p - 1) * 10 + m // 2) * 16)
                rows = LAST if t == TILES - 1 else P
                sp.dma_start(acc[0:rows, t % 2, :], x1_dram[t * P:t * P + rows, cols(n, HALF)]).then_inc(acc_in[t % 2], 16)

            def sums_out(p, m, to):
                t, n = m % TILES, m // TILES
                rows = LAST if t == TILES - 1 else P
                sp.wait_ge(acc_done, 20 * p + m + 1)
                sp.dma_start(to[t * P:t * P + rows, cols(n, HALF)], acc[0:rows, t % 2, :]).then_inc(x1_out[t % 2], 16)

            def moe(p, to):
                last = past_pairs(p)
                load_chunks(sp, "O0", p)
                load_chunks(sp, "O1", p, 0, RAW)
                sums_in(p, 0)
                for m in range(2 * TILES):
                    if m == TILES - 2:
                        load_chunks(sp, "O1", p, RAW, RAW + 2)
                    if m == TILES - 1:
                        load_chunks(sp, "O1", p, RAW + 2)
                    if m == TILES and not last:
                        load_chunks(sp, "VB", p, 0, RAW)
                    if m == 2 * TILES - 2 and not last:
                        load_chunks(sp, "VB", p, RAW, RAW + 2)
                    if m == 2 * TILES - 1 and not last:
                        load_chunks(sp, "VB", p, RAW + 2)
                    if m + 1 < 2 * TILES:
                        sums_in(p, m + 1)
                    sums_out(p, m, to)

            load_chunks(sp, "QK", 0, 3)
            load_chunks(sp, "VA", 0)
            load_chunks(sp, "VB", 0)
            sp.wait_ge(topT_out, 16)

            def pair(p):
                load_chunks(sp, "VA", p)
                load_chunks(sp, "QK", p)
                moe(p, x1_dram)

            with sp.Fori(1, PAIRS - 1) as p:
                pair(p)
            pair(PAIRS - 1)
            moe(PAIRS, out)
            for i in range(2):
                sp.wait_ge(x1_out[i], (5 + PAIRS * 10) * 16)

        @block.gpsimd
        def _(pool):
            exact = dict(channel_multiplier=0, base=0, allow_small_or_imprecise_dtypes=True)
            pool.iota(iota_f[:, :], [[1, KEYS]], **exact).then_inc(consts, 1)
            pool.iota(group_no[:, :], [[1, GROUPS]], **exact).then_inc(consts, 1)
            pool.iota(key_offset[:, :], [[-BLOCK_KEY, BLOCKS]], **exact).then_inc(consts, 1)
            pool.iota(block_lo[:, :], [[0, 1]], base=0, channel_multiplier=BLOCK,
                      allow_small_or_imprecise_dtypes=True).then_inc(consts, 1)
            pool.iota(rank[:, :], [[-1, EXPERTS]], base=EXPERTS, channel_multiplier=0,
                      allow_small_or_imprecise_dtypes=True).then_inc(consts, 1)
            pool.memset(ident[:, :], 0.0).then_inc(consts, 1)
            pool.memset(ident_b[:, :], 0.0).then_inc(consts, 1)
            pool.memset(causal[:, :, :], 0.0).then_inc(consts, 1)
            pool.wait_ge(consts, 8)
            for m in (ident, ident_b):
                pool.affine_select(out=m[:, :], in_=m[:, :], compare_op=ALU.not_equal, fill=1.0, base=0,
                                   pattern=[[-1, P]], channel_multiplier=1).then_inc(consts, 1)
            for i in range(2):
                pool.affine_select(out=causal[:, i, :], in_=causal[:, i, :], compare_op=ALU.is_ge, fill=NEG,
                                   base=P * i, pattern=[[-1, 2 * P]], channel_multiplier=1).then_inc(consts, 1)
            def hold(i):
                return pool.tensor_tensor(scratch[:, i:i + 1], ident[:, 0:1], ident[:, 0:1], ALU.add)

            pool.wait_ge(consts, 12)
            for i, (semaphore, start) in enumerate((
                    (m_hi_done, 40), (m_lo_done, 40), (m_used, 40),
                    (acc_done, 20))):
                pool.memset(scratch[:, 3 + i:4 + i], 0.0).then_inc(semaphore, start)

            split_lo(pool, "W0", 0)
            pool.wait_ge(table_in, 16)
            now, src_now = counter(pool, "now", 1), counter(pool, "src_now", 1)
            free = [counter(pool, f"free{slot}", slot + 1) for slot in range(OH_SLOTS)]
            for b in range(BLOCKS):
                first, end = block_range(pool, b)
                with pool.Fori(first, end) as g:
                    group = g.with_bounds(min_val=0, max_val=GROUPS - 1)
                    pool.wait_ge(src_ready, src_now)
                    pool.tensor_copy(pool_src[:, :], modT[:, bass.ds(group, 1), 0:SUB:PART].rearrange("p a s -> p (a s)")
                                     ).then_inc(pool_src_ready, 1)
                    for slot in range(OH_SLOTS):
                        pool.wait_ge(pool_src_ready, now)
                        pool.wait_ge(onehot_used, free[slot])
                        hold(slot)
                        pool.tensor_scalar(onehot[:, slot, 0, 0:P], iota[:, 0:P], pool_src[:, slot:slot + 1], None,
                                           ALU.is_equal).then_inc(src_ready, 1)
                        pool.reg_add(free[slot], free[slot], OH_SLOTS)
                    pool.reg_add(now, now, 1)
                    pool.reg_add(src_now, src_now, OH_SLOTS)
                u = b // 2
                if b % 2 == 0 and u == TILES - 1:
                    split_lo(pool, "W1", 0, 0, 2)
                if b % 2 == 1 and u == TILES - 1:
                    split_lo(pool, "W1", 0, 2)

            def stack_halves(p):
                low, high = slice(0, DH), slice(DH, P)
                for m, copies in enumerate((
                    ((q_st[0][high, :], q_lo[low, :]), (q_st[1][low, :], q_lo[high, :])),
                    ((kh_st[0][high, :], kh_st[0][low, :]), (kl_st[0][high, :], kl_st[0][low, :]),
                     (kh_st[1][low, :], kh_st[1][high, :]), (kl_st[1][low, :], kl_st[1][high, :])))):
                    pool.wait_ge(qk_lo, 4 * p + 2 * m + 2)
                    wait(pool, held, 2 * p + m)
                    hold(OH_SLOTS).then_inc(held, 1)
                    for to, of in copies:
                        pool.dma_start(to, of).then_inc((q_in, k_in)[m], 16)

            stack_halves(0)
            with pool.Fori(1, PAIRS - 1) as p:
                stack_halves(p)
            stack_halves(PAIRS - 1)

        @block.scalar
        def _(act):
            def sqrt_of(w, n):
                act.wait_ge(ln_var, n)
                act.activation(nt[:, 1, 0:w], nt[:, 0, 0:w], ACT.Sqrt).then_inc(ln_sqrt, 1)

            def xT_hi_part(t, n):
                act.wait_ge(xT_pe, n + 1)
                b = xT_bank(n)
                act.activation(xT_hi[:, :, cols(t)], bank[:, b:b + 2, :].rearrange("p b (k c) -> p (b k) c", c=P),
                               ACT.Copy).then_inc(xT_hi_done, 1)

            def h_part(n, t):
                u = n * TILES + t
                wait_dense(act, h_pe, f"W{n}", 0, n, t)
                act.activation(h[:, t, cols(n, HALF)], bank[:, 4 + u % 2, :], ACT.Copy).then_inc(h_done, 1)

            def block_part(b):
                act.wait_ge(block_pe, b + 1)
                act.activation(a_u16[:, :, cols(b, BLOCK)],
                               bank[:, 6 + b % 2, 0:KEYS].rearrange("p (d s) -> p s d", s=TILES),
                               ACT.Copy).then_inc(block_done, 1)

            def a_hi_part(t):
                if t == 0:
                    act.wait_ge(a_loops, TILES)
                    act.wait_ge(chunk_used, CHUNK_FIRST["G", 0])
                if t >= 2:
                    act.wait_ge(agg_pe, t - 1)
                act.activation(a_hi[:, t % 2, :, :], a_u16[:, :, cols(t)], ACT.Copy).then_inc(a_hi_done, 1)

            split_hi(act, "W0", 0)
            for t in range(2):
                sqrt_of(1, t + 1)
            xT_hi_part(0, 0)
            act.wait_ge(table_done, 1)
            act.wait_ge(table_out, 16)
            for u in range(2 * TILES):
                n, t = u // TILES, u % TILES
                if u + 1 < TILES:
                    xT_hi_part(u + 1, u + 1)
                if u == TILES - 1:
                    act.wait_ge(xT_pe, TILES)
                    split_hi(act, "W1", 0, 0, 2)
                block_part(2 * u)
                h_part(n, t)
                if u == TILES - 1:
                    split_hi(act, "W1", 0, 2)
                if u + 2 < TILES:
                    sqrt_of(1, u + 3)
                block_part(2 * u + 1)
            act.wait_ge(a_summed, TILES)
            act.wait_ge(chunk_used, CHUNK_FIRST["G", 0])
            act.activation(a_sum_f[:, :], a_sum[:, :], ACT.Copy).then_inc(sum_ready, 1)
            a_hi_part(0)
            sqrt_of(TILES, TILES + 1)
            act.wait_ge(dinv_done, 1)
            for t in range(TILES):
                act.activation(h_hi[:, t, :], h[:, t, :], ACT.Copy, scale=dinv[:, t:t + 1]).then_inc(h_hi_done, 1)
            a_hi_part(1)
            for t in range(TILES):
                sqrt_of(1, TILES + 2 + t)
                if t + 2 < TILES:
                    a_hi_part(t + 2)
            for t in range(TILES):
                xT_hi_part(t, TILES + t)
            split_hi(act, "G", 0)
            split_hi(act, "QK", 0, 0, 2)
            act.wait_ge(gate_pe, 1)
            act.activation(logitT[:, :], bank[0:HEADS * EXPERTS, 5:8, :].rearrange("p b c -> p (b c)")[:, 0:NP],
                           ACT.Copy).then_inc(gate_act, 1)
            split_hi(act, "QK", 0, 2)
            act.wait_ge(gate_pe, 2)
            act.activation(g_all[:, :, :].rearrange("p a e -> p (a e)"),
                           bank[:, 0:2, :].rearrange("p b c -> p (b c)")[:, 0:TILES * HEADS * EXPERTS],
                           ACT.Sigmoid).then_inc(gate_act, 1)

            def topT_part():
                act.wait_ge(gate_pe, 3)
                act.activation(topT[:, :], bank[0:HEADS * EXPERTS, 2:5, :].rearrange("p b c -> p (b c)")[:, 0:NP],
                               ACT.Copy).then_inc(gate_act, 1)
                act.wait_ge(gate_act, 3)
                act.dma_start(topT_dram, topT[:, :]).then_inc(topT_out, 16)

            def exps(g, i, w):
                n = 10 * g + i
                act.wait_ge(neg_done, n + 1)
                wait(act, pT_pe, 15 * g + (i // 2) * (i // 2 + 1) // 2)
                act.activation(prob[:, i % 2, 0:w], bank[:, 2:5, :].rearrange("p b c -> p (b c)")[:, 0:w], ACT.Exp,
                               bias=rowstat[:, 0, i % 2:i % 2 + 1], scale=SCALE,
                               accum_out=rowstat[:, 1, i % 2:i % 2 + 1]).then_inc(exp_done, 1)

            def pT_hi_parts(g, s, q):
                for j in range(q + 1):
                    n = 15 * g + q * (q + 1) // 2 + j
                    b = (15 * s + q * (q + 1) // 2 + j) % 2
                    if s == 0 and q == 0 and j == 0:
                        for i in range(2):
                            act.wait_ge(x1_out[i], (5 * g + 5) * 16)
                    act.wait_ge(pT_pe, n + 1)
                    wait(act, pv_pe, n - 1)
                    act.activation(pT_hi[:, b, :], bank[:, 5 + b, :], ACT.Copy).then_inc(pT_hi_done, 1)

            def o_hi_part(g, s, q):
                act.wait_ge(pv_pe, 15 * g + (q + 1) * (q + 2) // 2)
                if s == 0 and q == 0:
                    act.wait_ge(m_lo_done, 20 * g + 40)
                part = slice(s * DH, (s + 1) * DH)
                side = (s + q) % 2
                act.activation(oT_hi[part, cols(q, 2 * P)], bank[part, 7, cols(side, 2 * P)], ACT.Copy).then_inc(o_hi, 1)

            def attention(g, s, beside=None):
                for i in range(TILES):
                    ready = due(g, s, i)
                    if ready:
                        pT_hi_parts(*ready)
                    if i == 0 and s == 0:
                        act.wait_ge(m_used, 20 * g + 40)
                        act.wait_ge(acc_done, 10 * g + 20)
                    exps(g, i, (i // 2 + 1) * 2 * P)
                    if ready:
                        o_hi_part(*ready)
                    if i == TILES - 2 and beside:
                        split_hi(act, *beside, 0, 2)
                if beside:
                    split_hi(act, *beside, 2)

            def qk_hi_parts(p, m):
                act.wait_ge(chunk_used, chunk_number("QK", p, 2 * m + 1) + 1)
                b = 2 + 3 * m
                for s in range(2):
                    part = slice(s * DH, (s + 1) * DH)
                    to = (q_st, kh_st)[m][s]
                    act.activation(to[part, :], bank[part, b:b + 3, :].rearrange("p b c -> p (b c)")[:, 0:NP],
                                   ACT.Copy).then_inc(qk_hi, 1)

            def masks_in(p, m):
                t = m % TILES
                act.wait_ge(m_lo_done, (20 * p + m - 1) * 2)
                for s in range(2):
                    rows = topT_dram[bass.ds((2 * (p - 1) + s) * EXPERTS, EXPERTS), cols(t)]
                    act.dma_start(mask[s * DH:(s + 1) * DH, t % 2, :, :],
                                 rows.unsqueeze(0).broadcast_to([DH, EXPERTS, P])).then_inc(mask_in[t % 2], 16)

            def first_masks(p):
                act.wait_ge(pv_pe, (2 * p) * 15)
                if not past_pairs(p):
                    act.wait_ge(v_step, (2 * p + 1) * 3)
                for m in range(2):
                    masks_in(p, m)

            def moe(p, following=None):
                for m in range(2, TILES + 2):
                    masks_in(p, m)
                    if m == TILES:
                        split_hi(act, "O1", p, 0, 2)
                split_hi(act, "O1", p, 2)
                for m in range(TILES + 2, 2 * TILES):
                    masks_in(p, m)
                if following:
                    split_hi(act, *following)

            qk_hi_parts(0, 0)
            split_hi(act, "VA", 0)
            qk_hi_parts(0, 1)
            topT_part()
            split_hi(act, "VB", 0)
            act.wait_ge(topT_out, 16)
            attention(0, 0, ("VA", 1))

            def pair(p, following):
                attention(2 * p - 1, 1, ("QK", p))
                pT_hi_parts(2 * p - 1, 1, QUADS - 1)
                o_hi_part(2 * p - 1, 1, QUADS - 1)
                split_hi(act, "O0", p, 0, 6)
                qk_hi_parts(p, 0)
                split_hi(act, "O0", p, 6)
                first_masks(p)
                qk_hi_parts(p, 1)
                moe(p, ("VB", p))
                attention(2 * p, 0, following)

            with act.Fori(1, PAIRS - 1) as p:
                pair(p, ("VA", p + 1))
            pair(PAIRS - 1, None)
            attention(2 * PAIRS - 1, 1, ("O0", PAIRS))
            pT_hi_parts(2 * PAIRS - 1, 1, QUADS - 1)
            o_hi_part(2 * PAIRS - 1, 1, QUADS - 1)
            first_masks(PAIRS)
            moe(PAIRS)

        @block.tensor
        def _(pe):
            def transposes(n, tile_in):
                pe.wait_ge(ln_done, n + 1)
                if 2 <= n < TILES:
                    pe.wait_ge(xT_lo_done, n - 1)
                elif n >= TILES + 4:
                    pe.wait_ge(xT_lo_done, n - 3)
                b = xT_bank(n)
                for k in range(KT):
                    last = pe.transpose(bank[:, b + k // 4, cols(k % 4)], tile_in[:, cols(k)], ident[:, :])
                last.then_inc(xT_pe, 1)

            def dense(stage, p, t, acc_ap, done, ready=None, begin=0, end=KT):
                for k, place in list(enumerate(SLOTS[stage]))[begin:end]:
                    attend_step(ready, k)
                    if t == 0:
                        pe.wait_ge(chunk_lo, chunk_number(stage, p, k) + 1)
                    last = three(pe, acc_ap, xT_hi[:, k, cols(t)], xT_lo[:, k, cols(t)],
                                 ring_hi[:, place, :], ring_lo[:, place, :], k == 0, k == KT - 1)[-1]
                    if t == TILES - 1:
                        last.then_inc(chunk_used, 1)
                if t < TILES - 1 and end == KT:
                    last.then_inc(done, 1)

            def attend_step(ready, k):
                if ready is None:
                    return
                g, s, q = ready
                if k <= q:
                    n = 15 * g + q * (q + 1) // 2 + k
                    b = (15 * s + q * (q + 1) // 2 + k) % 2
                    if k == 0:
                        pe.wait_ge(prob_done, 10 * g + 2 * q + 2)
                if 2 <= k <= q + 2:
                    side = (s + q) % 2
                    rows = slice(0, DH) if s == 0 else slice(0, P)
                    o = bank[rows, 7, cols(side, 2 * P)]
                    j = k - 2
                    nj = 15 * g + q * (q + 1) // 2 + j
                    bj = (15 * s + q * (q + 1) // 2 + j) % 2
                    if j == 0:
                        pe.wait_ge(v_step, 3 * g + 3)
                        wait(pe, o_done, 5 * g + q - 1)
                    pe.wait_ge(pT_lo_done, nj + 1)
                    for jj in range(2):
                        u = 2 * j + jj
                        last = three(pe, o, v_hi[:, u, rows], v_lo[:, u, rows], pT_hi[:, bj, cols(jj, 2 * P)],
                                     pT_lo[:, bj, cols(jj, 2 * P)], u == 0, u == 2 * q + 1)[-1]
                    last.then_inc(pv_pe, 1)
                if k <= q:
                    wait(pe, pT_lo_done, n - 1)
                    for jj in range(2):
                        for i in range(2):
                            last = pe.transpose(bank[:, 5 + b, (2 * jj + i) * P:(2 * jj + i + 1) * P],
                                                prob[:, i, cols(2 * k + jj)], ident[:, :])
                    last.then_inc(pT_pe, 1)

            pe.wait_ge(consts, 12)
            pe.wait_ge(table_ready, 1)
            for n, of in enumerate((f_key, f_src)):
                for s in range(SUB):
                    last = pe.transpose(bank[:, 4 + n, cols(s, GROUPS)], of[:, cols(s)], ident[0:GROUPS, 0:GROUPS])
                last.then_inc(table_pe, 1)
            pe.matmul(bank[0:BLOCKS, 6, 0:2 * GROUPS], ones[0:GROUPS, 0:BLOCKS], diag[:, :],
                      start=True, stop=True).then_inc(table_pe, 1)
            pe.wait_ge(table_done, 1)

            dst_count = [counter(pe, f"dst_count{slot}", slot + 1) for slot in range(OH_SLOTS)]
            src_count = [counter(pe, f"src_count{slot}", slot + 2) for slot in range(OH_SLOTS)]

            def count_block(b, between):
                first, end = block_range(pe, b)
                counts = bank[:, 6 + b % 2, 0:KEYS]
                free = dict(skip_group_check=True)

                def group(begin):
                    for slot in range(OH_SLOTS):
                        pe.wait_ge(dst_ready, dst_count[slot])
                        pe.wait_ge(src_ready, src_count[slot])
                        for s in range(PART):
                            last = pe.matmul(counts, onehot[:, slot, s, 0:P], onehot[:, slot, s, P:P + KEYS],
                                             start=(begin and slot == s == 0), stop=False, **free)
                        last.then_inc(onehot_used, 1)
                        pe.reg_add(dst_count[slot], dst_count[slot], OH_SLOTS)
                        pe.reg_add(src_count[slot], src_count[slot], OH_SLOTS)

                if b >= 2:
                    pe.wait_ge(block_done, b - 1)
                group(True)
                between()
                with pe.Fori(first, pe.snap(end - 1)):
                    group(False)
                pe.matmul(counts, zeros_b[:, 0:P], zeros_b[:, :], start=False, stop=True, **free).then_inc(block_pe, 1)

            transposes(0, xin[0])
            for u in range(2 * TILES):
                n, t = u // TILES, u % TILES
                if u + 1 < TILES:
                    transposes(u + 1, xin[(u + 1) % 2])
                pe.wait_ge(xT_lo_done, t + 1)
                if u >= 2:
                    pe.wait_ge(h_done, u - 1)

                def quarter(i):
                    dense(f"W{n}", 0, t, bank[:, 4 + u % 2, :], h_pe, None, i * KT // 4, (i + 1) * KT // 4)

                quarter(0)
                if u == 0:
                    pe.wait_ge(table_in, 16)
                count_block(2 * u, lambda: quarter(1))
                quarter(2)
                count_block(2 * u + 1, lambda: quarter(3))
            pe.wait_ge(sum_ready, 1)
            for t in range(TILES):
                last = pe.matmul(bank[:, 4, t:t + 1], a_sum_f[:, cols(t)], ones[:, 0:1], start=True, stop=True)
            last.then_inc(deg_pe, 1)
            pe.wait_ge(most_ready, 1)
            pe.transpose(bank[0:1, 5, 0:P], most[:, 0:1], ident[:, :]).then_inc(most_pe, 1)
            for t in range(TILES):
                if t >= 2:
                    pe.wait_ge(agg_read, t - 1)
                pe.wait_ge(a_lo_done, t + 1)
                for u in range(TILES):
                    if t == 0:
                        pe.wait_ge(h_lo_done, u + 1)
                    for n in range(2):
                        to = bank[:, 2 * (t % 2) + n, :]
                        pe.matmul(to, a_hi[:, t % 2, u, :], h_hi[:, u, cols(n, HALF)], start=(u == 0), stop=False)
                        pe.matmul(to, a_hi[:, t % 2, u, :], h_lo[:, u, cols(n, HALF)], start=False, stop=(u == TILES - 1))
                if t == 0:
                    pe.wait_ge(many_ready, 1)
                    lo_parts = pe.value_load(many[0:1, 0:1], min_val=0, max_val=1)
                with pe.If(lo_parts > 0):
                    for u in range(TILES):
                        for n in range(2):
                            pe.matmul(bank[:, 2 * (t % 2) + n, :], a_lo[:, t % 2, u, :], h_hi[:, u, cols(n, HALF)],
                                      start=False, stop=(u == TILES - 1), skip_group_check=True)
                pe.drain().then_inc(agg_pe, 1)
            pe.wait_ge(xT_lo_done, TILES)
            for t in range(TILES):
                if t == 2:
                    pe.wait_ge(agg_read, TILES)
                transposes(TILES + t, h[:, t, :])
            pe.wait_ge(xT_lo_done, 2 * TILES)
            pe.wait_ge(chunk_lo, chunk_number("G", 0, 0) + 1)
            GE = HEADS * EXPERTS
            place = SLOTS["G"][0]
            for k in range(KT):
                for c, w in ((0, HALF), (HALF, HALF), (2 * HALF, NP - 2 * HALF)):
                    last = three(pe, bank[0:GE, 5 + c // HALF, 0:w], ring_hi[:, place, cols(k, GE)],
                                 ring_lo[:, place, cols(k, GE)], xT_hi[:, k, c:c + w], xT_lo[:, k, c:c + w],
                                 k == 0, k == KT - 1)[-1]
            last.then_inc(gate_pe, 1)

            def gate_logits():
                pe.wait_ge(gate_act, 1)
                for t in range(TILES):
                    last = pe.transpose(bank[:, t // 8, cols(t % 8, GE)], logitT[:, cols(t)], ident[0:GE, 0:GE])
                last.then_inc(gate_pe, 1)

            def top_transposes():
                pe.wait_ge(gate_step, 5)
                pe.wait_ge(qk_lo, 2)
                for t in range(TILES):
                    last = pe.transpose(bank[0:GE, 2 + t // 4, cols(t % 4)], top[:, t, :], ident[:, :])
                last.then_inc(gate_pe, 1)

            def values_tile(g, stage, p, t, ready):
                n = 10 * g + t
                wait(pe, picked_done, n - 1)
                if stage == "VB" and t < 2:
                    pe.wait_ge(acc_done, 20 * p + 19 + t)
                dense(stage, p, t, bank[:, t % 2, :], values_pe, ready)

            def sim_row(g, s, i):
                n = 10 * g + i
                w = (i // 2 + 1) * 2 * P
                if i == 0 and s == 0:
                    pe.wait_ge(q_in, 16 * g + 32)
                    pe.wait_ge(k_in, 32 * g + 64)
                wait(pe, exp_done, n)
                for c in range(0, w, HALF):
                    e = min(w, c + HALF)
                    to = bank[:, 2 + c // HALF, 0:e - c]
                    lhs = q_st[s][:, cols(i)]
                    pe.matmul(to, lhs, kh_st[s][:, c:e], start=True, stop=False)
                    last = pe.matmul(to, lhs, kl_st[s][:, c:e], start=False, stop=True)
                    if e == w:
                        edge = bank[:, 2 + c // HALF, e - c - 2 * P:e - c]
                        last = pe.matmul(edge, ident_b[:, :], causal[:, i % 2, :], start=False, stop=True,
                                         skip_group_check=True)
                last.then_inc(sim_pe, 1)

            def values_and_attention(gv, stage, p, ga, sa):
                for t in range(TILES):
                    if ga is not None:
                        sim_row(ga, sa, t)
                    values_tile(gv, stage, p, t, due(ga, sa, t) if ga is not None else None)

            def qk(p, ready=None):
                for m in range(2):
                    if ready is None and m == 1:
                        gate_logits()
                    b = 2 + 3 * m
                    if m == 0:
                        wait(pe, exp_done, 20 * p)
                    else:
                        wait(pe, pT_lo_done, 30 * p)
                        wait(pe, o_done, 10 * p)
                    for j in range(2):
                        place = SLOTS["QK"][2 * m + j]
                        pe.wait_ge(chunk_lo, chunk_number("QK", p, 2 * m + j) + 1)
                        for kk in range(4):
                            k = 4 * j + kk
                            if m == 0:
                                attend_step(ready, k)
                            for c, w in ((0, HALF), (HALF, HALF), (2 * HALF, NP - 2 * HALF)):
                                last = three(pe, bank[:, b + c // HALF, 0:w], ring_hi[:, place, cols(kk)],
                                             ring_lo[:, place, cols(kk)], xT_hi[:, k, c:c + w], xT_lo[:, k, c:c + w],
                                             k == 0, k == KT - 1)[-1]
                        last.then_inc(chunk_used, 1)

            def moe(p):
                pe.wait_ge(picked_done, 2 * TILES * PAIRS if past_pairs(p) else 20 * p + 10)
                for n in range(2):
                    stage = f"O{n}"
                    for t in range(TILES):
                        m = 20 * p + TILES * n + t
                        pe.wait_ge(acc_done, m - 1)
                        for e in range(EXPERTS):
                            G = 2 * m + e // 4
                            u = (2 * (TILES * n + t) + e // 4) % M_SLOTS
                            place = SLOTS[stage][e]
                            if t == 0:
                                pe.wait_ge(chunk_lo, chunk_number(stage, p, e) + 1)
                            if e % 4 == 0:
                                pe.wait_ge(m_lo_done, G + 1)
                            of_three = three(pe, bank[:, t % 2, :], m_hi[:, u, e % 4, :], m_lo[:, u, e % 4, :],
                                             ring_hi[:, place, :], ring_lo[:, place, :], e == 0, e == EXPERTS - 1)
                            last = of_three[-1]
                            if t == TILES - 1 and e == 4:
                                of_three[0].then_inc(chunk_used, 1)
                            if e % 4 == 3:
                                last.then_inc(m_used, 1)
                            elif t == TILES - 1:
                                last.then_inc(chunk_used, 1)
                        if t == TILES - 1:
                            pe.drain().then_inc(chunk_used, 1)

            pe.matmul(bank[0:1, 0, 0:1], ones[:, 0:1], ones[:, 0:1], start=True, stop=True).then_inc(chunk_used, 1)
            qk(0)
            pe.wait_ge(gate_act, 2)
            for t in range(TILES):
                values_tile(0, "VA", 0, t, None)
                if t == 1:
                    top_transposes()
            pe.wait_ge(gate_act, 3)
            values_and_attention(1, "VB", 0, 0, 0)

            def pair(p):
                values_and_attention(2 * p, "VA", p, 2 * p - 1, 1)
                qk(p, (2 * p - 1, 1, QUADS - 1))
                moe(p)
                values_and_attention(2 * p + 1, "VB", p, 2 * p, 0)

            with pe.Fori(1, PAIRS - 1) as p:
                pair(p)
            pair(PAIRS - 1)
            for i in range(TILES + 1):
                if i < TILES:
                    sim_row(2 * PAIRS - 1, 1, i)
                ready = due(2 * PAIRS - 1, 1, i)
                for k in range(QUADS + 2):
                    attend_step(ready, k)
            moe(PAIRS)

        @block.vector
        def _(dve):
            dve.memset(e_dst[:, :], -(1 << 20)).then_inc(filled, 1)
            dve.memset(e_dst_hi[:, :], 1 << 20).then_inc(filled, 1)
            dve.memset(e_src[:, :], 0).then_inc(filled, 1)
            steps = {}

            def chain(ins, semaphore=table_step):
                steps[id(semaphore)] = steps.get(id(semaphore), 0) + 1
                ins.then_inc(semaphore, 1)
                dve.wait_ge(semaphore, steps[id(semaphore)])

            dve.memset(ones[:, :], 1.0).then_inc(table_step, 1)
            dve.memset(pool_src[:, :], 0.0).then_inc(src_ready, 1)
            dve.memset(zeros_b[:, :], 0.0).then_inc(onehot_used, OH_SLOTS)
            steps[id(table_step)] = 1
            dve.wait_ge(consts, 12)
            dve.wait_ge(edges_in, 96)
            chain(dve.tensor_copy(iota[:, :], iota_f[:, :]))
            chain(dve.tensor_single_scalar(e_t0[:, :], e_dst[:, :], 5, ALU.arith_shift_right))
            chain(dve.tensor_single_scalar(e_t1[:, :], e_src[:, :], 7, ALU.arith_shift_right))
            for to, of in ((f_dst, e_dst), (f_dst_hi, e_dst_hi), (f_src, e_src), (f_key, e_t0), (f_hi, e_t1)):
                chain(dve.tensor_copy(to[:, :], of[:, :]))
            chain(dve.tensor_reduce(minmax[:, 0:1], f_dst_hi[:, :], AX_X, ALU.min))
            chain(dve.tensor_reduce(minmax[:, 1:2], f_dst[:, :], AX_X, ALU.max))
            chain(dve.tensor_scalar(f_dst_hi[:, :], f_dst[:, :], float(TILES), None, ALU.mult))
            chain(dve.scalar_tensor_tensor(out=f_key[:, :], in0=f_key[:, :], scalar=float(BLOCK_KEY - TILES * BLOCK),
                                           in1=f_dst_hi[:, :], op0=ALU.mult, op1=ALU.add))
            chain(dve.tensor_tensor(f_key[:, :], f_key[:, :], f_hi[:, :], ALU.add))
            chain(dve.scalar_tensor_tensor(out=f_src[:, :], in0=f_hi[:, :], scalar=-float(P), in1=f_src[:, :],
                                           op0=ALU.mult, op1=ALU.add))
            for i in range(2):
                last = dve.tensor_scalar(diag[:, cols(i, GROUPS)], ident[0:GROUPS, 0:GROUPS], minmax[:, i:i + 1], None,
                                         ALU.mult)
            last.then_inc(table_ready, 1)
            dve.wait_ge(table_pe, 3)
            chain(dve.tensor_copy(keyT[:, :, :].rearrange("p g s -> p s g"),
                                  bank[:, 4, 0:SUB * GROUPS].rearrange("p (s g) -> p s g", s=SUB)))
            chain(dve.tensor_copy(modT[:, :, :].rearrange("p g s -> p s g"),
                                  bank[:, 5, 0:SUB * GROUPS].rearrange("p (s g) -> p s g", s=SUB)))
            least, greatest = bank[0:BLOCKS, 6, 0:GROUPS], bank[0:BLOCKS, 6, GROUPS:2 * GROUPS]
            chain(dve.tensor_scalar(over_t[:, 0, :], least, -float(BLOCK - 1), block_lo[0:BLOCKS, :], ALU.add, ALU.is_le))
            chain(dve.tensor_scalar(over_t[:, 1, :], greatest, block_lo[0:BLOCKS, :], None, ALU.is_ge))
            chain(dve.tensor_tensor(over[:, :], over_t[:, 0, :], over_t[:, 1, :], ALU.mult))
            chain(dve.scalar_tensor_tensor(out=over_t[:, 0, :], in0=over[:, :], scalar=-1000.0,
                                           in1=group_no[0:BLOCKS, :], op0=ALU.mult, op1=ALU.add))
            chain(dve.tensor_reduce(table_f[:, 0:1], over_t[:, 0, :], AX_X, ALU.min))
            chain(dve.tensor_scalar(table_f[:, 0:1], table_f[:, 0:1], 1000.0, float(GROUPS - 2), ALU.add, ALU.min))
            chain(dve.scalar_tensor_tensor(out=over_t[:, 1, :], in0=group_no[0:BLOCKS, :], scalar=1.0,
                                           in1=over[:, :], op0=ALU.add, op1=ALU.mult))
            chain(dve.tensor_reduce(table_f[:, 1:2], over_t[:, 1, :], AX_X, ALU.max))
            chain(dve.tensor_tensor(table_f[:, 1:2], table_f[:, 1:2], table_f[:, 0:1], ALU.subtract))
            chain(dve.tensor_scalar(table_f[:, 1:2], table_f[:, 1:2], 2.0, None, ALU.max))
            chain(dve.tensor_tensor(table_f[:, 1:2], table_f[:, 1:2], table_f[:, 0:1], ALU.add))
            dve.scalar_tensor_tensor(out=table_i[:, :], in0=table_f[:, 1:2], scalar=128.0, in1=table_f[:, 0:1],
                                     op0=ALU.mult, op1=ALU.add).then_inc(table_done, 1)

            ln = [0]

            def ln_chain(ins):
                ln[0] += 1
                ins.then_inc(ln_step, 1)
                dve.wait_ge(ln_step, ln[0])

            roots = [0]

            def rsqrt(to, w, done=None):
                roots[0] += 1
                dve.wait_ge(ln_sqrt, roots[0])
                ln_chain(dve.reciprocal(nt[:, 2, 0:w], nt[:, 1, 0:w]))
                ln_chain(dve.tensor_tensor(nt[:, 3, 0:w], nt[:, 2, 0:w], nt[:, 2, 0:w], ALU.mult))
                ln_chain(dve.tensor_tensor(nt[:, 3, 0:w], nt[:, 3, 0:w], nt[:, 0, 0:w], ALU.mult))
                ln_chain(dve.tensor_scalar(nt[:, 3, 0:w], nt[:, 3, 0:w], -0.5, 1.5, ALU.mult, ALU.add))
                last = dve.tensor_tensor(to, nt[:, 2, 0:w], nt[:, 3, 0:w], ALU.mult)
                if done is None:
                    ln_chain(last)
                else:
                    last.then_inc(done, 1)
                    dve.wait_ge(done, 1)

            def statistics(tile, t):
                for n in range(2):
                    dve.bn_stats(stats[:, n, :], tile[:, cols(n, HALF)]).then_inc(ln_step, 1)
                ln[0] += 2
                dve.wait_ge(ln_step, ln[0])
                ln_chain(dve.bn_aggr(mv[:, t, :], stats[:, :, :]))
                dve.tensor_scalar(nt[:, 0, 0:1], mv[:, t, 1:2], LN_EPS, None, ALU.add).then_inc(ln_var, 1)

            def normalise(to, tile, t):
                rsqrt(rstd[:, t:t + 1], 1)
                dve.tensor_scalar(to, tile, mv[:, t, 0:1], rstd[:, t:t + 1], ALU.subtract, ALU.mult).then_inc(ln_done, 1)

            def xT_lo_part(t, n):
                dve.wait_ge(xT_hi_done, n + 1)
                b = xT_bank(n)
                dve.tensor_tensor(xT_lo[:, :, cols(t)], bank[:, b:b + 2, :].rearrange("p b (k c) -> p (b k) c", c=P),
                                  xT_hi[:, :, cols(t)], ALU.subtract).then_inc(xT_lo_done, 1)

            def x_statistics(t):
                if t == TILES - 1:
                    dve.wait_ge(xT_pe, TILES - 2)
                    dve.memset(xin[t % 2][96:P, :], 0.0).then_inc(filled, 1)
                    dve.wait_ge(filled, 4)
                dve.wait_ge(xin_in[t % 2], 16 * (t // 2 + 1))
                statistics(xin[t % 2], t)

            free_count = [counter(dve, f"free_count{slot}", slot + 1) for slot in range(OH_SLOTS)]

            def onehots(b):
                first, end = block_range(dve, b)
                with dve.Fori(first, end) as i:
                    g = i.with_bounds(min_val=0, max_val=GROUPS - 1)
                    for slot in range(OH_SLOTS):
                        dve.wait_ge(onehot_used, free_count[slot])
                        for s in range(1, PART):
                            dve.tensor_scalar(onehot[:, slot, s, 0:P], iota[:, 0:P],
                                              modT[:, bass.ds(g, 1), PART * slot + s], None, ALU.is_equal)
                        for s in range(PART):
                            last = dve.tensor_scalar(onehot[:, slot, s, P:P + KEYS], iota[:, :],
                                                     keyT[:, bass.ds(g, 1), PART * slot + s], key_offset[:, b:b + 1],
                                                     ALU.subtract, ALU.is_equal)
                        last.then_inc(dst_ready, 1)
                        dve.reg_add(free_count[slot], free_count[slot], OH_SLOTS)

            def sums_of(t):
                dve.wait_ge(block_done, (t + 1) * P // BLOCK)
                dve.tensor_tensor(a_u16[:, t, cols(t)], a_u16[:, t, cols(t)], ident[:, :], ALU.add).then_inc(a_loops, 1)
                dve.wait_ge(a_loops, t + 1)
                with nc.allow_low_precision("counts of at most 40001 are exact in 16 bits"):
                    dve.tensor_reduce(a_sum[:, cols(t)], a_u16[:, :, cols(t)].rearrange("p u c -> p c u"), AX_X,
                                      ALU.add).then_inc(a_summed, 1)

            for t in range(2):
                x_statistics(t)
                normalise(xin[t][:, :], xin[t][:, :], t)
            xT_lo_part(0, 0)
            dve.wait_ge(table_in, 16)
            for u in range(2 * TILES):
                onehots(2 * u)
                if u + 1 < TILES:
                    xT_lo_part(u + 1, u + 1)
                if u + 2 < TILES:
                    x_statistics(u + 2)
                onehots(2 * u + 1)
                if u + 2 < TILES:
                    normalise(xin[u % 2][:, :], xin[u % 2][:, :], u + 2)
                if u >= 2 and u % 2 == 0:
                    sums_of(u // 2 - 1)
            sums_of(TILES - 1)
            dve.wait_ge(deg_pe, 1)
            dve.tensor_copy(nt[:, 0, :], bank[:, 4, 0:TILES]).then_inc(ln_var, 1)
            dve.tensor_reduce(most[:, 0:1], bank[:, 4, 0:TILES], AX_X, ALU.max).then_inc(most_ready, 1)
            rsqrt(dinv[:, :], TILES, dinv_done)

            def a_lo_part(t):
                dve.wait_ge(a_hi_done, t + 1)
                dve.tensor_tensor(a_lo[:, t % 2, :, :], a_u16[:, :, cols(t)], a_hi[:, t % 2, :, :],
                                  ALU.subtract).then_inc(a_lo_done, 1)

            dve.wait_ge(most_pe, 1)
            dve.tensor_reduce(most[0:1, 1:2], bank[0:1, 5, 0:P], AX_X, ALU.max).then_inc(most_ready, 1)
            dve.wait_ge(most_ready, 2)
            dve.tensor_scalar(many[:, :], most[0:1, 1:2], 4096.0, None, ALU.is_gt).then_inc(many_ready, 1)
            a_lo_part(0)
            for t in range(TILES):
                dve.wait_ge(h_hi_done, t + 1)
                dve.scalar_tensor_tensor(out=h_lo[:, t, :], in0=h[:, t, :], scalar=dinv[:, t:t + 1], in1=h_hi[:, t, :],
                                         op0=ALU.mult, op1=ALU.subtract).then_inc(h_lo_done, 1)
            a_lo_part(1)
            dve.wait_ge(h_lo_done, TILES)
            dve.wait_ge(bias_in, 16)
            for t in range(TILES):
                tile = xres[:, t % 2, :]
                if t == TILES - 1:
                    dve.wait_ge(x1_out[t % 2], 16 * (t // 2))
                    dve.wait_ge(ln_done, TILES + t)
                    dve.memset(xres[96:P, t % 2, :], 0.0).then_inc(filled, 1)
                    dve.wait_ge(filled, 5)
                dve.wait_ge(agg_pe, t + 1)
                b = 2 * (t % 2)
                dve.scalar_tensor_tensor(out=y[:, :], in0=bank[:, b:b + 2, :].rearrange("p b c -> p (b c)"),
                                         scalar=dinv[:, t:t + 1], in1=bias[:, :], op0=ALU.mult,
                                         op1=ALU.add).then_inc(agg_read, 1)
                dve.wait_ge(agg_read, t + 1)
                dve.wait_ge(xres_in[t % 2], 16 * (t // 2 + 1))
                dve.scalar_tensor_tensor(out=tile, in0=y[:, :], scalar=0.0, in1=tile, op0=ALU.max,
                                         op1=ALU.add).then_inc(x1_ready, 1)
                dve.wait_ge(x1_ready, t + 1)
                statistics(tile, t)
                normalise(h[:, t, :], tile, t)
                if t + 2 < TILES:
                    a_lo_part(t + 2)
            for t in range(TILES):
                xT_lo_part(t, TILES + t)
            for i in range(2):
                dve.wait_ge(x1_out[i], 16 * TILES // 2)
            dve.wait_ge(ln_done, 2 * TILES)
            split_lo(dve, "G", 0)
            split_lo(dve, "QK", 0)
            steps[id(gate_step)] = 0
            dve.wait_ge(gate_act, 2)
            flat = [P, TILES * HEADS, EXPERTS]
            of_max = gate[:, :, :].rearrange("p t h -> p (t h)").unsqueeze(2).broadcast_to(flat)
            ranks = rank[:, :].unsqueeze(1).broadcast_to(flat)
            top_v = top[:, :, :].rearrange("p t (h e) -> p (t h) e", e=EXPERTS)
            chain(dve.tensor_reduce(gate[:, :, :].rearrange("p t h -> p (t h)"), g_all[:, :, :], AX_X, ALU.max), gate_step)
            chain(dve.tensor_tensor(g_t[:, :, :], g_all[:, :, :], of_max, ALU.is_equal), gate_step)
            chain(dve.tensor_tensor(g_t[:, :, :], g_t[:, :, :], ranks, ALU.mult), gate_step)
            chain(dve.tensor_reduce(g_m[:, :], g_t[:, :, :], AX_X, ALU.max), gate_step)
            chain(dve.tensor_tensor(top_v, g_t[:, :, :], g_m[:, :].unsqueeze(2).broadcast_to(flat), ALU.is_equal), gate_step)
            def pick(g, t, stage, p, after_vb=None):
                n = 10 * g + t
                if stage == "VB" and t == TILES - 1:
                    dve.wait_ge(chunk_used, after_vb)
                else:
                    wait_dense(dve, values_pe, stage, p, g, t)
                wait(dve, value_done, n - 1)
                hot = top[:, t, bass.ds(g * EXPERTS, EXPERTS)].unsqueeze(2).broadcast_to([P, EXPERTS, DH])
                mul = picked[:, t % 2, :].rearrange("p (e c) -> p e c", e=EXPERTS)
                dve.tensor_tensor(mul, bank[:, t % 2, :].rearrange("p (e c) -> p e c", e=EXPERTS), hot,
                                  ALU.mult).then_inc(picked_done, 1)
                dve.wait_ge(picked_done, n + 1)
                wait(dve, v_step, 3 * g)
                dve.tensor_reduce(v_raw[:, t, :], mul.rearrange("p e c -> p c e"), AX_X, ALU.add).then_inc(value_done, 1)

            def finish_values(g, s):
                dve.wait_ge(value_done, 10 * g + 10)
                if s == 0:
                    wait(dve, pv_pe, 15 * g)
                mine = slice(s * DH, (s + 1) * DH)
                gates = gate[:, :, bass.ds(g, 1)].broadcast_to([P, TILES, DH])
                dve.tensor_tensor(v_raw[:, :, :], v_raw[:, :, :], gates, ALU.mult).then_inc(v_step, 1)
                dve.wait_ge(v_step, 3 * g + 1)
                dve.tensor_copy(v_hi[:, :, mine], v_raw[:, :, :]).then_inc(v_step, 1)
                dve.wait_ge(v_step, 3 * g + 2)
                dve.tensor_tensor(v_lo[:, :, mine], v_raw[:, :, :], v_hi[:, :, mine], ALU.subtract).then_inc(v_step, 1)

            def row_max(g, i, w):
                n = 10 * g + i
                dve.wait_ge(sim_pe, n + 1)
                wait(dve, norm_done, n - 1)
                dve.tensor_reduce(rowstat[:, 2, i % 2:i % 2 + 1],
                                  bank[:, 2:5, :].rearrange("p b c -> p (b c)")[:, 0:w], AX_X, ALU.max).then_inc(max_done, 1)
                dve.wait_ge(max_done, n + 1)
                wait(dve, exp_done, n - 1)
                dve.tensor_scalar(rowstat[:, 0, i % 2:i % 2 + 1], rowstat[:, 2, i % 2:i % 2 + 1], -SCALE, None,
                                  ALU.mult).then_inc(neg_done, 1)

            def row_norm(g, i, w):
                n = 10 * g + i
                one = slice(i % 2, i % 2 + 1)
                dve.wait_ge(exp_done, n + 1)
                dve.wait_ge(neg_done, n + 1)
                dve.reciprocal(rowstat[:, 2, one], rowstat[:, 1, one]).then_inc(inv_done, 1)
                dve.wait_ge(inv_done, n + 1)
                wait(dve, prob_done, n - 1)
                dve.tensor_tensor(rowstat[:, 3, one], rowstat[:, 2, one], gate[:, i, bass.ds(g, 1)],
                                  ALU.mult).then_inc(norm_done, 1)
                dve.wait_ge(norm_done, n + 1)
                dve.tensor_scalar(prob[:, i % 2, 0:w], prob[:, i % 2, 0:w], rowstat[:, 3, one], None,
                                  ALU.mult).then_inc(prob_done, 1)

            def pT_lo_part(g, s, q, j):
                n = 15 * g + q * (q + 1) // 2 + j
                b = (15 * s + q * (q + 1) // 2 + j) % 2
                dve.wait_ge(pT_hi_done, n + 1)
                dve.tensor_tensor(pT_lo[:, b, :], bank[:, 5 + b, :], pT_hi[:, b, :], ALU.subtract).then_inc(pT_lo_done, 1)

            def o_lo_part(g, s, q):
                part = slice(s * DH, (s + 1) * DH)
                side = (s + q) % 2
                dve.wait_ge(o_hi, 5 * g + q + 1)
                dve.tensor_tensor(oT_lo[part, cols(q, 2 * P)], bank[part, 7, cols(side, 2 * P)],
                                  oT_hi[part, cols(q, 2 * P)], ALU.subtract).then_inc(o_done, 1)

            def attention(g, s, values=None, following=None, after_vb=None):
                for i in range(TILES):
                    w = (i // 2 + 1) * 2 * P
                    row_max(g, i, w)
                    ready = due(g, s, i)
                    if ready:
                        pT_lo_part(*ready, 0)
                    if values and i >= 1:
                        pick(values[0], i - 1, *values[1:])
                    if s == 1 and i == 0:
                        pick(g, TILES - 1, "VB", None, after_vb)
                    if ready:
                        for j in range(1, ready[2] + 1):
                            pT_lo_part(*ready, j)
                    if i == TILES - 1 and following and following[0] != "QK":
                        split_lo(dve, *following, 2, 4)
                    row_norm(g, i, w)
                    if ready:
                        o_lo_part(*ready)
                    if s == 1 and i == 0:
                        finish_values(g, 1)
                    if i == TILES - 2 and following:
                        split_lo(dve, *following, 0, 2)
                if following:
                    split_lo(dve, *following, 2 if following[0] == "QK" else 4)

            def last_rows(g):
                for j in range(QUADS):
                    pT_lo_part(g, 1, QUADS - 1, j)
                o_lo_part(g, 1, QUADS - 1)

            def qk_lo_parts(p, m):
                for s in range(2):
                    part = slice(s * DH, (s + 1) * DH)
                    dve.wait_ge(qk_hi, 4 * p + 2 * m + s + 1)
                    hi, lo = ((q_st[s], q_lo), (kh_st[s], kl_st[s]))[m]
                    b = 2 + 3 * m
                    dve.tensor_tensor(lo[part, :], bank[part, b:b + 3, :].rearrange("p b c -> p (b c)")[:, 0:NP],
                                      hi[part, :], ALU.subtract).then_inc(qk_lo, 1)

            def make(p, m):
                t = m % TILES
                for u in range(2):
                    n = 2 * m + u
                    G = 40 * p + n
                    if u == 0:
                        dve.wait_ge(mask_in[m % 2], 32 * ((p - 1) * 10 + m // 2 + 1))
                    if n == 0:
                        dve.wait_ge(o_done, 10 * p)
                    dve.wait_ge(m_used, G if n == 0 else G - M_SLOTS + 1)
                    for oT, to, done in ((oT_hi, m_hi, m_hi_done), (oT_lo, m_lo, m_lo_done)):
                        dve.tensor_tensor(to[:, n % M_SLOTS, :, :], oT[:, cols(t)].unsqueeze(1).broadcast_to([P, 4, P]),
                                          mask[:, t % 2, 4 * u:4 * u + 4, :], ALU.mult).then_inc(done, 1)

            def moe_half(p, half, following=None):
                def add(m):
                    t = m % TILES
                    M = 20 * p + m
                    rows = LAST if t == TILES - 1 else P
                    dve.wait_ge(m_used, 2 * M + 2)
                    dve.wait_ge(acc_in[t % 2], 16 * ((p - 1) * 10 + m // 2 + 1))
                    dve.tensor_tensor(acc[0:rows, t % 2, :], acc[0:rows, t % 2, :], bank[0:rows, t % 2, :],
                                      ALU.add).then_inc(acc_done, 1)

                for t in range(TILES):
                    m = half * TILES + t
                    if m < 2 * TILES - 1:
                        make(p, m + 1)
                    if t >= 1:
                        add(m - 1)
                    if t == TILES - 2 and following:
                        split_lo(dve, *following, 0, 2)
                if following:
                    split_lo(dve, *following, 2)
                add(half * TILES + TILES - 1)

            qk_lo_parts(0, 0)
            split_lo(dve, "VA", 0)
            qk_lo_parts(0, 1)
            for t in range(TILES):
                pick(0, t, "VA", 0)
            finish_values(0, 0)
            split_lo(dve, "VB", 0)
            attention(0, 0, (1, "VB", 0), ("VA", 1))

            def pair(p, following):
                attention(2 * p - 1, 1, (2 * p, "VA", p), ("QK", p), chunk_number("VA", p, 0))
                pick(2 * p, TILES - 1, "VA", p)
                last_rows(2 * p - 1)
                split_lo(dve, "O0", p, 0, 6)
                qk_lo_parts(p, 0)
                finish_values(2 * p, 0)
                split_lo(dve, "O0", p, 6)
                make(p, 0)
                qk_lo_parts(p, 1)
                moe_half(p, 0, ("O1", p))
                moe_half(p, 1, ("VB", p))
                attention(2 * p, 0, (2 * p + 1, "VB", p), following)

            with dve.Fori(1, PAIRS - 1) as p:
                pair(p, ("VA", p + 1))
            pair(PAIRS - 1, None)
            attention(2 * PAIRS - 1, 1, None, ("O0", PAIRS), chunk_number("O0", PAIRS, 0))
            last_rows(2 * PAIRS - 1)
            make(PAIRS, 0)
            moe_half(PAIRS, 0, ("O1", PAIRS))
            moe_half(PAIRS, 1)


_INS = ["x", "src", "dst", "L0_gnn_W", "L0_gnn_b", "L0_ffn_w_q", "L0_ffn_w_k", "L0_ffn_w_gate",
        "L0_ffn_value_experts", "L0_ffn_output_experts"]


def kernel(**inputs):
    import numpy as _np
    import concourse.bacc as _bacc
    from concourse import mybir as _mybir
    from concourse.bass_utils import run_bass_kernel_spmd as _run

    nc = _bacc.Bacc("TRN2", target_bir_lowering=False, num_devices=1)
    arrays, args = {}, []
    for name in _INS:
        a = _np.ascontiguousarray(inputs[name])
        arrays[f"in_{name}_dram"] = a
        args.append(nc.dram_tensor(f"in_{name}_dram", a.shape, _mybir.dt.from_np(a.dtype), kind="ExternalInput").ap())
    out = nc.dram_tensor("out_0_dram", (N, D), F32, kind="ExternalOutput").ap()
    build(nc, *args, out)
    r = _run(nc, [arrays], core_ids=[0])
    return r.results[0]["out_0_dram"]
```
